# Optimizing a Trainium2 kernel written in Bass

```python
import numpy as np
import jax
import jax.numpy as jnp

def _softmax(x, axis=-1):
    return jax.nn.softmax(x, axis=axis)

def _gelu(x):
    return jax.nn.gelu(x, approximate=True)

def _silu(x):
    return jax.nn.silu(x)

def _sigmoid(x):
    return jax.nn.sigmoid(x)

def _layernorm(x, axis=-1, eps=1e-05):
    m = jnp.mean(x, axis=axis, keepdims=True)
    v = jnp.var(x, axis=axis, keepdims=True)
    return (x - m) / jnp.sqrt(v + eps)

def _scatter_add(tgt, idx, src, axis=0):
    return tgt.at[idx].add(src)

def _segment_sum(src, seg, n):
    return jax.ops.segment_sum(src, seg, n)
kernel_name = 'mk_decoder_postln_d1_seqx_r8_eb8826'

def setup_inputs(seed: int=0):
    np.random.seed(seed)
    _w = jnp.asarray

    def _rec_inputs():
        import jax
        import jax.numpy as jnp
        _rk = jax.random.key(seed)
        x = -0.0003929 + 0.9999 * jax.random.normal(jax.random.fold_in(_rk, 1), (32, 64, 128), jnp.float32)
        _lenS = 64 - jax.random.randint(jax.random.fold_in(_rk, 7), (32,), 0, max(1, 64 // 4) + 1, jnp.int32)
        _lenS2 = 64 - jax.random.randint(jax.random.fold_in(_rk, 8), (32,), 0, max(1, 64 // 4) + 1, jnp.int32)
        _ctx_512P = jax.random.normal(jax.random.fold_in(_rk, 11), (32, 16, 64), jnp.float32)
        _ctx_512c = jax.random.dirichlet(jax.random.fold_in(_rk, 511), 0.3 * jnp.ones((16,), jnp.float32), (32, 64))
        _ctx_512t = jnp.einsum('bsk,bkd->bsd', _ctx_512c, _ctx_512P)
        _ctx_512t = _ctx_512t * jax.lax.rsqrt(jnp.mean(jnp.square(_ctx_512t)) + 1e-12) * 0.953939
        ctx_512 = 4.13588e-05 + 0.999923 * (_ctx_512t + 0.3 * jax.random.normal(jax.random.fold_in(_rk, 611), (32, 64, 64), jnp.float32))
        return (x, ctx_512)
    x, ctx_512 = _rec_inputs()

    def _L0_attn_setup():
        import jax, jax.numpy as jnp
        import numpy as np
        B, S, E = (8, 128, 128)
        H = 16
        D = E // H

        def _split_heads(t, b, s):
            return t.reshape(b, s, H, D).transpose(0, 2, 1, 3)
        key = jax.random.key(seed)
        ks = jax.random.split(key, 5)
        scale = 1.0 / np.sqrt(E)
        return {'x': jax.random.normal(ks[0], (B, S, E), dtype=jnp.float32), 'Wq': jax.random.normal(ks[1], (E, E), dtype=jnp.float32) * scale, 'Wk': jax.random.normal(ks[2], (E, E), dtype=jnp.float32) * scale, 'Wv': jax.random.normal(ks[3], (E, E), dtype=jnp.float32) * scale, 'Wo': jax.random.normal(ks[4], (E, E), dtype=jnp.float32) * scale}
    _L0_attn_all = _L0_attn_setup()
    _L0_attn_in = {k: v for k, v in _L0_attn_all.items() if k in ('Wq', 'Wk', 'Wv', 'Wo')}
    del _L0_attn_all

    def _L0_xattn_setup():
        import jax, jax.numpy as jnp
        import numpy as np
        B, LQ, LK = (8, 256, 256)
        QD, KD, VD = (128, 64, 64)
        key = jax.random.key(seed)
        ks = jax.random.split(key, 9)
        s = 0.02
        return {'query': jax.random.normal(ks[0], (B, LQ, QD), jnp.float32), 'key': jax.random.normal(ks[1], (B, LK, KD), jnp.float32), 'value': jax.random.normal(ks[2], (B, LK, VD), jnp.float32), 'Wq': jax.random.normal(ks[3], (QD, QD), jnp.float32) * s, 'bq': jnp.zeros((QD,), jnp.float32), 'Wk': jax.random.normal(ks[4], (KD, QD), jnp.float32) * s, 'bk': jnp.zeros((QD,), jnp.float32), 'Wv': jax.random.normal(ks[5], (VD, QD), jnp.float32) * s, 'bv': jnp.zeros((QD,), jnp.float32)}
    _L0_xattn_all = _L0_xattn_setup()
    _L0_xattn_in = {k: v for k, v in _L0_xattn_all.items() if k in ('Wq', 'bq', 'Wk', 'bk', 'Wv', 'bv')}
    del _L0_xattn_all

    def _L0_ffn_setup():
        import jax, jax.numpy as jnp
        import numpy as np
        D_MODEL = 128
        N_HEADS = 16
        N_GROUPS = 4
        D_FF = 512
        N_EXPERTS = 8
        TOP_K = 2
        BATCH = 2
        SEQ = 128
        D_K = D_MODEL // N_HEADS
        HPG = N_HEADS // N_GROUPS
        EPS = 1e-06

        def rms_norm(x, w):
            rms = jnp.sqrt(jnp.mean(x * x, axis=-1, keepdims=True) + EPS)
            return x / rms * w

        def rope(x):
            d = x.shape[-1]
            half = d // 2
            theta = 1.0 / 10000.0 ** (jnp.arange(half, dtype=jnp.float32) / half)
            pos = jnp.arange(x.shape[1], dtype=jnp.float32)[:, None]
            ang = pos * theta[None, :]
            cos, sin = (jnp.cos(ang), jnp.sin(ang))
            xe, xo = (x[..., 0::2], x[..., 1::2])
            return jnp.concatenate([xe * cos - xo * sin, xe * sin + xo * cos], axis=-1)

        def attention(x, Wq, Wk, Wv, Wo):
            B, S, _ = x.shape
            xr = rope(x)
            Q = (xr @ Wq).reshape(B, S, N_HEADS, D_K).transpose(0, 2, 1, 3)
            Q = Q.reshape(B, N_GROUPS, HPG, S, D_K)
            K = (xr @ Wk).reshape(B, S, N_GROUPS, D_K).transpose(0, 2, 1, 3)
            V = (xr @ Wv).reshape(B, S, N_GROUPS, D_K).transpose(0, 2, 1, 3)
            scores = jnp.einsum('bghsd,bgtd->bghst', Q, K) / jnp.sqrt(jnp.float32(D_K))
            mask = jnp.triu(jnp.full((S, S), -1000000000.0, dtype=scores.dtype), k=1)
            attn = jax.nn.softmax(scores + mask, axis=-1)
            out = jnp.einsum('bghst,bgtd->bghsd', attn, V)
            out = out.reshape(B, N_HEADS, S, D_K).transpose(0, 2, 1, 3).reshape(B, S, D_MODEL)
            return out @ Wo

        def moe(x, router_w, router_b, W1, b1, W2, b2, W3, b3):
            B, S, _ = x.shape
            logits = x @ router_w + router_b
            topv, topi = jax.lax.top_k(logits, TOP_K)
            topw = jax.nn.softmax(topv, axis=-1)
            onehot = jax.nn.one_hot(topi, N_EXPERTS, dtype=x.dtype)
            comb = jnp.einsum('bsk,bske->bse', topw, onehot)
            h1 = jnp.einsum('bsd,edf->ebsf', x, W1) + b1[:, None, None, :]
            h2 = jnp.einsum('bsd,edf->ebsf', x, W2) + b2[:, None, None, :]
            h = h2 * jax.nn.silu(h1)
            eo = jnp.einsum('ebsf,efd->ebsd', h, W3) + b3[:, None, None, :]
            return jnp.einsum('bse,ebsd->bsd', comb, eo)
        key = jax.random.key(seed)
        ks = jax.random.split(key, 16)
        s = 0.02
        return {'x': jax.random.normal(ks[0], (BATCH, SEQ, D_MODEL), dtype=jnp.float32), 'norm1_w': jnp.ones((D_MODEL,), jnp.float32), 'Wq': jax.random.normal(ks[1], (D_MODEL, D_MODEL), jnp.float32) * s, 'Wk': jax.random.normal(ks[2], (D_MODEL, N_GROUPS * D_K), jnp.float32) * s, 'Wv': jax.random.normal(ks[3], (D_MODEL, N_GROUPS * D_K), jnp.float32) * s, 'Wo': jax.random.normal(ks[4], (D_MODEL, D_MODEL), jnp.float32) * s, 'norm2_w': jnp.ones((D_MODEL,), jnp.float32), 'router_w': jax.random.normal(ks[5], (D_MODEL, N_EXPERTS), jnp.float32) * s, 'router_b': jnp.zeros((N_EXPERTS,), jnp.float32), 'W1': jax.random.normal(ks[6], (N_EXPERTS, D_MODEL, D_FF), jnp.float32) * s, 'b1': jnp.zeros((N_EXPERTS, D_FF), jnp.float32), 'W2': jax.random.normal(ks[7], (N_EXPERTS, D_MODEL, D_FF), jnp.float32) * s, 'b2': jnp.zeros((N_EXPERTS, D_FF), jnp.float32), 'W3': jax.random.normal(ks[8], (N_EXPERTS, D_FF, D_MODEL), jnp.float32) * s, 'b3': jnp.zeros((N_EXPERTS, D_MODEL), jnp.float32)}
    _L0_ffn_all = _L0_ffn_setup()
    _L0_ffn_in = {k: v for k, v in _L0_ffn_all.items() if k in ('norm1_w', 'Wq', 'Wk', 'Wv', 'Wo', 'norm2_w', 'router_w', 'router_b', 'W1', 'b1', 'W2', 'b2', 'W3', 'b3')}
    del _L0_ffn_all
    return {'x': x, 'ctx_512': ctx_512, 'L0_attn_Wq': _L0_attn_in['Wq'], 'L0_attn_Wk': _L0_attn_in['Wk'], 'L0_attn_Wv': _L0_attn_in['Wv'], 'L0_attn_Wo': _L0_attn_in['Wo'], 'L0_xattn_Wq': _L0_xattn_in['Wq'], 'L0_xattn_bq': _L0_xattn_in['bq'], 'L0_xattn_Wk': _L0_xattn_in['Wk'], 'L0_xattn_bk': _L0_xattn_in['bk'], 'L0_xattn_Wv': _L0_xattn_in['Wv'], 'L0_xattn_bv': _L0_xattn_in['bv'], 'L0_ffn_norm1_w': _L0_ffn_in['norm1_w'], 'L0_ffn_Wq': _L0_ffn_in['Wq'], 'L0_ffn_Wk': _L0_ffn_in['Wk'], 'L0_ffn_Wv': _L0_ffn_in['Wv'], 'L0_ffn_Wo': _L0_ffn_in['Wo'], 'L0_ffn_norm2_w': _L0_ffn_in['norm2_w'], 'L0_ffn_router_w': _L0_ffn_in['router_w'], 'L0_ffn_router_b': _L0_ffn_in['router_b'], 'L0_ffn_W1': _L0_ffn_in['W1'], 'L0_ffn_b1': _L0_ffn_in['b1'], 'L0_ffn_W2': _L0_ffn_in['W2'], 'L0_ffn_b2': _L0_ffn_in['b2'], 'L0_ffn_W3': _L0_ffn_in['W3'], 'L0_ffn_b3': _L0_ffn_in['b3']}

def reference(x, ctx_512, L0_attn_Wq, L0_attn_Wk, L0_attn_Wv, L0_attn_Wo, L0_xattn_Wq, L0_xattn_bq, L0_xattn_Wk, L0_xattn_bk, L0_xattn_Wv, L0_xattn_bv, L0_ffn_norm1_w, L0_ffn_Wq, L0_ffn_Wk, L0_ffn_Wv, L0_ffn_Wo, L0_ffn_norm2_w, L0_ffn_router_w, L0_ffn_router_b, L0_ffn_W1, L0_ffn_b1, L0_ffn_W2, L0_ffn_b2, L0_ffn_W3, L0_ffn_b3):
    import jax
    import jax.numpy as jnp

    def _L0_attn_ref(x, Wq, Wk, Wv, Wo):
        import jax, jax.numpy as jnp
        import numpy as np
        B, S, E = (8, 128, 128)
        H = 16
        D = E // H

        def _split_heads(t, b, s):
            return t.reshape(b, s, H, D).transpose(0, 2, 1, 3)
        b, s, e = x.shape
        q = _split_heads(x @ Wq.T, b, s)
        k = _split_heads(x @ Wk.T, b, s)
        v = _split_heads(x @ Wv.T, b, s)
        d = q.shape[-1]
        q_c = q - q.mean(axis=-1, keepdims=True)
        k_c = k - k.mean(axis=-1, keepdims=True)
        cov = jnp.einsum('bhqd,bhkd->bhqk', q_c, k_c) / d
        q_var = (q_c * q_c).sum(axis=-1, keepdims=True) / (d - 1)
        k_var = (k_c * k_c).sum(axis=-1, keepdims=True) / (d - 1)
        var = jnp.einsum('bhqo,bhko->bhqk', q_var, k_var) / d
        attn = jax.nn.softmax(cov + var, axis=-1)
        out = jnp.einsum('bhqk,bhkd->bhqd', attn, v)
        out = out.transpose(0, 2, 1, 3).reshape(b, s, e)
        return out @ Wo.T

    def _L0_xattn_ref(query, key, value, Wq, bq, Wk, bk, Wv, bv):
        import jax, jax.numpy as jnp
        import numpy as np
        B, LQ, LK = (8, 256, 256)
        QD, KD, VD = (128, 64, 64)
        q = jnp.einsum('bld,de->ble', query, Wq) + bq
        k = jnp.einsum('bld,de->ble', key, Wk) + bk
        v = jnp.einsum('bld,de->ble', value, Wv) + bv
        scores = jnp.einsum('bqe,bke->bqk', q, k)
        attn = jax.nn.softmax(scores, axis=-1)
        out = jnp.einsum('bqk,bke->bqe', attn, v)
        return out

    def _L0_ffn_ref(x, norm1_w, Wq, Wk, Wv, Wo, norm2_w, router_w, router_b, W1, b1, W2, b2, W3, b3):
        import jax, jax.numpy as jnp
        import numpy as np
        D_MODEL = 128
        N_HEADS = 16
        N_GROUPS = 4
        D_FF = 512
        N_EXPERTS = 8
        TOP_K = 2
        BATCH = 2
        SEQ = 128
        D_K = D_MODEL // N_HEADS
        HPG = N_HEADS // N_GROUPS
        EPS = 1e-06

        def rms_norm(x, w):
            rms = jnp.sqrt(jnp.mean(x * x, axis=-1, keepdims=True) + EPS)
            return x / rms * w

        def rope(x):
            d = x.shape[-1]
            half = d // 2
            theta = 1.0 / 10000.0 ** (jnp.arange(half, dtype=jnp.float32) / half)
            pos = jnp.arange(x.shape[1], dtype=jnp.float32)[:, None]
            ang = pos * theta[None, :]
            cos, sin = (jnp.cos(ang), jnp.sin(ang))
            xe, xo = (x[..., 0::2], x[..., 1::2])
            return jnp.concatenate([xe * cos - xo * sin, xe * sin + xo * cos], axis=-1)

        def attention(x, Wq, Wk, Wv, Wo):
            B, S, _ = x.shape
            xr = rope(x)
            Q = (xr @ Wq).reshape(B, S, N_HEADS, D_K).transpose(0, 2, 1, 3)
            Q = Q.reshape(B, N_GROUPS, HPG, S, D_K)
            K = (xr @ Wk).reshape(B, S, N_GROUPS, D_K).transpose(0, 2, 1, 3)
            V = (xr @ Wv).reshape(B, S, N_GROUPS, D_K).transpose(0, 2, 1, 3)
            scores = jnp.einsum('bghsd,bgtd->bghst', Q, K) / jnp.sqrt(jnp.float32(D_K))
            mask = jnp.triu(jnp.full((S, S), -1000000000.0, dtype=scores.dtype), k=1)
            attn = jax.nn.softmax(scores + mask, axis=-1)
            out = jnp.einsum('bghst,bgtd->bghsd', attn, V)
            out = out.reshape(B, N_HEADS, S, D_K).transpose(0, 2, 1, 3).reshape(B, S, D_MODEL)
            return out @ Wo

        def moe(x, router_w, router_b, W1, b1, W2, b2, W3, b3):
            B, S, _ = x.shape
            logits = x @ router_w + router_b
            topv, topi = jax.lax.top_k(logits, TOP_K)
            topw = jax.nn.softmax(topv, axis=-1)
            onehot = jax.nn.one_hot(topi, N_EXPERTS, dtype=x.dtype)
            comb = jnp.einsum('bsk,bske->bse', topw, onehot)
            h1 = jnp.einsum('bsd,edf->ebsf', x, W1) + b1[:, None, None, :]
            h2 = jnp.einsum('bsd,edf->ebsf', x, W2) + b2[:, None, None, :]
            h = h2 * jax.nn.silu(h1)
            eo = jnp.einsum('ebsf,efd->ebsd', h, W3) + b3[:, None, None, :]
            return jnp.einsum('bse,ebsd->bsd', comb, eo)
        h = x + attention(rms_norm(x, norm1_w), Wq, Wk, Wv, Wo)
        h = h + moe(rms_norm(h, norm2_w), router_w, router_b, W1, b1, W2, b2, W3, b3)
        return h
    x = _layernorm(x + _L0_attn_ref(x, L0_attn_Wq, L0_attn_Wk, L0_attn_Wv, L0_attn_Wo), axis=-1)
    x = _layernorm(x + _L0_xattn_ref(x, ctx_512, ctx_512, L0_xattn_Wq, L0_xattn_bq, L0_xattn_Wk, L0_xattn_bk, L0_xattn_Wv, L0_xattn_bv), axis=-1)
    x = _layernorm(x + _L0_ffn_ref(x, L0_ffn_norm1_w, L0_ffn_Wq, L0_ffn_Wk, L0_ffn_Wv, L0_ffn_Wo, L0_ffn_norm2_w, L0_ffn_router_w, L0_ffn_router_b, L0_ffn_W1, L0_ffn_b1, L0_ffn_W2, L0_ffn_b2, L0_ffn_W3, L0_ffn_b3), axis=-1)
    return x

_drawn_inputs = setup_inputs


def setup_inputs(seed=0):
    import zlib

    import numpy as np

    out = dict(_drawn_inputs(seed))
    spreads = {'L0_xattn_bq': (0.0, 0.8),
     'L0_xattn_bk': (0.0, 2.0),
     'L0_xattn_bv': (0.0, 0.1),
     'L0_ffn_norm1_w': (1.0, 0.6),
     'L0_ffn_norm2_w': (1.0, 0.6),
     'L0_ffn_router_b': (0.0, 0.424),
     'L0_ffn_b1': (0.0, 0.8),
     'L0_ffn_b2': (0.0, 0.8),
     'L0_ffn_b3': (0.0, 0.8)}
    factors = {'L0_xattn_Wq': 3.818,
     'L0_xattn_Wk': 3.557,
     'L0_ffn_Wq': 8.0,
     'L0_ffn_Wk': 8.0,
     'L0_ffn_Wv': 6.505,
     'L0_ffn_Wo': 6.325,
     'L0_ffn_W1': 8.0,
     'L0_ffn_W2': 8.0,
     'L0_ffn_W3': 8.0}
    for name, (base, spread) in spreads.items():
        noise = np.random.default_rng([zlib.crc32(name.encode()), seed]).standard_normal(out[name].shape)
        drawn = base * np.exp(spread * noise) if base else spread * noise
        out[name] = jnp.asarray(drawn.astype(out[name].dtype))
    for name, factor in factors.items():
        out[name] = (out[name] * factor).astype(out[name].dtype)
    return out
```

```python
import concourse.bass as bass
from concourse import mybir
from contextlib import ExitStack

P = 128
NB, S, D = 32, 64, 128
T = NB * S // P
H, DH = 16, 8
G4, J4 = 4, 4
SLOT = P // J4
PAIRS = H // 2
VW = DH + 1
GR = 4
NG = T // GR
CD = 64
E, F, FC = 8, 512, 4
ROWS = NB * S
REGION = ROWS + P
NBLK = (2 * ROWS + E * (P - 1)) // P
XW = D + 1
EPS_LN, EPS_RMS = 1e-5, 1e-6

fp32, bf16, f16 = mybir.dt.float32, mybir.dt.bfloat16, mybir.dt.float16
i32, u32 = mybir.dt.int32, mybir.dt.uint32
ALU = mybir.AluOpType
ACT = mybir.ActivationFunctionType
X = mybir.AxisListType.X


def program(nc, a, out):
    ctx = ExitStack()
    with ctx:
        def sb(name, shape, dt=fp32):
            return ctx.enter_context(nc.sbuf_tensor(name, shape, dt))

        def sem(name):
            return ctx.enter_context(nc.semaphore(name))

        bank = [ctx.enter_context(nc.psum_tensor(f"bank{i}", [P, 512], fp32)) for i in range(8)]
        x_rows = nc.dram_tensor("x_rows", [(E + 1) * REGION, XW], fp32, kind="Internal").ap()
        y_rows = nc.dram_tensor("y_rows", [2 * ROWS, D], fp32, kind="Internal").ap()

        x_in = sb("x_in", [P, T, D])
        x_res = sb("x_res", [P, T, D])
        xT = sb("xT", [P, T * P])
        xT_tile = sb("xT_tile", [P, 2, 2, 2, S])
        r_tile = sb("r_tile", [P, D])
        stats_tile = sb("stats_tile", [P, 6])
        stats = sb("stats", [P, T, 6])
        wqk = [sb(f"wqk{k}", [P, 2, D]) for k in range(2)]
        wv = [sb(f"wv{k}", [P, D]) for k in range(2)]
        wo = [sb(f"wo{k}", [P, D]) for k in range(2)]
        wkv_g = sb("wkv_g", [P, 2, 32])
        wmean = sb("wmean", [P, 32])
        xwq = sb("xwq", [P, D])
        xwk = sb("xwk", [CD, D])
        xwv = sb("xwv", [CD, D])
        xbq = sb("xbq", [P, 1])
        xbk = sb("xbk", [P, 1])
        xbv = sb("xbv", [P, D])
        w1 = sb("w1", [P, E, F])
        w2 = sb("w2", [P, E, F])
        w3 = sb("w3", [P, E, FC, D])
        rw = sb("rw", [P, E])
        rb = sb("rb", [P, E])
        n1w = sb("n1w", [P, D])
        n2w = sb("n2w", [P, D])
        bias = sb("bias", [3 * E, 2 * F + D])
        bias_hi = sb("bias_hi", [3 * E, 2 * F + D], bf16)
        bias_rest = sb("bias_rest", [3 * E, 2 * F + D])
        bias_mid = sb("bias_mid", [3 * E, 2 * F + D], bf16)
        bias_lo = sb("bias_lo", [3 * E, 2 * F + D])
        bias3 = sb("bias3", [3 * E, 2 * F + D], bf16)
        part_sel = sb("part_sel", [3 * E, 3])
        ident = sb("ident", [P, P])
        ident2 = sb("ident2", [P, S])
        vmask = sb("vmask", [P, 2 * H, 2])
        slot_mask = sb("slot_mask", [P, J4, S])
        causal_q = sb("causal_q", [P, P], f16)
        causal_k = sb("causal_k", [P, J4, S], f16)
        rope = sb("rope", [P, 3, D // 2])
        rope_e = sb("rope_e", [P, 2, D // 2])
        rope_o = sb("rope_o", [P, 2, D // 2])
        before = sb("before", [P, P])
        ones = sb("ones", [P, P])
        expert_m8 = sb("expert_m8", [P, E])
        expert_row = sb("expert_row", [P, E])
        blk128 = sb("blk128", [P, T])
        blk_id = sb("blk_id", [P, NBLK])
        expert_sel = sb("expert_sel", [3 * E, E, P], f16)
        neg_half = sb("neg_half", [P, T])
        pad_rows = sb("pad_rows", [P, XW])
        tri = sb("tri", [P, E, E])
        out_row = sb("out_row", [P, T, 2])
        q_nat = sb("q_nat", [P, 2, H, SLOT])
        squares = sb("squares", [P, 2, D])
        var = sb("var", [P, 2 * H])
        qT = sb("qT", [P, G4, P])
        kT = sb("kT", [P, G4, S])
        k_diag = sb("k_diag", [P, G4, J4, S])
        v_diag = sb("v_diag", [P, T, PAIRS, 2, 2, VW])
        row_max = sb("row_max", [P, 2, 8])
        probs = sb("probs", [P, H, S])
        probsT = sb("probsT", [P, PAIRS, P])
        inv_sum = sb("inv_sum", [P, H])
        o_nat = sb("o_nat", [P, H, DH])
        oT = sb("oT", [P, P])

        ctxT = sb("ctxT", [CD, T * P])
        s_ctx = sem("ctx_loaded")
        s_x = sem("x_loaded"); s_const = sem("const_loaded"); s_aw = sem("attn_weights_loaded")
        s_xw = sem("xattn_weights_loaded"); s_mw = sem("moe_weights_loaded")
        s_prep = sem("zeros_set"); s_wprep = sem("weights_prepared"); s_link = sem("dve_link")
        s_plink = sem("pool_link")
        s_store = sem("stored")

        def view(ap):
            return ap.rearrange("(t b) s d -> (b s) t d", b=2)

        links = {s_plink: 1}

        def link(eng, ins, sm):
            links[sm] = links.get(sm, 0) + 1
            ins.then_inc(sm, 1)
            eng.wait_ge(sm, links[sm])

        CONSTS = [(ident, "ident"), (ident2, "ident2"), (vmask, "vmask"), (slot_mask, "slot_mask"), (causal_q, "causal_q"),
                  (causal_k, "causal_k"), (rope, "rope"), (before, "before"), (expert_m8, "expert_m8"),
                  (expert_row, "expert_row"), (blk128, "blk128"), (blk_id, "blk_id"), (expert_sel, "expert_sel"),
                  (pad_rows, "pad_rows"), (part_sel, "part_sel"), (tri, "tri"), (out_row, "out_row")]
        ATTN_W = [(wqk[0][:, 0, :], a["L0_attn_Wq"]), (wqk[0][:, 1, :], a["L0_attn_Wk"]), (wv[0][:], a["L0_attn_Wv"]),
                  (wo[0][:], a["L0_attn_Wo"]), (wqk[1][:, 0, :], a["L0_ffn_Wq"]), (wkv_g[:, 0, :], a["L0_ffn_Wk"]),
                  (wkv_g[:, 1, :], a["L0_ffn_Wv"]), (wo[1][:], a["L0_ffn_Wo"])]

        def row(name):
            return a[name].rearrange("(o d) -> o d", o=1)

        def col(name):
            return a[name].rearrange("(d o) -> d o", o=1)

        with nc.Block() as block:
            @block.sync
            def _(sp):
                for dst, src in ATTN_W:
                    sp.dma_start(dst, src).then_inc(s_aw, 16)
                sp.dma_start(xT[:], a["xT"]).then_inc(s_x, 16)
                sp.dma_start(x_in[:], view(a["x"])).then_inc(s_x, 16)
                sp.dma_start(ctxT[:], a["ctxT"]).then_inc(s_ctx, 16)
                for dst, src in [(xwq[:], a["L0_xattn_Wq"]), (xwk[:], a["L0_xattn_Wk"]), (xwv[:], a["L0_xattn_Wv"]),
                                 (xbq[:], col("L0_xattn_bq")), (xbk[:], col("L0_xattn_bk")),
                                 (xbv[:], row("L0_xattn_bv").broadcast_to([P, D])),
                                 (n1w[:], row("L0_ffn_norm1_w").broadcast_to([P, D])),
                                 (n2w[:], row("L0_ffn_norm2_w").broadcast_to([P, D])),
                                 (rb[:], row("L0_ffn_router_b").broadcast_to([P, E])),
                                 (rw[:], a["L0_ffn_router_w"])]:
                    sp.dma_start(dst, src).then_inc(s_xw, 16)
                sp.dma_start(w1[:], a["L0_ffn_W1"].rearrange("e d f -> d e f")).then_inc(s_mw, 16)
                sp.dma_start(w2[:], a["L0_ffn_W2"].rearrange("e d f -> d e f")).then_inc(s_mw, 16)
                sp.dma_start(w3[:], a["L0_ffn_W3"].rearrange("e (c p) d -> p e c d", p=P)).then_inc(s_mw, 16)
                for r in range(3):
                    for o, w, n in ((0, F, "b1"), (F, F, "b2"), (2 * F, D, "b3")):
                        sp.dma_start(bias[r * E:(r + 1) * E, o:o + w], a["L0_ffn_" + n]).then_inc(s_mw, 16)

            @block.scalar
            def _(act):
                for dst, name in CONSTS:
                    act.dma_start(dst[:], a[name]).then_inc(s_const, 16)

            @block.gpsimd
            def _(pool):
                nc.gpsimd.memset(v_diag[:], 0.0).then_inc(s_plink, 1)
                nc.gpsimd.memset(neg_half[:], -0.5)
                nc.gpsimd.memset(ones[:], 1.0).then_inc(s_prep, 1)

            @block.vector
            def _(dve):
                nc.vector.memset(q_nat[:], 0.0).then_inc(s_prep, 1)
                dve.wait_ge(s_aw, 16 * len(ATTN_W))
                w = wqk[0][:].rearrange("p a (h d) -> p (a h) d", d=DH)
                link(dve, nc.vector.tensor_reduce(wmean[:], w, X, ALU.add), s_link)
                link(dve, nc.vector.tensor_scalar(wmean[:], wmean[:], 1.0 / DH, None, ALU.mult), s_link)
                link(dve, nc.vector.tensor_tensor(w, w, wmean[:].unsqueeze(2).broadcast_to([P, 32, DH]), ALU.subtract), s_link)
                nc.vector.tensor_scalar(wqk[0][:, 1, :], wqk[0][:, 1, :], 1.0 / DH, None, ALU.mult)
                for dst, k, f in ((wqk[1][:, 1, :], 0, float(DH) ** -0.5), (wv[1][:], 1, 1.0)):
                    src = wkv_g[:, k, :].rearrange("p (g d) -> p g d", d=DH).unsqueeze(2).broadcast_to([P, G4, J4, DH])
                    last = nc.vector.tensor_scalar(dst.rearrange("p (g j d) -> p g j d", g=G4, j=J4), src, f, None, ALU.mult)
                last.then_inc(s_wprep, 1)
                dve.wait_ge(s_plink, 1)
                for h2 in range(2):
                    last = nc.vector.memset(v_diag[64 * h2:64 * h2 + 64, :, :, :, h2, DH:VW], 1.0)
                last.then_inc(s_prep, 1)

        def attention(k, x_src):
            nm = f"a{k}_"
            s_xt = sem(nm + "xT_tile_ready")
            s_proj = sem(nm + "proj_ready")
            s_nat = sem(nm + "slots_ready")
            s_var = sem(nm + "var_ready")
            s_bt = sem(nm + "qkT_ready")
            s_qT = sem(nm + "qT_copied")
            s_kT = sem(nm + "kT_copied")
            s_kd = sem(nm + "k_diag_ready")
            s_sc = sem(nm + "scores_ready")
            s_mx = sem(nm + "max_ready")
            s_sh = sem(nm + "scores_shifted")
            s_ex = sem(nm + "probs_ready")
            s_pt = sem(nm + "probsT_ready")
            s_ps = sem(nm + "probsT_copied")
            s_pv = sem(nm + "pv_ready")
            s_iv = sem(nm + "inv_sum_ready")
            s_on = sem(nm + "o_normalised")
            s_ot = sem(nm + "oT_ready")
            s_oc = sem(nm + "oT_copied")
            s_wo = sem(nm + "wo_ready")
            s_rs = sem(nm + "residual_ready")
            s_st = sem(nm + "stats_ready")
            s_vr = sem(nm + "var_summed")
            W = P // 2

            def pe_project(pe, t, buf):
                pe.wait_ge(s_xt, t + 1)
                cols = xT_tile[:, buf].rearrange("p b r s -> p (b r s)")
                nc.tensor.matmul(bank[0][:, 0:2 * D], cols[:, S:3 * S], wqk[k][:].rearrange("p a d -> p (a d)"),
                                 start=True, stop=True)
                for b in range(2):
                    last = nc.tensor.matmul(bank[0][:, (2 + b) * D:(3 + b) * D], cols[:, 2 * b * S:2 * (b + 1) * S], wv[k][:], start=True, stop=True)
                last.then_inc(s_proj, 1)

            def pe_transpose_qk(pe, t):
                pe.wait_ge(s_nat, t + 1)
                if k == 0:
                    pe.wait_ge(s_var, t + 1)
                for g in range(G4):
                    nc.tensor.transpose(bank[2][:, g * P:(g + 1) * P],
                                        q_nat[:, 0, g * J4:(g + 1) * J4, :].rearrange("p j s -> p (j s)"), ident[:])
                for g in range(G4):
                    last = nc.tensor.matmul(bank[1][:, g * S:(g + 1) * S],
                                            q_nat[:, 1, g * J4:(g + 1) * J4, :].rearrange("p j s -> p (j s)"), ident2[:],
                                            start=True, stop=True)
                last.then_inc(s_bt, 1)

            def pe_scores(pe, t):
                pe.wait_ge(s_qT, t + 1)
                pe.wait_ge(s_kd, t + 1)
                for half in range(2):
                    for g2 in range(2):
                        g = 2 * half + g2
                        dst = bank[4 + half][:, g2 * 256:(g2 + 1) * 256]
                        if k == 1:
                            nc.tensor.matmul(dst, causal_q[:], causal_k[:].rearrange("p h s -> p (h s)"), start=True, stop=False)
                        last = nc.tensor.matmul(dst, qT[:, g, :], k_diag[:, g, :, :].rearrange("p j s -> p (j s)"),
                                                start=(k == 0), stop=True)
                    last.then_inc(s_sc, 1)

            def pe_transpose_probs(pe, t):
                for half in range(2):
                    pe.wait_ge(s_ex, 2 * t + half + 1)
                    for q in range(4):
                        pr = 4 * half + q
                        last = nc.tensor.transpose(bank[6 + half][:, q * P:(q + 1) * P],
                                                   probs[:, 2 * pr:2 * pr + 2, :].rearrange("p h s -> p (h s)"), ident[:])
                    last.then_inc(s_pt, 1)

            def pe_pv(pe, t, residual_done):
                pe.wait_ge(s_ps, 2 * t + 2)
                if residual_done:
                    pe.wait_ge(s_rs, t)
                for pr in range(PAIRS):
                    last = nc.tensor.matmul(bank[3][:, pr * 4 * VW:(pr + 1) * 4 * VW], probsT[:, pr, :],
                                            v_diag[:, t, pr, :, :, :].rearrange("p b h w -> p (b h w)"),
                                            start=True, stop=True)
                last.then_inc(s_pv, 1)

            def pe_transpose_o(pe, t, qT_count):
                pe.wait_ge(s_on, t + 1)
                pe.wait_ge(s_qT, qT_count)
                nc.tensor.transpose(bank[2][:, 0:P], o_nat[:].rearrange("p h d -> p (h d)"), ident[:]).then_inc(s_ot, 1)

            def pe_out(pe, t):
                pe.wait_ge(s_oc, t + 1)
                nc.tensor.matmul(bank[3][:, 0:D], oT[:], wo[k][:], start=True, stop=True).then_inc(s_wo, 1)

            def act_slots(act, t):
                act.wait_ge(s_proj, t + 1)
                for b in range(2):
                    nc.scalar.activation(
                        q_nat[b * W:(b + 1) * W, :, :, b * DH:(b + 1) * DH].rearrange("p a h d -> p (a h) d"),
                        bank[0][b * W:(b + 1) * W, 0:2 * D].rearrange("p (h d) -> p h d", d=DH), ACT.Copy)
                if k == 0:
                    nc.scalar.activation(squares[:].rearrange("p a d -> p (a d)"), bank[0][:, 0:2 * D], ACT.Square)
                for h2 in range(2):
                    src = bank[0][h2 * W:(h2 + 1) * W, 2 * D:4 * D].rearrange("p (b q h d) -> p b q h d", b=2, q=PAIRS, h=2)
                    last = nc.scalar.activation(
                        v_diag[h2 * W:(h2 + 1) * W, t, :, :, h2, 0:DH].rearrange("p q b d -> p b q d"),
                        src[:, :, :, h2, :], ACT.Copy)
                last.then_inc(s_nat, 1)

            def act_qT(act, t):
                act.wait_ge(s_bt, t + 1)
                nc.scalar.activation(qT[:].rearrange("p g q -> p (g q)"), bank[2][:], ACT.Copy).then_inc(s_qT, 1)

            def act_exp(act, t, half):
                act.wait_ge(s_sh, 2 * t + half + 1)
                p = probs[:, 8 * half:8 * half + 8, :].rearrange("p h s -> p (h s)")
                nc.scalar.activation(p, p, ACT.Exp).then_inc(s_ex, 1)

            def act_probsT(act, t, half):
                act.wait_ge(s_pt, 2 * t + half + 1)
                nc.scalar.activation(probsT[:, 4 * half:4 * half + 4, :].rearrange("p h s -> p (h s)"), bank[6 + half][:],
                                     ACT.Copy).then_inc(s_ps, 1)

            def act_oT(act, t):
                act.wait_ge(s_ot, t + 1)
                nc.scalar.activation(oT[:], bank[2][:, 0:P], ACT.Copy).then_inc(s_oc, 1)

            def dve_softmax(dve, t):
                for half in range(2):
                    dve.wait_ge(s_sc, 2 * t + half + 1)
                    sc = bank[4 + half][:].rearrange("p (h s) -> p h s", s=S)
                    nc.vector.tensor_reduce(row_max[:, half, :], sc, X, ALU.max).then_inc(s_mx, 1)
                    dve.wait_ge(s_mx, 2 * t + half + 1)
                    nc.vector.tensor_tensor(probs[:, 8 * half:8 * half + 8, :], sc,
                                            row_max[:, half, :].unsqueeze(2).broadcast_to([P, 8, S]),
                                            ALU.subtract).then_inc(s_sh, 1)

            def dve_kT(dve, t):
                dve.wait_ge(s_bt, t + 1)
                nc.vector.tensor_copy(kT[:].rearrange("p g s -> p (g s)"), bank[1][:, 0:G4 * S]).then_inc(s_kT, 1)

            def dve_var(dve, t):
                if k == 1:
                    return
                dve.wait_ge(s_nat, t + 1)
                nc.vector.tensor_reduce(var[:], squares[:].rearrange("p a (h d) -> p (a h) d", d=DH), X,
                                        ALU.add).then_inc(s_vr, 1)
                dve.wait_ge(s_vr, t + 1)
                nc.vector.tensor_tensor(q_nat[:, :, :, 2 * DH:2 * DH + 2].rearrange("p a h b -> p (a h) b"),
                                        var[:].unsqueeze(2).broadcast_to([P, 2 * H, 2]), vmask[:],
                                        ALU.mult).then_inc(s_var, 1)

            def dve_normalise(dve, t):
                dve.wait_ge(s_pv, t + 1)
                o = bank[3][:, 0:PAIRS * 4 * VW].rearrange("p (q b h w) -> p q b h w", b=2, h=2, w=VW)
                for b in range(2):
                    r = slice(b * W, (b + 1) * W)
                    last = nc.vector.reciprocal(inv_sum[r, :].rearrange("p (q h) -> p q h", h=2), o[r, :, b, :, DH])
                last.then_inc(s_iv, 1)
                dve.wait_ge(s_iv, t + 1)
                for b in range(2):
                    r = slice(b * W, (b + 1) * W)
                    last = nc.vector.tensor_tensor(
                        o_nat[r].rearrange("p (q h) d -> p q h d", h=2), o[r, :, b, :, 0:DH],
                        inv_sum[r, :].rearrange("p (q h) -> p q h", h=2).unsqueeze(3).broadcast_to([W, PAIRS, 2, DH]),
                        ALU.mult)
                last.then_inc(s_on, 1)

            def dve_residual(dve, t):
                dve.wait_ge(s_wo, t + 1)
                nc.vector.tensor_tensor(r_tile[:], bank[3][:, 0:D], x_src[:, t, :], ALU.add).then_inc(s_rs, 1)
                dve.wait_ge(s_rs, t + 1)
                nc.vector.tensor_copy(x_res[:, t, :], r_tile[:])
                nc.vector.bn_stats(stats_tile[:], r_tile[:]).then_inc(s_st, 1)
                dve.wait_ge(s_st, t + 1)
                nc.vector.tensor_copy(stats[:, t, :], stats_tile[:])

            def pool_xT(pool, t, buf, need):
                if need is not None:
                    pool.wait_ge(s_proj, need)
                    pool.nop(nofuse=True)
                src = xT[:, bass.ds(t * P, P)].rearrange("p (b s) -> p b s", b=2).unsqueeze(2).broadcast_to([P, 2, 2, S])
                nc.gpsimd.tensor_copy(xT_tile[:, buf], src).then_inc(s_xt, 1)

            def pool_diag(pool, t):
                pool.wait_ge(s_kT, t + 1)
                pool.nop(nofuse=True)
                src = kT[:].unsqueeze(2).broadcast_to([P, G4, J4, S])
                own = slot_mask[:].unsqueeze(1).broadcast_to([P, G4, J4, S])
                last = nc.gpsimd.tensor_tensor(k_diag[:], src, own, ALU.mult)
                last.then_inc(s_kd, 1)

            def pe_step(pe, n, buf, prev=True, nxt=True, nxt2=True):
                pe_scores(pe, n)
                if prev:
                    pe_pv(pe, n - 1, prev != "first")
                if nxt:
                    pe_transpose_qk(pe, n + 1)
                if nxt2:
                    pe_project(pe, n + 2, buf)
                if prev:
                    pe_transpose_o(pe, n - 1, n + 2 if nxt else n + 1)
                pe_transpose_probs(pe, n)
                if prev:
                    pe_out(pe, n - 1)

            def act_step(act, n, prev=True, nxt=True, nxt2=True):
                act_exp(act, n, 0)
                if nxt:
                    act_qT(act, n + 1)
                act_exp(act, n, 1)
                if nxt2:
                    act_slots(act, n + 2)
                if prev:
                    act_oT(act, n - 1)
                act_probsT(act, n, 0)
                act_probsT(act, n, 1)

            def dve_step(dve, n, prev=True, nxt=True, nxt2=True):
                dve_softmax(dve, n)
                if nxt:
                    dve_kT(dve, n + 1)
                if prev:
                    dve_normalise(dve, n - 1)
                if nxt2:
                    dve_var(dve, n + 2)
                if prev:
                    dve_residual(dve, n - 1)

            with nc.Block() as block:
                @block.tensor
                def _(pe):
                    if k == 0:
                        pe.wait_ge(s_const, 16 * len(CONSTS))
                        pe.wait_ge(s_wprep, 1)
                        pe.wait_ge(s_prep, 3)
                    pe_project(pe, 0, 0)
                    pe_transpose_qk(pe, 0)
                    pe_project(pe, 1, 1)
                    pe_step(pe, 0, 0, prev=False)
                    pe_step(pe, 1, 1, prev="first")
                    with pe.Fori(1, T // 2 - 1) as i:
                        for u in range(2):
                            pe_step(pe, 2 * i + u, u)
                    pe_step(pe, T - 2, 0, nxt2=False)
                    pe_step(pe, T - 1, 1, nxt=False, nxt2=False)
                    pe_pv(pe, T - 1, True)
                    pe_transpose_o(pe, T - 1, T)
                    pe_out(pe, T - 1)

                @block.scalar
                def _(act):
                    if k == 0:
                        act.wait_ge(s_prep, 3)
                    act_slots(act, 0)
                    act_qT(act, 0)
                    act_slots(act, 1)
                    act_step(act, 0, prev=False)
                    with act.Fori(1, T - 2) as n:
                        act_step(act, n)
                    act_step(act, T - 2, nxt2=False)
                    act_step(act, T - 1, nxt=False, nxt2=False)
                    act_oT(act, T - 1)

                @block.vector
                def _(dve):
                    if k == 0:
                        dve.wait_ge(s_const, 16 * len(CONSTS))
                        dve.wait_ge(s_x, 32)
                    dve_var(dve, 0)
                    dve_kT(dve, 0)
                    dve_var(dve, 1)
                    dve_step(dve, 0, prev=False)
                    with dve.Fori(1, T - 2) as n:
                        dve_step(dve, n)
                    dve_step(dve, T - 2, nxt2=False)
                    dve_step(dve, T - 1, nxt=False, nxt2=False)
                    dve_normalise(dve, T - 1)
                    dve_residual(dve, T - 1)

                @block.gpsimd
                def _(pool):
                    if k == 0:
                        pool.wait_ge(s_x, 32)
                        pool.wait_ge(s_const, 16 * len(CONSTS))
                        pool.wait_ge(s_prep, 3)
                    pool_xT(pool, 0, 0, None)
                    pool_xT(pool, 1, 1, None)
                    pool_diag(pool, 0)
                    pool_xT(pool, 2, 0, 1)
                    pool_diag(pool, 1)
                    pool_xT(pool, 3, 1, 2)
                    with pool.Fori(1, T // 2 - 1) as i:
                        for u in range(2):
                            pool_diag(pool, 2 * i + u)
                            pool_xT(pool, 2 * i + u + 2, u, 2 * i + u + 1)
                    pool_diag(pool, T - 2)
                    pool_diag(pool, T - 1)

        attention(0, x_in)


        def dve_mean_var(dve, st, mean, var_eps, scr, eps, sm):
            nc.vector.tensor_tensor(mean, st[:, :, 1], st[:, :, 4], ALU.add)
            nc.vector.tensor_tensor(scr, st[:, :, 1], st[:, :, 4], ALU.subtract)
            link(dve, nc.vector.tensor_tensor(var_eps, st[:, :, 2], st[:, :, 5], ALU.add), sm)
            nc.vector.tensor_scalar(mean, mean, 0.5, None, ALU.mult)
            nc.vector.tensor_scalar(var_eps, var_eps, 1.0 / D, eps, ALU.mult, ALU.add)
            link(dve, nc.vector.scalar_tensor_tensor(out=scr, in0=scr, scalar=0.25, in1=scr, op0=ALU.mult, op1=ALU.mult), sm)
            return nc.vector.tensor_tensor(var_eps, var_eps, scr, ALU.add)

        def per_token(ap, width=D):
            return ap.unsqueeze(2).broadcast_to([P, ap.shape[1], width])

        xaT = [sb(f"xaT{i}", [P, GR * P]) for i in range(2)]
        xq = [sb(f"xq{i}", [P, GR, P]) for i in range(2)]
        xk = [sb(f"xk{i}", [P, GR, P]) for i in range(2)]
        xv = sb("xv", [P, T, D])
        xp = [sb(f"xp{i}", [P, GR, P]) for i in range(2)]
        xpT = sb("xpT", [P, GR, P])
        xmax = sb("xmax", [P, GR])
        xsum = [sb(f"xsum{i}", [P, GR]) for i in range(2)]
        mean = sb("mean", [P, T]); rstd = sb("rstd", [P, T]); vscr = sb("vscr", [P, T])
        xst = sb("xst", [P, GR, 6])
        gmean = sb("gmean", [P, GR]); gvar = sb("gvar", [P, GR]); gscr = sb("gscr", [P, GR]); grstd = sb("grstd", [P, GR])
        gms = sb("gms", [P, GR]); grms = sb("grms", [P, GR])
        gsq = sb("gsq", [P, GR, D])
        ra = sb("ra", [P, GR, 2, D // 2])
        rb_ = sb("rb_", [P, GR, 2, D // 2])
        xr = sb("xr", [P, GR, D])

        def cross_attention():
            s_va = sem("x_var_ready")
            s_rd = sem("x_rstd_ready")
            s_z = sem("x_zeros_set")
            s_rp = sem("x_rope_tables")
            s_xn = sem("x_normed")
            s_ht = sem("x_xT_ready")
            s_hc = sem("x_xT_copied")
            s_q = sem("x_qkv_ready")
            s_qc = sem("x_qk_copied")
            s_v = sem("x_v_copied")
            s_s = sem("x_scores_ready")
            s_sh = sem("x_scores_shifted")
            s_e = sem("x_probs_ready")
            s_t = sem("x_probsT_ready")
            s_tc = sem("x_probsT_copied")
            s_p = sem("x_pv_ready")
            s_x2 = sem("x_residual_ready")
            s_gv = sem("x_gvar_ready")
            s_gr = sem("x_grstd_ready")
            s_x3 = sem("x_x3_ready")
            s_sq = sem("x_squares_ready")
            s_ms = sem("x_ms_ready")
            s_rr = sem("x_rope_ready")
            s_xr = sem("x_xr_ready")
            s_rt = sem("x_xrT_ready")
            s_rc = sem("x_xrT_copied")
            order = []
            for g in range(NG + 2):
                order += [("H", g)] if g < NG else []
                order += [("M", g - 1)] if 1 <= g <= NG else []
                order += [("T", g - 2)] if g >= 2 else []

            def tiles(g):
                return slice(g * GR, (g + 1) * GR)

            with nc.Block() as block:
                @block.tensor
                def _(pe):
                    pe.wait_ge(s_ctx, 16)
                    pe.wait_ge(s_xw, 160)
                    for part, g in order:
                        b = g % 2
                        if part == "H":
                            pe.wait_ge(s_xn, g + 1)
                            for i in range(GR):
                                last = nc.tensor.transpose(bank[0][:, i * P:(i + 1) * P], x_res[:, g * GR + i, :], ident[:])
                            last.then_inc(s_ht, 1)
                            cg = slice(g * GR * P, (g + 1) * GR * P)
                            if g:
                                pe.wait_ge(s_qc, g)
                                pe.wait_ge(s_v, g)
                            nc.tensor.matmul(bank[2][:], xwk[:], ctxT[:, cg], start=True, stop=True)
                            for i in range(GR):
                                t = g * GR + i
                                last = nc.tensor.matmul(bank[3][:, i * P:(i + 1) * P], ctxT[:, t * P:(t + 1) * P], xwv[:],
                                                        start=True, stop=True)
                            last.then_inc(s_q, 1)
                            pe.wait_ge(s_hc, g + 1)
                            nc.tensor.matmul(bank[1][:], xwq[:], xaT[b][:], start=True, stop=True).then_inc(s_q, 1)
                        if part == "M":
                            pe.wait_ge(s_qc, g + 1)
                            if g:
                                pe.wait_ge(s_sh, g)
                            for i in range(GR):
                                last = nc.tensor.matmul(bank[4][:, i * P:(i + 1) * P], xq[b][:, i, :], xk[b][:, i, :],
                                                        start=True, stop=True)
                            last.then_inc(s_s, 1)
                            pe.wait_ge(s_e, g + 1)
                            if g:
                                pe.wait_ge(s_tc, g)
                            for i in range(GR):
                                last = nc.tensor.transpose(bank[5][:, i * P:(i + 1) * P], xp[b][:, i, :], ident[:])
                            last.then_inc(s_t, 1)
                            pe.wait_ge(s_tc, g + 1)
                            pe.wait_ge(s_v, g + 1)
                            if g:
                                pe.wait_ge(s_x2, g)
                            for i in range(GR):
                                last = nc.tensor.matmul(bank[6][:, i * P:(i + 1) * P], xpT[:, i, :], xv[:, g * GR + i, :],
                                                        start=True, stop=True)
                            last.then_inc(s_p, 1)
                        if part == "T":
                            pe.wait_ge(s_xr, g + 1)
                            if g:
                                pe.wait_ge(s_rc, g)
                            for i in range(GR):
                                last = nc.tensor.transpose(bank[7][:, i * P:(i + 1) * P], xr[:, i, :], ident[:])
                            last.then_inc(s_rt, 1)

                @block.scalar
                def _(act):
                    act.wait_ge(s_z, 1)
                    for part, g in order:
                        b = g % 2
                        if part == "H":
                            act.wait_ge(s_ht, g + 1)
                            nc.scalar.activation(xaT[b][:], bank[0][:], ACT.Copy).then_inc(s_hc, 1)
                            act.wait_ge(s_q, 2 * g + 1)
                            nc.scalar.activation(xk[b][:].rearrange("p i q -> p (i q)"), bank[2][:], ACT.Identity, bias=xbk[:, 0:1])
                            act.wait_ge(s_q, 2 * g + 2)
                            nc.scalar.activation(xq[b][:].rearrange("p i q -> p (i q)"), bank[1][:], ACT.Identity,
                                                 bias=xbq[:, 0:1]).then_inc(s_qc, 1)
                        if part == "M":
                            act.wait_ge(s_sh, g + 1)
                            for h in range(2):
                                r = slice(64 * h, 64 * h + 64)
                                last = nc.scalar.activation(xp[b][r, :, r], xp[b][r, :, r], ACT.Exp)
                            last.then_inc(s_e, 1)
                            act.wait_ge(s_t, g + 1)
                            nc.scalar.activation(xpT[:].rearrange("p i q -> p (i q)"), bank[5][:], ACT.Copy).then_inc(s_tc, 1)
                        if part == "T":
                            act.wait_ge(s_x3, g + 1)
                            if g:
                                act.wait_ge(s_ms, g)
                            nc.scalar.activation(gsq[:], x_in[:, tiles(g), :], ACT.Square).then_inc(s_sq, 1)
                            act.wait_ge(s_rt, g + 1)
                            nc.scalar.activation(xT[:, g * GR * P:(g + 1) * GR * P], bank[7][:], ACT.Copy).then_inc(s_rc, 1)

                @block.vector
                def _(dve):
                    nc.vector.memset(q_nat[:, :, :, 2 * DH:2 * DH + 2], 0.0)
                    dve_mean_var(dve, stats, mean[:], rstd[:], vscr[:], EPS_LN, s_link).then_inc(s_va, 1)
                    dve.wait_ge(s_rd, 1)
                    for part, g in order:
                        b = g % 2
                        tg = tiles(g)
                        if part == "H":
                            xs = x_res[:, tg, :]
                            link(dve, nc.vector.tensor_tensor(xs, xs, per_token(mean[:, tg]), ALU.subtract), s_link)
                            nc.vector.tensor_tensor(xs, xs, per_token(rstd[:, tg]), ALU.mult).then_inc(s_xn, 1)
                            dve.wait_ge(s_q, 2 * g + 1)
                            nc.vector.tensor_tensor(xv[:, tg, :], bank[3][:].rearrange("p (i d) -> p i d", i=GR),
                                                    xbv[:].unsqueeze(1).broadcast_to([P, GR, D]), ALU.add).then_inc(s_v, 1)
                        if part == "M":
                            dve.wait_ge(s_s, g + 1)
                            s4 = bank[4][:].rearrange("p (i k) -> p i k", i=GR)
                            for h in range(2):
                                r = slice(64 * h, 64 * h + 64)
                                last = nc.vector.tensor_reduce(xmax[r, :], s4[r, :, r], X, ALU.max)
                            link(dve, last, s_link)
                            for h in range(2):
                                r = slice(64 * h, 64 * h + 64)
                                last = nc.vector.tensor_tensor(xp[b][r, :, r], s4[r, :, r],
                                                               xmax[r, :].unsqueeze(2).broadcast_to([64, GR, S]), ALU.subtract)
                            last.then_inc(s_sh, 1)
                            dve.wait_ge(s_e, g + 1)
                            link(dve, nc.vector.tensor_reduce(xsum[b][:], xp[b][:], X, ALU.add), s_link)
                            link(dve, nc.vector.reciprocal(xsum[b][:], xsum[b][:]), s_link)
                            dve.wait_ge(s_p, g + 1)
                            for i in range(GR):
                                last = nc.vector.scalar_tensor_tensor(
                                    out=x_res[:, g * GR + i, :], in0=bank[6][:, i * P:(i + 1) * P], scalar=xsum[b][:, i:i + 1],
                                    in1=x_res[:, g * GR + i, :], op0=ALU.mult, op1=ALU.add)
                            last.then_inc(s_x2, 1)
                        if part == "T":
                            dve.wait_ge(s_x2, g + 1)
                            for i in range(GR):
                                last = nc.vector.bn_stats(xst[:, i, :], x_res[:, g * GR + i, :])
                            link(dve, last, s_link)
                            dve_mean_var(dve, xst, gmean[:], gvar[:], gscr[:], EPS_LN, s_link).then_inc(s_gv, 1)
                            xs, x3 = x_res[:, tg, :], x_in[:, tg, :]
                            link(dve, nc.vector.tensor_tensor(x3, xs, per_token(gmean[:]), ALU.subtract), s_link)
                            dve.wait_ge(s_gr, g + 1)
                            nc.vector.tensor_tensor(x3, x3, per_token(grstd[:]), ALU.mult).then_inc(s_x3, 1)
                            dve.wait_ge(s_sq, g + 1)
                            link(dve, nc.vector.tensor_reduce(gms[:], gsq[:], X, ALU.add), s_link)
                            nc.vector.tensor_scalar(gms[:], gms[:], 1.0 / D, EPS_RMS, ALU.mult, ALU.add).then_inc(s_ms, 1)
                            dve.wait_ge(s_rr, g + 1)
                            if g:
                                dve.wait_ge(s_rt, g)
                            nc.vector.tensor_tensor(xr[:], ra[:].rearrange("p i c d -> p i (c d)"), per_token(grms[:]),
                                                    ALU.mult).then_inc(s_xr, 1)

                @block.gpsimd
                def _(pool):
                    for b in range(2):
                        last = nc.gpsimd.memset(xp[b][:], 0.0)
                    last.then_inc(s_z, 1)
                    pool.wait_ge(s_mw, 16 * 12)
                    link(pool, nc.gpsimd.tensor_copy(bias_hi[:], bias[:]), s_plink)
                    link(pool, nc.gpsimd.tensor_tensor(bias_rest[:], bias[:], bias_hi[:], ALU.subtract), s_plink)
                    link(pool, nc.gpsimd.tensor_copy(bias_mid[:], bias_rest[:]), s_plink)
                    link(pool, nc.gpsimd.tensor_tensor(bias_lo[:], bias_rest[:], bias_mid[:], ALU.subtract), s_plink)
                    link(pool, nc.gpsimd.tensor_scalar(bias_lo[:], bias_lo[:], part_sel[:, 2:3], None, ALU.mult), s_plink)
                    for r, part in ((0, bias_hi), (1, bias_mid)):
                        link(pool, nc.gpsimd.tensor_scalar(bias_rest[:], part[:], part_sel[:, r:r + 1], None, ALU.mult), s_plink)
                        link(pool, nc.gpsimd.tensor_tensor(bias_lo[:], bias_lo[:], bias_rest[:], ALU.add), s_plink)
                    link(pool, nc.gpsimd.tensor_copy(bias3[:], bias_lo[:]), s_plink)
                    w_eo = n1w[:].rearrange("p (d e) -> p e d", e=2)
                    pool.wait_ge(s_xw, 160)
                    nc.gpsimd.tensor_tensor(rope_e[:], rope[:, 0:2, :], w_eo[:, 0, :].unsqueeze(1).broadcast_to([P, 2, D // 2]), ALU.mult)
                    nc.gpsimd.tensor_tensor(rope_o[:, 1, :], rope[:, 0, :], w_eo[:, 1, :], ALU.mult)
                    nc.gpsimd.tensor_tensor(rope_o[:, 0, :], rope[:, 2, :], w_eo[:, 1, :], ALU.mult).then_inc(s_rp, 1)
                    pool.wait_ge(s_va, 1)
                    nc.gpsimd.tensor_tensor(rstd[:], rstd[:], neg_half[:], ALU.pow).then_inc(s_rd, 1)
                    pool.wait_ge(s_rp, 1)
                    for g in range(NG):
                        pool.wait_ge(s_gv, g + 1)
                        nc.gpsimd.tensor_tensor(grstd[:], gvar[:], neg_half[:, 0:GR], ALU.pow).then_inc(s_gr, 1)
                        pool.wait_ge(s_x3, g + 1)
                        if g:
                            pool.wait_ge(s_xr, g)
                        eo = x_in[:, tiles(g), :].rearrange("p i (d e) -> p i e d", e=2)
                        for dst, e, tab in ((ra, 0, rope_e), (rb_, 1, rope_o)):
                            last = nc.gpsimd.tensor_tensor(dst[:], eo[:, :, e, :].unsqueeze(2).broadcast_to([P, GR, 2, D // 2]),
                                                           tab[:].unsqueeze(1).broadcast_to([P, GR, 2, D // 2]), ALU.mult)
                        link(pool, last, s_plink)
                        nc.gpsimd.tensor_tensor(ra[:], ra[:], rb_[:], ALU.add)
                        pool.wait_ge(s_ms, g + 1)
                        nc.gpsimd.tensor_tensor(grms[:], gms[:], neg_half[:, 0:GR], ALU.pow).then_inc(s_rr, 1)

        cross_attention()
        attention(1, x_in)

        freed = v_diag[:].rearrange("p t q b h w -> p (t q b h w)")
        xs_rows = freed[:, 0:T * 2 * XW].rearrange("p (t c w) -> p t c w", t=T, c=2)
        xnT = sb("xnT", [P, GR * P])
        lg = sb("lg", [P, GR, E]); lg2 = sb("lg2", [P, GR, E]); hit = sb("hit", [P, GR, E])
        top = sb("top", [P, 2, GR]); pick = sb("pick", [P, 2, GR])
        chosen = sb("chosen", [P, 2, GR, E])
        both = sb("both", [P, T, E])
        so_far = sb("so_far", [P, T + 1, E])
        pos = sb("pos", [P, GR, E]); pos2 = sb("pos2", [P, 2, GR, E]); slot = sb("slot", [P, 2, GR])
        slot_ids = sb("slot_ids", [P, NG, 2, GR], u32)
        gap = sb("gap", [P, GR]); share = sb("share", [P, 2, T])
        cnt = sb("cnt", [P, E]); over = sb("over", [P, E, T]); nblk = sb("nblk", [P, E]); 
        trip = sb("trip", [P, E, E]); ends = sb("ends", [P, E])
        past = sb("past", [P, NBLK, E]); past2 = sb("past2", [P, NBLK, E])
        eb = sb("eb", [P, NBLK]); sbk = sb("sbk", [P, NBLK]); inside = sb("inside", [P, NBLK]); rowf = sb("rowf", [P, NBLK])
        expf = sb("expf", [P, NBLK]); padf = sb("padf", [P, E])
        row_tab = sb("row_tab", [P, NBLK], i32); exp_tab = sb("exp_tab", [P, NBLK], i32); pad_tab = sb("pad_tab", [P, E], i32)
        s_xs = sem("rows_scattered")
        s_pad = sem("pads_written")
        s_tab = sem("block_tables_ready")

        def route():
            s_sq = sem("r_squares_ready")
            s_ms = sem("r_ms_ready")
            s_rr = sem("r_rms_ready")
            s_xn = sem("r_rows_ready")
            s_t = sem("r_xnT_ready")
            s_tc = sem("r_xnT_copied")
            s_lg = sem("r_logits_ready")
            s_ch = sem("r_choices_ready")
            s_gp = sem("r_gap_ready")
            s_ge = sem("r_gap_exp")
            s_ps = sem("r_positions_ready")
            s_sl = sem("r_slots_ready")
            s_cn = sem("r_counts_ready")

            def tiles(g):
                return slice(g * GR, (g + 1) * GR)

            with nc.Block() as block:
                @block.tensor
                def _(pe):
                    for g in range(NG):
                        pe.wait_ge(s_xn, g + 1)
                        for i in range(GR):
                            last = nc.tensor.transpose(bank[0][:, i * P:(i + 1) * P], xs_rows[:, g * GR + i, 0, 0:D], ident[:])
                        last.then_inc(s_t, 1)
                        pe.wait_ge(s_tc, g + 1)
                        for i in range(GR):
                            last = nc.tensor.matmul(bank[1][:, i * E:(i + 1) * E], xnT[:, i * P:(i + 1) * P], rw[:],
                                                    start=True, stop=True)
                        last.then_inc(s_lg, 1)
                        pe.wait_ge(s_ch, g + 1)
                        dst = bank[2][:, 0:GR * E]
                        nc.tensor.matmul(dst, before[:], both[:, tiles(g), :].rearrange("p t e -> p (t e)"), start=True, stop=False)
                        nc.tensor.matmul(dst, ones[:], so_far[:, tiles(g), :].rearrange("p t e -> p (t e)"), start=False,
                                         stop=True).then_inc(s_ps, 1)
                    nc.tensor.matmul(bank[3][:, 0:E], ones[:], so_far[:, T, :], start=True, stop=True).then_inc(s_cn, 1)

                @block.scalar
                def _(act):
                    for g in range(NG):
                        if g:
                            act.wait_ge(s_ms, g)
                        nc.scalar.activation(gsq[:], x_res[:, tiles(g), :], ACT.Square).then_inc(s_sq, 1)
                        act.wait_ge(s_t, g + 1)
                        nc.scalar.activation(xnT[:], bank[0][:], ACT.Copy).then_inc(s_tc, 1)
                        act.wait_ge(s_gp, g + 1)
                        nc.scalar.activation(gap[:], gap[:], ACT.Exp).then_inc(s_ge, 1)

                @block.gpsimd
                def _(pool):
                    for g in range(NG):
                        pool.wait_ge(s_ms, g + 1)
                        nc.gpsimd.tensor_tensor(grms[:], gms[:], neg_half[:, 0:GR], ALU.pow).then_inc(s_rr, 1)
                        pool.wait_ge(s_sl, g + 1)
                        for i in range(GR):
                            for c in range(2):
                                pool.indirect_dma_start(
                                    out=x_rows[:, :], out_offset=bass.IndirectOffsetOnAxis(ap=slot_ids[:, g, c, i:i + 1], axis=0),
                                    in_=xs_rows[:, g * GR + i, c, :], in_offset=None).then_inc(s_xs, 16)

                @block.sync
                def _(sp):
                    sp.dma_start(x_rows[E * REGION:E * REGION + P, :], pad_rows[:]).then_inc(s_pad, 16)
                    sp.wait_ge(s_tab, 1)
                    for e in range(E):
                        first = sp.value_load(pad_tab[0:1, e:e + 1], min_val=0, max_val=E * REGION - P)
                        sp.dma_start(x_rows[bass.ds(first, P), :], pad_rows[:]).then_inc(s_pad, 16)

                @block.vector
                def _(dve):
                    TT, TR, TS = nc.vector.tensor_tensor, nc.vector.tensor_reduce, nc.vector.tensor_scalar

                    def lk(ins):
                        link(dve, ins, s_link)

                    nc.vector.memset(so_far[:, 0, :], 0.0)
                    nc.vector.tensor_copy(xs_rows[:, :, :, D], out_row[:])
                    iota = expert_m8[:].unsqueeze(1).broadcast_to([P, GR, E])

                    def over_e(ap):
                        return ap.unsqueeze(2).broadcast_to([P, GR, E])

                    for g in range(NG):
                        tg = tiles(g)
                        dve.wait_ge(s_sq, g + 1)
                        lk(TR(gms[:], gsq[:], X, ALU.add))
                        TS(gms[:], gms[:], 1.0 / D, EPS_RMS, ALU.mult, ALU.add).then_inc(s_ms, 1)
                        dve.wait_ge(s_rr, g + 1)
                        lk(TT(xs_rows[:, tg, 1, 0:D], x_res[:, tg, :], per_token(grms[:]), ALU.mult))
                        w = n2w[:].unsqueeze(1).broadcast_to([P, GR, D])
                        TT(xs_rows[:, tg, 0, 0:D], xs_rows[:, tg, 1, 0:D], w, ALU.mult).then_inc(s_xn, 1)
                        dve.wait_ge(s_xn, g + 1)
                        nc.vector.tensor_copy(xs_rows[:, tg, 1, 0:D], xs_rows[:, tg, 0, 0:D])
                        dve.wait_ge(s_lg, g + 1)
                        lk(TT(lg[:], bank[1][:, 0:GR * E].rearrange("p (t e) -> p t e", e=E),
                              rb[:].unsqueeze(1).broadcast_to([P, GR, E]), ALU.add))
                        for c, src in ((0, lg), (1, lg2)):
                            lk(TR(top[:, c, :], src[:], X, ALU.max))
                            lk(TT(hit[:], src[:], over_e(top[:, c, :]), ALU.is_equal))
                            lk(TT(hit[:], hit[:], iota, ALU.mult))
                            lk(TR(pick[:, c, :], hit[:], X, ALU.min))
                            lk(TT(chosen[:, c], iota, over_e(pick[:, c, :]), ALU.is_equal))
                            if c == 0:
                                lk(nc.vector.scalar_tensor_tensor(out=lg2[:], in0=chosen[:, 0], scalar=-3.0e38, in1=lg[:],
                                                                  op0=ALU.mult, op1=ALU.add))
                        TT(gap[:], top[:, 1, :], top[:, 0, :], ALU.subtract).then_inc(s_gp, 1)
                        lk(TT(both[:, tg, :], chosen[:, 0], chosen[:, 1], ALU.add))
                        for i in range(GR):
                            t = g * GR + i
                            last = TT(so_far[:, t + 1, :], so_far[:, t, :], both[:, t, :], ALU.add)
                            if i < GR - 1:
                                lk(last)
                        last.then_inc(s_ch, 1)
                        dve.wait_ge(s_ge, g + 1)
                        lk(TS(share[:, 0, tg], gap[:], 1.0, None, ALU.add))
                        lk(nc.vector.reciprocal(share[:, 0, tg], share[:, 0, tg]))
                        TT(share[:, 1, tg], gap[:], share[:, 0, tg], ALU.mult)
                        dve.wait_ge(s_ps, g + 1)
                        lk(TT(pos[:], bank[2][:, 0:GR * E].rearrange("p (t e) -> p t e", e=E),
                              expert_row[:].unsqueeze(1).broadcast_to([P, GR, E]), ALU.add))
                        lk(TT(pos2[:], chosen[:], pos[:].unsqueeze(1).broadcast_to([P, 2, GR, E]), ALU.mult))
                        lk(TR(slot[:], pos2[:], X, ALU.add))
                        nc.vector.tensor_copy(slot_ids[:, g], slot[:]).then_inc(s_sl, 1)

                    dve.wait_ge(s_cn, 1)
                    lk(nc.vector.tensor_copy(cnt[:], bank[3][:, 0:E]))
                    TT(padf[:], cnt[:], expert_row[:], ALU.add)
                    lk(TT(over[:], cnt[:].unsqueeze(2).broadcast_to([P, E, T]), blk128[:].unsqueeze(1).broadcast_to([P, E, T]),
                          ALU.is_gt))
                    nc.vector.tensor_copy(pad_tab[:], padf[:])
                    lk(TR(nblk[:], over[:], X, ALU.add))
                    lk(TT(trip[:], tri[:], nblk[:].unsqueeze(1).broadcast_to([P, E, E]), ALU.mult))
                    lk(TR(ends[:], trip[:], X, ALU.add))
                    lk(TT(past[:], blk_id[:].unsqueeze(2).broadcast_to([P, NBLK, E]),
                          ends[:].unsqueeze(1).broadcast_to([P, NBLK, E]), ALU.is_ge))
                    TR(eb[:], past[:], X, ALU.add)
                    lk(TT(past2[:], past[:], nblk[:].unsqueeze(1).broadcast_to([P, NBLK, E]), ALU.mult))
                    lk(TR(sbk[:], past2[:], X, ALU.add))
                    TS(inside[:], eb[:], float(E), None, ALU.is_lt)
                    TS(expf[:], eb[:], float(E - 1), None, ALU.min)
                    lk(TT(sbk[:], blk_id[:], sbk[:], ALU.subtract))
                    lk(TT(sbk[:], sbk[:], inside[:], ALU.mult))
                    lk(TS(sbk[:], sbk[:], float(P), None, ALU.mult))
                    lk(nc.vector.scalar_tensor_tensor(out=rowf[:], in0=eb[:], scalar=float(REGION), in1=sbk[:],
                                                      op0=ALU.mult, op1=ALU.add))
                    nc.vector.tensor_copy(exp_tab[:], expf[:])
                    nc.vector.tensor_copy(row_tab[:], rowf[:]).then_inc(s_tab, 1)

        route()

        xb = [sb(f"xb{i}", [P, XW]) for i in range(2)]
        xbT = [sb(f"xbT{i}", [P, P]) for i in range(2)]
        act1 = [xT[:, i * F:(i + 1) * F] for i in range(2)]
        gated = [xT[:, (2 + i) * F:(3 + i) * F] for i in range(2)]
        gT = [probs[:].rearrange("p h s -> p (h s)")[:, i * F:(i + 1) * F].rearrange("p (c q) -> p c q", c=FC) for i in range(2)]
        yb = [sb(f"yb{i}", [P, D]) for i in range(2)]
        dst_f = sb("dst_f", [P, NBLK])
        dst_id = [sb(f"dst_id{i}", [P, 1], u32) for i in range(2)]
        s_y = [sem(f"y_scattered{i}") for i in range(2)]

        def experts():
            s_ld = [sem(f"m_block_loaded{i}") for i in range(2)]
            s_xt = sem("m_xT_ready")
            s_xc = sem("m_xT_copied")
            s_h = sem("m_h_ready")
            s_a = sem("m_silu_ready")
            s_id = sem("m_row_ids_kept")
            s_g = sem("m_gated_ready")
            s_gt = sem("m_gT_ready")
            s_gc = sem("m_gT_copied")
            s_o = sem("m_out_ready")
            s_oc = sem("m_out_copied")

            def pe_xT(pe, b, u, i):
                pe.wait_ge(s_ld[u], 16 * i + 16)
                nc.tensor.transpose(bank[0][:, 0:P], xb[u][:, 0:D], ident[:]).then_inc(s_xt, 1)

            def pe_hidden(pe, b, u):
                pe.wait_ge(s_xc, b + 1)
                e = pe.value_load(exp_tab[0:1, bass.ds(b, 1)], min_val=0, max_val=E - 1)
                for bk, w, o in ((bank[1 + u], w1, 0), (bank[3 + u], w2, F)):
                    nc.tensor.matmul(bk[:], expert_sel[:, e, :], bias3[:, o:o + F], start=True, stop=False)
                    last = nc.tensor.matmul(bk[:], xbT[u][:], w[:, e, :], start=False, stop=True)
                last.then_inc(s_h, 1)

            def pe_gT(pe, b, u, first=False):
                pe.wait_ge(s_g, b + 1)
                if not first:
                    pe.wait_ge(s_gc, b)
                for c in range(FC):
                    last = nc.tensor.transpose(bank[5][:, c * P:(c + 1) * P], gated[u][:, c * P:(c + 1) * P], ident[:])
                last.then_inc(s_gt, 1)

            def pe_down(pe, b, u, first=False):
                pe.wait_ge(s_gc, b + 1)
                if not first:
                    pe.wait_ge(s_oc, b - 1)
                e = pe.value_load(exp_tab[0:1, bass.ds(b, 1)], min_val=0, max_val=E - 1)
                dst = bank[6 + u][:, 0:D]
                nc.tensor.matmul(dst, expert_sel[:, e, :], bias3[:, 2 * F:2 * F + D], start=True, stop=False)
                for c in range(FC):
                    last = nc.tensor.matmul(dst, gT[u][:, c, :], w3[:, e, c, :], start=False, stop=(c == FC - 1))
                last.then_inc(s_o, 1)

            def act_xT(act, b, u):
                act.wait_ge(s_xt, b + 1)
                nc.scalar.activation(xbT[u][:], bank[0][:, 0:P], ACT.Copy).then_inc(s_xc, 1)

            def act_silu(act, b, u):
                act.wait_ge(s_h, b + 1)
                nc.scalar.activation(act1[u], bank[1 + u][:], ACT.Silu).then_inc(s_a, 1)

            def act_gT(act, b, u):
                act.wait_ge(s_gt, b + 1)
                nc.scalar.activation(gT[u].rearrange("p c q -> p (c q)"), bank[5][:], ACT.Copy).then_inc(s_gc, 1)

            def dve_gate(dve, b, u, i):
                dve.wait_ge(s_ld[u], 16 * i + 16)
                nc.vector.tensor_copy(dst_f[:, bass.ds(b, 1)], xb[u][:, D:XW]).then_inc(s_id, 1)
                dve.wait_ge(s_a, b + 1)
                nc.vector.tensor_tensor(gated[u], act1[u], bank[3 + u][:], ALU.mult).then_inc(s_g, 1)

            def dve_out(dve, b, u, i, first=False):
                dve.wait_ge(s_o, b + 1)
                if not first:
                    dve.wait_ge(s_y[u], 16 * i)
                nc.vector.tensor_copy(yb[u][:], bank[6 + u][:, 0:D])
                nc.vector.tensor_copy(dst_id[u][:], dst_f[:, bass.ds(b, 1)]).then_inc(s_oc, 1)

            def pool_out(pool, b, u):
                pool.wait_ge(s_oc, b + 1)
                pool.nop(nofuse=True)
                pool.indirect_dma_start(out=y_rows[:, :], out_offset=bass.IndirectOffsetOnAxis(ap=dst_id[u][:, 0:1], axis=0),
                                        in_=yb[u][:], in_offset=None, bounds_check=2 * ROWS - 1,
                                        oob_is_err=False).then_inc(s_y[u], 16)

            def sp_load(sp, b, u, first=False):
                if not first:
                    sp.wait_ge(s_xt, b - 1)
                    sp.wait_ge(s_id, b - 1)
                r = sp.value_load(row_tab[0:1, bass.ds(b, 1)], min_val=0, max_val=E * REGION)
                sp.dma_start(xb[u][:], x_rows[bass.ds(r, P), :]).then_inc(s_ld[u], 16)

            N = NBLK

            def pe_step(pe, b, u, i, down="all", nxt=True, nxt2=True):
                if nxt:
                    pe_hidden(pe, b + 1, 1 - u)
                if nxt2:
                    pe_xT(pe, b + 2, u, i + 1)
                pe_gT(pe, b, u, first=(down is None))
                if down:
                    pe_down(pe, b - 1, 1 - u, first=(down == "first"))

            with nc.Block() as block:
                @block.sync
                def _(sp):
                    sp.wait_ge(s_xs, 16 * 2 * T)
                    sp.wait_ge(s_pad, 16 * (E + 1))
                    sp_load(sp, 0, 0, True)
                    sp_load(sp, 1, 1, True)
                    with sp.Fori(1, N // 2) as i:
                        for u in range(2):
                            sp_load(sp, 2 * i + u, u)
                    sp_load(sp, N - 1, (N - 1) % 2)

                @block.tensor
                def _(pe):
                    pe_xT(pe, 0, 0, 0)
                    pe.wait_ge(s_xc, 1)
                    pe_xT(pe, 1, 1, 0)
                    pe_hidden(pe, 0, 0)
                    pe_step(pe, 0, 0, 0, down=None)
                    pe_step(pe, 1, 1, 0, down="first")
                    pe_step(pe, 2, 0, 1, down="first")
                    with pe.Fori(1, N // 2 - 1) as i:
                        pe_step(pe, 2 * i + 1, 1, i)
                        pe_step(pe, 2 * i + 2, 0, i + 1)
                    pe_step(pe, N - 2, 1, N // 2 - 1, nxt2=False)
                    pe_step(pe, N - 1, 0, N // 2, nxt=False, nxt2=False)
                    pe_down(pe, N - 1, 0)

                @block.scalar
                def _(act):
                    act_xT(act, 0, 0)
                    act_xT(act, 1, 1)
                    act_silu(act, 0, 0)
                    with act.Fori(0, N // 2 - 1) as i:
                        for u in range(2):
                            act_silu(act, 2 * i + u + 1, 1 - u)
                            act_xT(act, 2 * i + u + 2, u)
                            act_gT(act, 2 * i + u, u)
                    act_silu(act, N - 2, 1)
                    act_xT(act, N - 1, 0)
                    act_gT(act, N - 3, 0)
                    act_silu(act, N - 1, 0)
                    act_gT(act, N - 2, 1)
                    act_gT(act, N - 1, 0)

                @block.vector
                def _(dve):
                    nc.vector.tensor_tensor(x_res[:], x_res[:], x_in[:], ALU.add)
                    dve_gate(dve, 0, 0, 0)
                    dve_gate(dve, 1, 1, 0)
                    dve_gate(dve, 2, 0, 1)
                    dve_out(dve, 0, 0, 0, True)
                    dve_gate(dve, 3, 1, 1)
                    dve_out(dve, 1, 1, 0, True)
                    with dve.Fori(2, N // 2) as i:
                        dve_gate(dve, 2 * i, 0, i)
                        dve_out(dve, 2 * i - 2, 0, i - 1)
                        dve_gate(dve, 2 * i + 1, 1, i)
                        dve_out(dve, 2 * i - 1, 1, i - 1)
                    dve_gate(dve, N - 1, 0, N // 2)
                    dve_out(dve, N - 3, 0, N // 2 - 1)
                    dve_out(dve, N - 2, 1, N // 2 - 1)
                    dve_out(dve, N - 1, 0, N // 2)

                @block.gpsimd
                def _(pool):
                    pool_out(pool, 0, 0)
                    with pool.Fori(0, N // 2) as i:
                        pool_out(pool, 2 * i + 1, 1)
                        pool_out(pool, 2 * i + 2, 0)

        experts()

        yy = freed[:, 0:T * 2 * D].rearrange("p (t c d) -> p t c d", t=T, c=2)
        res = x_in

        def combine():
            s_yl = [sem(f"c_y_loaded{g}") for g in range(NG)]
            s_gv = sem("c_var_ready")
            s_gr = sem("c_rstd_ready")
            s_f = sem("c_result_ready")
            with nc.Block() as block:
                @block.sync
                def _(sp):
                    sp.wait_ge(s_y[0], 16 * ((NBLK + 1) // 2))
                    sp.wait_ge(s_y[1], 16 * (NBLK // 2))
                    src = y_rows.rearrange("(t p c) d -> p t c d", p=P, c=2)
                    for g in range(NG):
                        tg = slice(g * GR, (g + 1) * GR)
                        sp.dma_start(yy[:, tg], src[:, tg]).then_inc(s_yl[g], 16)
                    dst = view(out)
                    for g in range(NG):
                        tg = slice(g * GR, (g + 1) * GR)
                        sp.wait_ge(s_f, g + 1)
                        sp.dma_start(dst[:, tg, :], res[:, tg, :]).then_inc(s_store, 16)
                    sp.wait_ge(s_store, 16 * NG)

                @block.gpsimd
                def _(pool):
                    for g in range(NG):
                        pool.wait_ge(s_gv, g + 1)
                        nc.gpsimd.tensor_tensor(grstd[:], gvar[:], neg_half[:, 0:GR], ALU.pow).then_inc(s_gr, 1)

                @block.vector
                def _(dve):
                    for g in range(NG):
                        tg = slice(g * GR, (g + 1) * GR)
                        dve.wait_ge(s_yl[g], 16)
                        for c in range(2):
                            for i in range(GR):
                                t = g * GR + i
                                last = nc.vector.scalar_tensor_tensor(out=x_res[:, t, :], in0=yy[:, t, c, :],
                                                                      scalar=share[:, c, t:t + 1], in1=x_res[:, t, :],
                                                                      op0=ALU.mult, op1=ALU.add)
                            link(dve, last, s_link)
                        for i in range(GR):
                            last = nc.vector.bn_stats(xst[:, i, :], x_res[:, g * GR + i, :])
                        link(dve, last, s_link)
                        dve_mean_var(dve, xst, gmean[:], gvar[:], gscr[:], EPS_LN, s_link).then_inc(s_gv, 1)
                        link(dve, nc.vector.tensor_tensor(res[:, tg, :], x_res[:, tg, :], per_token(gmean[:]), ALU.subtract), s_link)
                        dve.wait_ge(s_gr, g + 1)
                        nc.vector.tensor_tensor(res[:, tg, :], res[:, tg, :], per_token(grstd[:]), ALU.mult).then_inc(s_f, 1)

        combine()


HALF_TYPE = ("causal_q", "causal_k", "expert_sel")


def constants():
    import numpy as np
    p = np.arange(P)
    half = p // S
    c = {"ident": np.eye(P), "ident2": np.vstack([np.eye(S), np.eye(S)])}
    own = (half[:, None] == np.arange(2)[None, :]).astype(np.float64)
    c["vmask"] = np.stack([own] * H + [own * (DH * DH / (7.0 * 7.0 * DH))] * H, axis=1)
    c["slot_mask"] = np.broadcast_to((p[:, None] // SLOT == np.arange(J4)[None, :])[:, :, None], (P, J4, S))
    r = np.arange(S)
    later = (r[:, None] > (p % S)[None, :]).astype(np.float64)
    c["causal_q"] = np.vstack([later * -30512.0, later * -357.0])
    k = np.broadcast_to(np.eye(S)[:, None, :], (S, J4, S))
    c["causal_k"] = np.vstack([k * 32768.0, k * 512.0])
    assert 30512 * 32768 + 357 * 512 == 10 ** 9
    theta = np.float32(1.0) / np.float32(10000.0) ** (np.arange(D // 2, dtype=np.float32) / np.float32(D // 2))
    ang = (p % S).astype(np.float32)[:, None] * theta[None, :]
    c["rope"] = np.stack([np.cos(ang), np.sin(ang), -np.sin(ang)], axis=1)
    c["before"] = (p[:, None] < p[None, :]).astype(np.float64)
    c["expert_m8"] = np.broadcast_to(np.arange(E) - E, (P, E))
    c["expert_row"] = np.broadcast_to(np.arange(E) * REGION, (P, E))
    c["blk128"] = np.broadcast_to(np.arange(T) * P, (P, T))
    c["blk_id"] = np.broadcast_to(np.arange(NBLK), (P, NBLK))
    c["expert_sel"] = np.broadcast_to((np.arange(3 * E)[:, None] % E == np.arange(E)[None, :])[:, :, None], (3 * E, E, P))
    c["tri"] = np.broadcast_to(np.tril(np.ones((E, E))), (P, E, E))
    c["out_row"] = 2 * (np.arange(T)[None, :, None] * P + p[:, None, None]) + np.arange(2)[None, None, :]
    c["part_sel"] = (np.arange(3 * E)[:, None] // E == np.arange(3)[None, :])
    c["pad_rows"] = np.concatenate([np.zeros((P, D)), np.full((P, 1), 4.0 * ROWS)], axis=1)
    return {n: np.ascontiguousarray(np.asarray(v).astype(np.float16 if n in HALF_TYPE else np.float32)) for n, v in c.items()}


def kernel(**inputs):
    import numpy as np
    import concourse.bacc as bacc
    from concourse.bass_utils import run_bass_kernel_spmd as run

    nc = bacc.Bacc("TRN2", target_bir_lowering=False, num_devices=1)
    arrays = {n: np.ascontiguousarray(v) for n, v in inputs.items()}
    arrays["xT"] = np.ascontiguousarray(arrays["x"].reshape(ROWS, D).T)
    arrays["ctxT"] = np.ascontiguousarray(arrays.pop("ctx_512").reshape(ROWS, CD).T)
    for n in ("Wq", "Wk", "Wv", "Wo"):
        arrays["L0_attn_" + n] = np.ascontiguousarray(arrays["L0_attn_" + n].T)
    arrays.update(constants())
    a = {n: nc.dram_tensor(n + "_dram", v.shape, mybir.dt.from_np(v.dtype), kind="ExternalInput").ap()
         for n, v in arrays.items()}
    out = nc.dram_tensor("out_dram", (NB, S, D), fp32, kind="ExternalOutput").ap()
    program(nc, a, out)
    r = run(nc, [{n + "_dram": v for n, v in arrays.items()}], core_ids=[0])
    return r.results[0]["out_dram"]
```

```python
import concourse.bass as bass
from concourse import mybir
from contextlib import ExitStack

P = 128
NB, S, D = 32, 64, 128
T = NB * S // P
H, DH = 16, 8
G4, J4 = 4, 4
SLOT = P // J4
PAIRS = H // 2
VW = DH + 1
GR = 4
NG = T // GR
CD = 64
E, F, FC = 8, 512, 4
ROWS = NB * S
REGION = ROWS + P
NBLK = (2 * ROWS + E * (P - 1)) // P
XW = D + 1
PIECES = P // E
BW = (2 * F + D) // PIECES
EPS_LN, EPS_RMS = 1e-5, 1e-6

fp32, bf16, f16 = mybir.dt.float32, mybir.dt.bfloat16, mybir.dt.float16
i32, u32 = mybir.dt.int32, mybir.dt.uint32
ALU = mybir.AluOpType
ACT = mybir.ActivationFunctionType
X = mybir.AxisListType.X


def program(nc, a, out):
    ctx = ExitStack()
    with ctx:
        def sb(name, shape, dt=fp32):
            return ctx.enter_context(nc.sbuf_tensor(name, shape, dt))

        def sem(name):
            return ctx.enter_context(nc.semaphore(name))

        bank = [ctx.enter_context(nc.psum_tensor(f"bank{i}", [P, 512], fp32)) for i in range(8)]
        x_rows = nc.dram_tensor("x_rows", [(E + 1) * REGION, XW], fp32, kind="Internal").ap()
        y_rows = nc.dram_tensor("y_rows", [2 * ROWS, D], fp32, kind="Internal").ap()

        x_in = sb("x_in", [P, T, D])
        x_res = sb("x_res", [P, T, D])
        xT = sb("xT", [P, T * P])
        xT_tile = sb("xT_tile", [P, 2, 2, 2, S])
        r_tile = sb("r_tile", [P, D])
        stats_tile = sb("stats_tile", [P, 6])
        stats = sb("stats", [P, T, 6])
        wqk = [sb(f"wqk{k}", [P, 2, D]) for k in range(2)]
        wv = [sb(f"wv{k}", [P, D]) for k in range(2)]
        wo = [sb(f"wo{k}", [P, D]) for k in range(2)]
        wkv_g = sb("wkv_g", [P, 2, 32])
        wmean = sb("wmean", [P, 32])
        xwq = sb("xwq", [P, D])
        xwk = sb("xwk", [CD, D])
        xwv = sb("xwv", [CD, D])
        xbq = sb("xbq", [P, 1])
        xbk = sb("xbk", [P, 1])
        xbv = sb("xbv", [P, D])
        w1 = sb("w1", [P, E, F])
        w2 = sb("w2", [P, E, F])
        w3 = sb("w3", [P, E, FC, D])
        rw = sb("rw", [P, E])
        rb = sb("rb", [P, E])
        n1w = sb("n1w", [P, D])
        n2w = sb("n2w", [P, D])
        bias = sb("bias", [P, BW])
        bias_rest = sb("bias_rest", [P, BW])
        bias_part = sb("bias_part", [P, 3, BW], bf16)
        bias3 = sb("bias3", [3 * E, 2 * F + D], bf16)
        ident = sb("ident", [P, P])
        vmask = sb("vmask", [P, 2 * H, 2])
        slot_mask = sb("slot_mask", [P, J4, S])
        causal_q = sb("causal_q", [P, P], f16)
        causal_k = sb("causal_k", [P, J4, S], f16)
        rope = sb("rope", [P, 3, D // 2])
        rope_e = sb("rope_e", [P, 2, D // 2])
        rope_o = sb("rope_o", [P, 2, D // 2])
        before = sb("before", [P, P])
        ones = sb("ones", [P, P])
        expert_m8 = sb("expert_m8", [P, E])
        expert_row = sb("expert_row", [P, E])
        blk128 = sb("blk128", [P, T])
        blk_id = sb("blk_id", [P, NBLK])
        expert_sel = sb("expert_sel", [3 * E, E, P], f16)
        neg_half = sb("neg_half", [P, T])
        pad_rows = sb("pad_rows", [P, XW])
        tri = sb("tri", [P, E, E])
        out_row = sb("out_row", [P, T, 2])
        q_nat = sb("q_nat", [P, 2, H, SLOT])
        squares = sb("squares", [P, 2, D])
        var = sb("var", [P, 2 * H])
        qT = sb("qT", [P, 2, G4, P])
        kT = sb("kT", [P, 2, G4, S])
        k_diag = sb("k_diag", [P, 2, G4, J4, S])
        v_diag = sb("v_diag", [P, T, PAIRS, 2, 2, VW])
        row_max = sb("row_max", [P, 2, 8])
        probs = sb("probs", [P, H, S])
        probsT = sb("probsT", [P, PAIRS, P])
        inv_sum = sb("inv_sum", [P, H])
        o_nat = sb("o_nat", [P, H, DH])
        oT = sb("oT", [P, P])

        ctxT = sb("ctxT", [CD, T * P])
        s_ctx = sem("ctx_loaded")
        s_x = sem("x_loaded"); s_const = sem("const_loaded"); s_aw = sem("attn_weights_loaded")
        s_xw = sem("xattn_weights_loaded"); s_mw = sem("moe_weights_loaded")
        s_prep = sem("zeros_set"); s_wprep = sem("weights_prepared"); s_link = sem("dve_link")
        s_plink = sem("pool_link")
        s_bi = sem("biases_loaded"); s_bp = sem("bias_parts_ready"); s_b3 = sem("bias_rows_ready")
        s_store = sem("stored")

        def view(ap):
            return ap.rearrange("(t b) s d -> (b s) t d", b=2)

        links = {s_plink: 1}

        def link(eng, ins, sm):
            links[sm] = links.get(sm, 0) + 1
            ins.then_inc(sm, 1)
            eng.wait_ge(sm, links[sm])

        CONSTS = [(ident, "ident"), (vmask, "vmask"), (slot_mask, "slot_mask"), (causal_q, "causal_q"),
                  (causal_k, "causal_k"), (rope, "rope"), (before, "before"), (expert_m8, "expert_m8"),
                  (expert_row, "expert_row"), (blk128, "blk128"), (blk_id, "blk_id"), (expert_sel, "expert_sel"),
                  (pad_rows, "pad_rows"), (tri, "tri"), (out_row, "out_row")]
        ATTN_W = [(wqk[0][:, 0, :], a["L0_attn_Wq"]), (wqk[0][:, 1, :], a["L0_attn_Wk"]), (wv[0][:], a["L0_attn_Wv"]),
                  (wo[0][:], a["L0_attn_Wo"]), (wqk[1][:, 0, :], a["L0_ffn_Wq"]), (wkv_g[:, 0, :], a["L0_ffn_Wk"]),
                  (wkv_g[:, 1, :], a["L0_ffn_Wv"]), (wo[1][:], a["L0_ffn_Wo"])]

        def row(name):
            return a[name].rearrange("(o d) -> o d", o=1)

        def col(name):
            return a[name].rearrange("(d o) -> d o", o=1)

        with nc.Block() as block:
            @block.sync
            def _(sp):
                for dst, src in ATTN_W:
                    sp.dma_start(dst, src).then_inc(s_aw, 16)
                sp.dma_start(xT[:], a["xT"]).then_inc(s_x, 16)
                sp.dma_start(x_in[:], view(a["x"])).then_inc(s_x, 16)
                sp.dma_start(ctxT[:], a["ctxT"]).then_inc(s_ctx, 16)
                for dst, src in [(xwq[:], a["L0_xattn_Wq"]), (xwk[:], a["L0_xattn_Wk"]), (xwv[:], a["L0_xattn_Wv"]),
                                 (xbq[:], col("L0_xattn_bq")), (xbk[:], col("L0_xattn_bk")),
                                 (xbv[:], row("L0_xattn_bv").broadcast_to([P, D])),
                                 (n1w[:], row("L0_ffn_norm1_w").broadcast_to([P, D])),
                                 (n2w[:], row("L0_ffn_norm2_w").broadcast_to([P, D])),
                                 (rb[:], row("L0_ffn_router_b").broadcast_to([P, E])),
                                 (rw[:], a["L0_ffn_router_w"])]:
                    sp.dma_start(dst, src).then_inc(s_xw, 16)
                sp.dma_start(w1[:], a["L0_ffn_W1"].rearrange("e d f -> d e f")).then_inc(s_mw, 16)
                sp.dma_start(w2[:], a["L0_ffn_W2"].rearrange("e d f -> d e f")).then_inc(s_mw, 16)
                sp.dma_start(w3[:], a["L0_ffn_W3"].rearrange("e (c p) d -> p e c d", p=P)).then_inc(s_mw, 16)
                for o, n in ((0, "b1"), (F // PIECES, "b2"), (2 * F // PIECES, "b3")):
                    src = a["L0_ffn_" + n].rearrange("e (c j) -> (e c) j", c=PIECES)
                    sp.dma_start(bias[:, o:o + src.shape[1]], src).then_inc(s_bi, 16)

            @block.scalar
            def _(act):
                for dst, name in CONSTS:
                    act.dma_start(dst[:], a[name]).then_inc(s_const, 16)

            @block.gpsimd
            def _(pool):
                nc.gpsimd.memset(v_diag[:], 0.0).then_inc(s_plink, 1)
                nc.gpsimd.memset(neg_half[:], -0.5)
                nc.gpsimd.memset(ones[:], 1.0).then_inc(s_prep, 1)

            @block.vector
            def _(dve):
                nc.vector.memset(q_nat[:], 0.0).then_inc(s_prep, 1)
                dve.wait_ge(s_aw, 16 * len(ATTN_W))
                w = wqk[0][:].rearrange("p a (h d) -> p (a h) d", d=DH)
                link(dve, nc.vector.tensor_reduce(wmean[:], w, X, ALU.add), s_link)
                link(dve, nc.vector.tensor_scalar(wmean[:], wmean[:], 1.0 / DH, None, ALU.mult), s_link)
                link(dve, nc.vector.tensor_tensor(w, w, wmean[:].unsqueeze(2).broadcast_to([P, 32, DH]), ALU.subtract), s_link)
                nc.vector.tensor_scalar(wqk[0][:, 1, :], wqk[0][:, 1, :], 1.0 / DH, None, ALU.mult)
                for dst, k, f in ((wqk[1][:, 1, :], 0, float(DH) ** -0.5), (wv[1][:], 1, 1.0)):
                    src = wkv_g[:, k, :].rearrange("p (g d) -> p g d", d=DH).unsqueeze(2).broadcast_to([P, G4, J4, DH])
                    last = nc.vector.tensor_scalar(dst.rearrange("p (g j d) -> p g j d", g=G4, j=J4), src, f, None, ALU.mult)
                last.then_inc(s_wprep, 1)
                dve.wait_ge(s_plink, 1)
                for h2 in range(2):
                    last = nc.vector.memset(v_diag[64 * h2:64 * h2 + 64, :, :, :, h2, DH:VW], 1.0)
                last.then_inc(s_prep, 1)

        def attention(k, x_src):
            nm = f"a{k}_"
            s_xt = sem(nm + "xT_tile_ready")
            s_proj = sem(nm + "proj_ready")
            s_nat = sem(nm + "slots_ready")
            s_var = sem(nm + "var_ready")
            s_bt = sem(nm + "qkT_ready")
            s_qT = sem(nm + "qT_copied")
            s_kT = sem(nm + "kT_copied")
            s_kd = sem(nm + "k_diag_ready")
            s_sc = sem(nm + "scores_ready")
            s_mx = sem(nm + "max_ready")
            s_sh = sem(nm + "scores_shifted")
            s_ex = sem(nm + "probs_ready")
            s_pt = sem(nm + "probsT_ready")
            s_ps = sem(nm + "probsT_copied")
            s_pv = sem(nm + "pv_ready")
            s_iv = sem(nm + "inv_sum_ready")
            s_on = sem(nm + "o_normalised")
            s_ot = sem(nm + "oT_ready")
            s_oc = sem(nm + "oT_copied")
            s_wo = sem(nm + "wo_ready")
            s_rs = sem(nm + "residual_ready")
            s_st = sem(nm + "stats_ready")
            s_vr = sem(nm + "var_summed")
            W = P // 2

            def pe_project(pe, t, buf):
                pe.wait_ge(s_xt, t + 1)
                cols = xT_tile[:, buf].rearrange("p b r s -> p (b r s)")
                nc.tensor.matmul(bank[0][:, 0:2 * D], cols[:, S:3 * S], wqk[k][:].rearrange("p a d -> p (a d)"),
                                 start=True, stop=True)
                for b in range(2):
                    last = nc.tensor.matmul(bank[0][:, (2 + b) * D:(3 + b) * D], cols[:, 2 * b * S:2 * (b + 1) * S], wv[k][:], start=True, stop=True)
                last.then_inc(s_proj, 1)

            def pe_transpose_qk(pe, t, first=False):
                pe.wait_ge(s_nat, t + 1)
                if not first:
                    pe.wait_ge(s_kT, t)
                if k == 0:
                    pe.wait_ge(s_var, t + 1)
                for g in range(G4):
                    nc.tensor.transpose(bank[2][:, g * P:(g + 1) * P],
                                        q_nat[:, 0, g * J4:(g + 1) * J4, :].rearrange("p j s -> p (j s)"), ident[:])
                for g in range(G4):
                    last = nc.tensor.transpose(bank[1][:, g * P:(g + 1) * P],
                                               q_nat[:, 1, g * J4:(g + 1) * J4, :].rearrange("p j s -> p (j s)"), ident[:])
                last.then_inc(s_bt, 1)

            def pe_scores(pe, t, u):
                pe.wait_ge(s_qT, t + 1)
                pe.wait_ge(s_kd, t + 1)
                for half in range(2):
                    for g2 in range(2):
                        g = 2 * half + g2
                        dst = bank[4 + half][:, g2 * 256:(g2 + 1) * 256]
                        if k == 1:
                            nc.tensor.matmul(dst, causal_q[:], causal_k[:].rearrange("p h s -> p (h s)"), start=True, stop=False)
                        last = nc.tensor.matmul(dst, qT[:, u, g, :], k_diag[:, u, g, :, :].rearrange("p j s -> p (j s)"),
                                                start=(k == 0), stop=True)
                    last.then_inc(s_sc, 1)

            def pe_transpose_probs(pe, t):
                for half in range(2):
                    pe.wait_ge(s_ex, 2 * t + half + 1)
                    for q in range(4):
                        pr = 4 * half + q
                        last = nc.tensor.transpose(bank[6 + half][:, q * P:(q + 1) * P],
                                                   probs[:, 2 * pr:2 * pr + 2, :].rearrange("p h s -> p (h s)"), ident[:])
                    last.then_inc(s_pt, 1)

            def pe_pv(pe, t, residual_done):
                pe.wait_ge(s_ps, 2 * t + 2)
                if residual_done:
                    pe.wait_ge(s_rs, t)
                for pr in range(PAIRS):
                    last = nc.tensor.matmul(bank[3][:, pr * 4 * VW:(pr + 1) * 4 * VW], probsT[:, pr, :],
                                            v_diag[:, t, pr, :, :, :].rearrange("p b h w -> p (b h w)"),
                                            start=True, stop=True)
                last.then_inc(s_pv, 1)

            def pe_transpose_o(pe, t, qT_count):
                pe.wait_ge(s_on, t + 1)
                pe.wait_ge(s_qT, qT_count)
                nc.tensor.transpose(bank[2][:, 0:P], o_nat[:].rearrange("p h d -> p (h d)"), ident[:]).then_inc(s_ot, 1)

            def pe_out(pe, t):
                pe.wait_ge(s_oc, t + 1)
                nc.tensor.matmul(bank[3][:, 0:D], oT[:], wo[k][:], start=True, stop=True).then_inc(s_wo, 1)

            def act_slots(act, t):
                act.wait_ge(s_proj, t + 1)
                for b in range(2):
                    nc.scalar.activation(
                        q_nat[b * W:(b + 1) * W, :, :, b * DH:(b + 1) * DH].rearrange("p a h d -> p (a h) d"),
                        bank[0][b * W:(b + 1) * W, 0:2 * D].rearrange("p (h d) -> p h d", d=DH), ACT.Copy)
                if k == 0:
                    nc.scalar.activation(squares[:].rearrange("p a d -> p (a d)"), bank[0][:, 0:2 * D], ACT.Square)
                for h2 in range(2):
                    src = bank[0][h2 * W:(h2 + 1) * W, 2 * D:4 * D].rearrange("p (b q h d) -> p b q h d", b=2, q=PAIRS, h=2)
                    last = nc.scalar.activation(
                        v_diag[h2 * W:(h2 + 1) * W, t, :, :, h2, 0:DH].rearrange("p q b d -> p b q d"),
                        src[:, :, :, h2, :], ACT.Copy)
                last.then_inc(s_nat, 1)

            def act_qT(act, t, u):
                act.wait_ge(s_bt, t + 1)
                nc.scalar.activation(qT[:, u].rearrange("p g q -> p (g q)"), bank[2][:], ACT.Copy).then_inc(s_qT, 1)

            def act_exp(act, t, half):
                act.wait_ge(s_sh, 2 * t + half + 1)
                p = probs[:, 8 * half:8 * half + 8, :].rearrange("p h s -> p (h s)")
                nc.scalar.activation(p, p, ACT.Exp).then_inc(s_ex, 1)

            def act_probsT(act, t, half):
                act.wait_ge(s_pt, 2 * t + half + 1)
                nc.scalar.activation(probsT[:, 4 * half:4 * half + 4, :].rearrange("p h s -> p (h s)"), bank[6 + half][:],
                                     ACT.Copy).then_inc(s_ps, 1)

            def act_oT(act, t):
                act.wait_ge(s_ot, t + 1)
                nc.scalar.activation(oT[:], bank[2][:, 0:P], ACT.Copy).then_inc(s_oc, 1)

            def dve_softmax(dve, t):
                for half in range(2):
                    dve.wait_ge(s_sc, 2 * t + half + 1)
                    sc = bank[4 + half][:].rearrange("p (h s) -> p h s", s=S)
                    nc.vector.tensor_reduce(row_max[:, half, :], sc, X, ALU.max).then_inc(s_mx, 1)
                    dve.wait_ge(s_mx, 2 * t + half + 1)
                    nc.vector.tensor_tensor(probs[:, 8 * half:8 * half + 8, :], sc,
                                            row_max[:, half, :].unsqueeze(2).broadcast_to([P, 8, S]),
                                            ALU.subtract).then_inc(s_sh, 1)

            def dve_kT(dve, t, u):
                dve.wait_ge(s_bt, t + 1)
                nc.vector.tensor_reduce(kT[:, u], bank[1][:].rearrange("p (g b s) -> p g s b", g=G4, b=2), X,
                                        ALU.add).then_inc(s_kT, 1)

            def dve_var(dve, t):
                if k == 1:
                    return
                dve.wait_ge(s_nat, t + 1)
                nc.vector.tensor_reduce(var[:], squares[:].rearrange("p a (h d) -> p (a h) d", d=DH), X,
                                        ALU.add).then_inc(s_vr, 1)
                dve.wait_ge(s_vr, t + 1)
                nc.vector.tensor_tensor(q_nat[:, :, :, 2 * DH:2 * DH + 2].rearrange("p a h b -> p (a h) b"),
                                        var[:].unsqueeze(2).broadcast_to([P, 2 * H, 2]), vmask[:],
                                        ALU.mult).then_inc(s_var, 1)

            def dve_normalise(dve, t):
                dve.wait_ge(s_pv, t + 1)
                o = bank[3][:, 0:PAIRS * 4 * VW].rearrange("p (q b h w) -> p q b h w", b=2, h=2, w=VW)
                for b in range(2):
                    r = slice(b * W, (b + 1) * W)
                    last = nc.vector.reciprocal(inv_sum[r, :].rearrange("p (q h) -> p q h", h=2), o[r, :, b, :, DH])
                last.then_inc(s_iv, 1)
                dve.wait_ge(s_iv, t + 1)
                for b in range(2):
                    r = slice(b * W, (b + 1) * W)
                    last = nc.vector.tensor_tensor(
                        o_nat[r].rearrange("p (q h) d -> p q h d", h=2), o[r, :, b, :, 0:DH],
                        inv_sum[r, :].rearrange("p (q h) -> p q h", h=2).unsqueeze(3).broadcast_to([W, PAIRS, 2, DH]),
                        ALU.mult)
                last.then_inc(s_on, 1)

            def dve_residual(dve, t):
                dve.wait_ge(s_wo, t + 1)
                nc.vector.tensor_tensor(r_tile[:], bank[3][:, 0:D], x_src[:, t, :], ALU.add).then_inc(s_rs, 1)
                dve.wait_ge(s_rs, t + 1)
                nc.vector.tensor_copy(x_res[:, t, :], r_tile[:])
                nc.vector.bn_stats(stats_tile[:], r_tile[:]).then_inc(s_st, 1)
                dve.wait_ge(s_st, t + 1)
                nc.vector.tensor_copy(stats[:, t, :], stats_tile[:])

            def pool_xT(pool, t, buf, need):
                if need is not None:
                    pool.wait_ge(s_proj, need)
                    pool.nop(nofuse=True)
                src = xT[:, bass.ds(t * P, P)].rearrange("p (b s) -> p b s", b=2).unsqueeze(2).broadcast_to([P, 2, 2, S])
                nc.gpsimd.tensor_copy(xT_tile[:, buf], src).then_inc(s_xt, 1)

            def pool_diag(pool, t, u):
                pool.wait_ge(s_kT, t + 1)
                pool.nop(nofuse=True)
                src = kT[:, u].unsqueeze(2).broadcast_to([P, G4, J4, S])
                own = slot_mask[:].unsqueeze(1).broadcast_to([P, G4, J4, S])
                last = nc.gpsimd.tensor_tensor(k_diag[:, u], src, own, ALU.mult)
                last.then_inc(s_kd, 1)

            def pe_step(pe, n, u, prev=True, nxt2=True, nxt3=True):
                pe_scores(pe, n, u)
                if prev:
                    pe_pv(pe, n - 1, prev != "first")
                if nxt2:
                    pe_transpose_qk(pe, n + 2)
                if nxt3:
                    pe_project(pe, n + 3, 1 - u)
                if prev:
                    pe_transpose_o(pe, n - 1, n + 3 if nxt2 else T)
                pe_transpose_probs(pe, n)
                if prev:
                    pe_out(pe, n - 1)

            def act_step(act, n, u, prev=True, nxt2=True, nxt3=True):
                act_exp(act, n, 0)
                if nxt2:
                    act_qT(act, n + 2, u)
                act_exp(act, n, 1)
                if nxt3:
                    act_slots(act, n + 3)
                if prev:
                    act_oT(act, n - 1)
                act_probsT(act, n, 0)
                act_probsT(act, n, 1)

            def dve_step(dve, n, u, prev=True, nxt2=True, nxt3=True):
                dve_softmax(dve, n)
                if prev:
                    dve_normalise(dve, n - 1)
                if nxt2:
                    dve_kT(dve, n + 2, u)
                if nxt3:
                    dve_var(dve, n + 3)
                if prev:
                    dve_residual(dve, n - 1)

            def steps(eng, step):
                step(eng, 0, 0, prev=False)
                step(eng, 1, 1, prev="first")
                with eng.Fori(1, T // 2 - 2) as i:
                    for u in range(2):
                        step(eng, 2 * i + u, u)
                step(eng, T - 4, 0)
                step(eng, T - 3, 1, nxt3=False)
                step(eng, T - 2, 0, nxt2=False, nxt3=False)
                step(eng, T - 1, 1, nxt2=False, nxt3=False)

            with nc.Block() as block:
                @block.tensor
                def _(pe):
                    if k == 0:
                        pe.wait_ge(s_const, 16 * len(CONSTS))
                        pe.wait_ge(s_wprep, 1)
                        pe.wait_ge(s_prep, 3)
                    pe_project(pe, 0, 0)
                    pe_transpose_qk(pe, 0, True)
                    pe_project(pe, 1, 1)
                    pe.wait_ge(s_qT, 1)
                    pe_transpose_qk(pe, 1)
                    pe_project(pe, 2, 0)
                    pe.wait_ge(s_qT, 2)
                    steps(pe, pe_step)
                    pe_pv(pe, T - 1, True)
                    pe_transpose_o(pe, T - 1, T)
                    pe_out(pe, T - 1)

                @block.scalar
                def _(act):
                    if k == 0:
                        act.wait_ge(s_prep, 3)
                    act_slots(act, 0)
                    act_qT(act, 0, 0)
                    act_slots(act, 1)
                    act_qT(act, 1, 1)
                    act_slots(act, 2)
                    steps(act, act_step)
                    act_oT(act, T - 1)

                @block.vector
                def _(dve):
                    if k == 0:
                        dve.wait_ge(s_const, 16 * len(CONSTS))
                        dve.wait_ge(s_x, 32)
                    dve_var(dve, 0)
                    dve_kT(dve, 0, 0)
                    dve_var(dve, 1)
                    dve_kT(dve, 1, 1)
                    dve_var(dve, 2)
                    steps(dve, dve_step)
                    dve_normalise(dve, T - 1)
                    dve_residual(dve, T - 1)

                @block.gpsimd
                def _(pool):
                    if k == 0:
                        pool.wait_ge(s_x, 32)
                        pool.wait_ge(s_const, 16 * len(CONSTS))
                        pool.wait_ge(s_prep, 3)
                    pool_xT(pool, 0, 0, None)
                    pool_xT(pool, 1, 1, None)
                    pool_xT(pool, 2, 0, 1)
                    pool_diag(pool, 0, 0)
                    pool_xT(pool, 3, 1, 2)
                    with pool.Fori(0, T // 2 - 2) as i:
                        for u in range(2):
                            pool_diag(pool, 2 * i + u + 1, 1 - u)
                            pool_xT(pool, 2 * i + u + 4, u, 2 * i + u + 3)
                    for t in range(T - 3, T):
                        pool_diag(pool, t, t % 2)

        attention(0, x_in)


        def dve_mean_var(dve, st, mean, var_eps, scr, eps, sm):
            nc.vector.tensor_tensor(mean, st[:, :, 1], st[:, :, 4], ALU.add)
            nc.vector.tensor_tensor(scr, st[:, :, 1], st[:, :, 4], ALU.subtract)
            link(dve, nc.vector.tensor_tensor(var_eps, st[:, :, 2], st[:, :, 5], ALU.add), sm)
            nc.vector.tensor_scalar(mean, mean, 0.5, None, ALU.mult)
            nc.vector.tensor_scalar(var_eps, var_eps, 1.0 / D, eps, ALU.mult, ALU.add)
            link(dve, nc.vector.scalar_tensor_tensor(out=scr, in0=scr, scalar=0.25, in1=scr, op0=ALU.mult, op1=ALU.mult), sm)
            return nc.vector.tensor_tensor(var_eps, var_eps, scr, ALU.add)

        def per_token(ap, width=D):
            return ap.unsqueeze(2).broadcast_to([P, ap.shape[1], width])

        xaT = [sb(f"xaT{i}", [P, GR * P]) for i in range(2)]
        xq = [sb(f"xq{i}", [P, GR, P]) for i in range(2)]
        xk = [sb(f"xk{i}", [P, GR, P]) for i in range(2)]
        xv = sb("xv", [P, T, D])
        xp = [sb(f"xp{i}", [P, GR, P]) for i in range(2)]
        xpT = sb("xpT", [P, GR, P])
        xmax = sb("xmax", [P, GR])
        xsum = [sb(f"xsum{i}", [P, GR]) for i in range(2)]
        mean = sb("mean", [P, T]); rstd = sb("rstd", [P, T]); vscr = sb("vscr", [P, T])
        mean2 = sb("mean2", [P, T]); var2 = sb("var2", [P, T]); rstd2 = sb("rstd2", [P, T])
        ms2 = sb("ms2", [P, T]); rms2 = sb("rms2", [P, T])
        rope_a = sb("rope_a", [P, GR, 2, D // 2])
        rope_b = sb("rope_b", [P, GR, 2, D // 2])
        xr = sb("xr", [P, GR, D])

        def cross_attention():
            s_va = sem("x_var_ready")
            s_rd = sem("x_rstd_ready")
            s_z = sem("x_zeros_set")
            s_rp = sem("x_rope_tables")
            s_xn = sem("x_normed")
            s_ht = sem("x_xT_ready")
            s_hc = sem("x_xT_copied")
            s_kv = sem("x_kv_ready")
            s_q = sem("x_q_ready")
            s_qc = sem("x_qk_copied")
            s_v = sem("x_v_copied")
            s_s = sem("x_scores_ready")
            s_sh = sem("x_scores_shifted")
            s_e = sem("x_probs_ready")
            s_t = sem("x_probsT_ready")
            s_tc = sem("x_probsT_copied")
            s_p = sem("x_pv_ready")
            s_x2 = sem("x_residual_ready")
            s_gv = sem("x_var2_ready")
            s_gr = sem("x_rstd2_ready")
            s_ms = sem("x_ms2_ready")
            s_rr = sem("x_rms2_ready")
            s_x3 = sem("x_x3_ready")
            s_ro = sem("x_rope_odd")
            s_xr = sem("x_xr_ready")
            s_rt = sem("x_xrT_ready")
            s_rc = sem("x_xrT_copied")
            order = [(part, k - lag) for k in range(NG + 3) for part, lag in (("H", 0), ("S", 1), ("V", 2), ("R", 3))
                     if 0 <= k - lag < NG]

            def tiles(g):
                return slice(g * GR, (g + 1) * GR)

            def halves():
                return [slice(S * h, S * h + S) for h in range(2)]

            with nc.Block() as block:
                @block.tensor
                def _(pe):
                    pe.wait_ge(s_ctx, 16)
                    pe.wait_ge(s_xw, 160)
                    for part, g in order:
                        b = g % 2
                        if part == "H":
                            cg = slice(g * GR * P, (g + 1) * GR * P)
                            if g:
                                pe.wait_ge(s_qc, g)
                                pe.wait_ge(s_v, g)
                            nc.tensor.matmul(bank[2][:], xwk[:], ctxT[:, cg], start=True, stop=True)
                            for i in range(GR):
                                t = g * GR + i
                                last = nc.tensor.matmul(bank[3][:, i * P:(i + 1) * P], ctxT[:, t * P:(t + 1) * P], xwv[:],
                                                        start=True, stop=True)
                            last.then_inc(s_kv, 1)
                            pe.wait_ge(s_xn, g + 1)
                            for i in range(GR):
                                last = nc.tensor.transpose(bank[0][:, i * P:(i + 1) * P], x_res[:, g * GR + i, :], ident[:])
                            last.then_inc(s_ht, 1)
                            pe.wait_ge(s_hc, g + 1)
                            nc.tensor.matmul(bank[1][:], xwq[:], xaT[b][:], start=True, stop=True).then_inc(s_q, 1)
                        if part == "S":
                            pe.wait_ge(s_qc, g + 1)
                            if g:
                                pe.wait_ge(s_sh, g)
                            for i in range(GR):
                                last = nc.tensor.matmul(bank[4][:, i * P:(i + 1) * P], xq[b][:, i, :], xk[b][:, i, :],
                                                        start=True, stop=True)
                            last.then_inc(s_s, 1)
                        if part == "V":
                            pe.wait_ge(s_e, g + 1)
                            if g:
                                pe.wait_ge(s_tc, g)
                            for i in range(GR):
                                last = nc.tensor.transpose(bank[5][:, i * P:(i + 1) * P], xp[b][:, i, :], ident[:])
                            last.then_inc(s_t, 1)
                            pe.wait_ge(s_tc, g + 1)
                            pe.wait_ge(s_v, g + 1)
                            if g:
                                pe.wait_ge(s_x2, g)
                            for i in range(GR):
                                last = nc.tensor.matmul(bank[6][:, i * P:(i + 1) * P], xpT[:, i, :], xv[:, g * GR + i, :],
                                                        start=True, stop=True)
                            last.then_inc(s_p, 1)
                        if part == "R":
                            pe.wait_ge(s_xr, g + 1)
                            if g:
                                pe.wait_ge(s_rc, g)
                            for i in range(GR):
                                last = nc.tensor.transpose(bank[7][:, i * P:(i + 1) * P], xr[:, i, :], ident[:])
                            last.then_inc(s_rt, 1)

                @block.scalar
                def _(act):
                    act.wait_ge(s_z, 1)
                    for part, g in order:
                        b = g % 2
                        if part == "H":
                            act.wait_ge(s_kv, g + 1)
                            nc.scalar.activation(xk[b][:].rearrange("p i q -> p (i q)"), bank[2][:], ACT.Identity, bias=xbk[:, 0:1])
                            act.wait_ge(s_ht, g + 1)
                            nc.scalar.activation(xaT[b][:], bank[0][:], ACT.Copy).then_inc(s_hc, 1)
                            act.wait_ge(s_q, g + 1)
                            nc.scalar.activation(xq[b][:].rearrange("p i q -> p (i q)"), bank[1][:], ACT.Identity,
                                                 bias=xbq[:, 0:1]).then_inc(s_qc, 1)
                        if part == "S":
                            act.wait_ge(s_sh, g + 1)
                            for r in halves():
                                last = nc.scalar.activation(xp[b][r, :, r], xp[b][r, :, r], ACT.Exp)
                            last.then_inc(s_e, 1)
                        if part == "V":
                            act.wait_ge(s_t, g + 1)
                            nc.scalar.activation(xpT[:].rearrange("p i q -> p (i q)"), bank[5][:], ACT.Copy).then_inc(s_tc, 1)
                        if part == "R":
                            act.wait_ge(s_rt, g + 1)
                            nc.scalar.activation(xT[:, g * GR * P:(g + 1) * GR * P], bank[7][:], ACT.Copy).then_inc(s_rc, 1)

                @block.vector
                def _(dve):
                    nc.vector.memset(q_nat[:, :, :, 2 * DH:2 * DH + 2], 0.0)
                    dve_mean_var(dve, stats, mean[:], rstd[:], vscr[:], EPS_LN, s_link).then_inc(s_va, 1)
                    dve.wait_ge(s_rd, 1)
                    for part, g in order:
                        b = g % 2
                        tg = tiles(g)
                        if part == "H":
                            for t in range(g * GR, (g + 1) * GR):
                                last = nc.vector.tensor_scalar(x_res[:, t, :], x_res[:, t, :], mean[:, t:t + 1], rstd[:, t:t + 1],
                                                               ALU.subtract, ALU.mult)
                            last.then_inc(s_xn, 1)
                            dve.wait_ge(s_kv, g + 1)
                            nc.vector.tensor_tensor(xv[:, tg, :], bank[3][:].rearrange("p (i d) -> p i d", i=GR),
                                                    xbv[:].unsqueeze(1).broadcast_to([P, GR, D]), ALU.add).then_inc(s_v, 1)
                        if part == "S":
                            dve.wait_ge(s_s, g + 1)
                            s4 = bank[4][:].rearrange("p (i k) -> p i k", i=GR)
                            for r in halves():
                                last = nc.vector.tensor_reduce(xmax[r, :], s4[r, :, r], X, ALU.max)
                            link(dve, last, s_link)
                            for r in halves():
                                last = nc.vector.tensor_tensor(xp[b][r, :, r], s4[r, :, r],
                                                               xmax[r, :].unsqueeze(2).broadcast_to([S, GR, S]), ALU.subtract)
                            last.then_inc(s_sh, 1)
                        if part == "V":
                            dve.wait_ge(s_e, g + 1)
                            link(dve, nc.vector.tensor_reduce(xsum[b][:], xp[b][:], X, ALU.add), s_link)
                            link(dve, nc.vector.reciprocal(xsum[b][:], xsum[b][:]), s_link)
                            dve.wait_ge(s_p, g + 1)
                            for i in range(GR):
                                last = nc.vector.scalar_tensor_tensor(
                                    out=x_res[:, g * GR + i, :], in0=bank[6][:, i * P:(i + 1) * P], scalar=xsum[b][:, i:i + 1],
                                    in1=x_res[:, g * GR + i, :], op0=ALU.mult, op1=ALU.add)
                            last.then_inc(s_x2, 1)
                            dve.wait_ge(s_x2, g + 1)
                            for i in range(GR):
                                last = nc.vector.bn_stats(stats[:, g * GR + i, :], x_res[:, g * GR + i, :])
                            link(dve, last, s_link)
                            dve_mean_var(dve, stats[:, tg, :], mean2[:, tg], var2[:, tg], vscr[:, tg], EPS_LN,
                                         s_link).then_inc(s_gv, 1)
                        if part == "R":
                            dve.wait_ge(s_gr, g + 1)
                            for t in range(g * GR, (g + 1) * GR):
                                last = nc.vector.tensor_scalar(x_in[:, t, :], x_res[:, t, :], mean2[:, t:t + 1], rstd2[:, t:t + 1],
                                                               ALU.subtract, ALU.mult)
                            last.then_inc(s_x3, 1)
                            link(dve, nc.vector.tensor_scalar(ms2[:, tg], var2[:, tg], EPS_LN, None, ALU.subtract), s_link)
                            link(dve, nc.vector.tensor_tensor(ms2[:, tg], ms2[:, tg], rstd2[:, tg], ALU.mult), s_link)
                            link(dve, nc.vector.tensor_tensor(ms2[:, tg], ms2[:, tg], rstd2[:, tg], ALU.mult), s_link)
                            nc.vector.tensor_scalar(ms2[:, tg], ms2[:, tg], EPS_RMS, None, ALU.add).then_inc(s_ms, 1)
                            even = x_in[:, tg, :].rearrange("p i (d e) -> p i e d", e=2)[:, :, 0, :]
                            dve.wait_ge(s_x3, g + 1)
                            link(dve, nc.vector.tensor_tensor(rope_a[:], even.unsqueeze(2).broadcast_to([P, GR, 2, D // 2]),
                                                              rope_e[:].unsqueeze(1).broadcast_to([P, GR, 2, D // 2]),
                                                              ALU.mult), s_link)
                            dve.wait_ge(s_ro, g + 1)
                            if g:
                                dve.wait_ge(s_rt, g)
                            link(dve, nc.vector.tensor_tensor(xr[:], rope_a[:].rearrange("p i c d -> p i (c d)"),
                                                              rope_b[:].rearrange("p i c d -> p i (c d)"), ALU.add), s_link)
                            dve.wait_ge(s_rr, g + 1)
                            for i in range(GR):
                                t = g * GR + i
                                last = nc.vector.tensor_scalar(xr[:, i, :], xr[:, i, :], rms2[:, t:t + 1], None, ALU.mult)
                            last.then_inc(s_xr, 1)

                @block.gpsimd
                def _(pool):
                    pool.wait_ge(s_va, 1)
                    nc.gpsimd.tensor_tensor(rstd[:], rstd[:], neg_half[:], ALU.pow).then_inc(s_rd, 1)
                    for b in range(2):
                        last = nc.gpsimd.memset(xp[b][:], 0.0)
                    last.then_inc(s_z, 1)
                    w_eo = n1w[:].rearrange("p (d e) -> p e d", e=2)
                    pool.wait_ge(s_xw, 160)
                    nc.gpsimd.tensor_tensor(rope_e[:], rope[:, 0:2, :], w_eo[:, 0, :].unsqueeze(1).broadcast_to([P, 2, D // 2]), ALU.mult)
                    nc.gpsimd.tensor_tensor(rope_o[:, 1, :], rope[:, 0, :], w_eo[:, 1, :], ALU.mult)
                    nc.gpsimd.tensor_tensor(rope_o[:, 0, :], rope[:, 2, :], w_eo[:, 1, :], ALU.mult).then_inc(s_rp, 1)
                    pool.wait_ge(s_bi, 48)
                    link(pool, nc.gpsimd.tensor_copy(bias_part[:, 0, :], bias[:]), s_plink)
                    link(pool, nc.gpsimd.tensor_tensor(bias_rest[:], bias[:], bias_part[:, 0, :], ALU.subtract), s_plink)
                    link(pool, nc.gpsimd.tensor_copy(bias_part[:, 1, :], bias_rest[:]), s_plink)
                    link(pool, nc.gpsimd.tensor_tensor(bias_rest[:], bias_rest[:], bias_part[:, 1, :], ALU.subtract), s_plink)
                    nc.gpsimd.tensor_copy(bias_part[:, 2, :], bias_rest[:]).then_inc(s_bp, 1)
                    pool.wait_ge(s_rp, 1)
                    for k in range(NG + 1):
                        if k < NG:
                            tg = tiles(k)
                            pool.wait_ge(s_gv, k + 1)
                            nc.gpsimd.tensor_tensor(rstd2[:, tg], var2[:, tg], neg_half[:, tg], ALU.pow).then_inc(s_gr, 1)
                        if k >= 1:
                            g = k - 1
                            tg = tiles(g)
                            pool.wait_ge(s_x3, g + 1)
                            if g:
                                pool.wait_ge(s_xr, g)
                            odd = x_in[:, tg, :].rearrange("p i (d e) -> p i e d", e=2)[:, :, 1, :]
                            nc.gpsimd.tensor_tensor(rope_b[:], odd.unsqueeze(2).broadcast_to([P, GR, 2, D // 2]),
                                                    rope_o[:].unsqueeze(1).broadcast_to([P, GR, 2, D // 2]), ALU.mult).then_inc(s_ro, 1)
                            pool.wait_ge(s_ms, g + 1)
                            nc.gpsimd.tensor_tensor(rms2[:, tg], ms2[:, tg], neg_half[:, tg], ALU.pow).then_inc(s_rr, 1)

        cross_attention()
        attention(1, x_in)

        freed = v_diag[:].rearrange("p t q b h w -> p (t q b h w)")
        xs_rows = freed[:, 0:T * 2 * XW].rearrange("p (t c w) -> p t c w", t=T, c=2)
        xnT = sb("xnT", [P, GR * P])
        xst = sb("xst", [P, GR, 6])
        gmean = sb("gmean", [P, GR]); gvar = sb("gvar", [P, GR]); gscr = sb("gscr", [P, GR]); grstd = sb("grstd", [P, GR])
        gms = sb("gms", [P, GR]); grms = sb("grms", [P, GR])
        gsq = sb("gsq", [P, GR, D])
        lg = sb("lg", [P, GR, E]); lg2 = sb("lg2", [P, GR, E]); hit = sb("hit", [P, GR, E])
        top = sb("top", [P, 2, GR]); pick = sb("pick", [P, 2, GR])
        chosen = sb("chosen", [P, 2, GR, E])
        both = sb("both", [P, T, E])
        so_far = sb("so_far", [P, T + 1, E])
        pos = sb("pos", [P, GR, E]); pos2 = sb("pos2", [P, 2, GR, E]); slot = sb("slot", [P, 2, GR])
        slot_ids = sb("slot_ids", [P, NG, 2, GR], u32)
        gap = sb("gap", [P, GR]); share = sb("share", [P, 2, T])
        cnt = sb("cnt", [P, E]); over = sb("over", [P, E, T]); nblk = sb("nblk", [P, E]); 
        trip = sb("trip", [P, E, E]); ends = sb("ends", [P, E])
        past = sb("past", [P, NBLK, E]); past2 = sb("past2", [P, NBLK, E])
        eb = sb("eb", [P, NBLK]); sbk = sb("sbk", [P, NBLK]); inside = sb("inside", [P, NBLK]); rowf = sb("rowf", [P, NBLK])
        expf = sb("expf", [P, NBLK]); padf = sb("padf", [P, E])
        row_tab = sb("row_tab", [P, NBLK], i32); exp_tab = sb("exp_tab", [P, NBLK], i32); pad_tab = sb("pad_tab", [P, E], i32)
        s_xs = sem("rows_scattered")
        s_pad = sem("pads_written")
        s_tab = sem("block_tables_ready")

        def route():
            s_sq = sem("r_squares_ready")
            s_ms = sem("r_ms_ready")
            s_rr = sem("r_rms_ready")
            s_xn = sem("r_rows_ready")
            s_t = sem("r_xnT_ready")
            s_tc = sem("r_xnT_copied")
            s_lg = sem("r_logits_ready")
            s_ch = sem("r_choices_ready")
            s_gp = sem("r_gap_ready")
            s_ge = sem("r_gap_exp")
            s_ps = sem("r_positions_ready")
            s_sl = sem("r_slots_ready")
            s_cn = sem("r_counts_ready")

            def tiles(g):
                return slice(g * GR, (g + 1) * GR)

            with nc.Block() as block:
                @block.tensor
                def _(pe):
                    for g in range(NG):
                        pe.wait_ge(s_xn, g + 1)
                        for i in range(GR):
                            last = nc.tensor.transpose(bank[0][:, i * P:(i + 1) * P], xs_rows[:, g * GR + i, 0, 0:D], ident[:])
                        last.then_inc(s_t, 1)
                        pe.wait_ge(s_tc, g + 1)
                        for i in range(GR):
                            last = nc.tensor.matmul(bank[1][:, i * E:(i + 1) * E], xnT[:, i * P:(i + 1) * P], rw[:],
                                                    start=True, stop=True)
                        last.then_inc(s_lg, 1)
                        pe.wait_ge(s_ch, g + 1)
                        dst = bank[2][:, 0:GR * E]
                        nc.tensor.matmul(dst, before[:], both[:, tiles(g), :].rearrange("p t e -> p (t e)"), start=True, stop=False)
                        nc.tensor.matmul(dst, ones[:], so_far[:, tiles(g), :].rearrange("p t e -> p (t e)"), start=False,
                                         stop=True).then_inc(s_ps, 1)
                    nc.tensor.matmul(bank[3][:, 0:E], ones[:], so_far[:, T, :], start=True, stop=True).then_inc(s_cn, 1)

                @block.scalar
                def _(act):
                    for g in range(NG):
                        if g:
                            act.wait_ge(s_ms, g)
                        nc.scalar.activation(gsq[:], x_res[:, tiles(g), :], ACT.Square).then_inc(s_sq, 1)
                        act.wait_ge(s_t, g + 1)
                        nc.scalar.activation(xnT[:], bank[0][:], ACT.Copy).then_inc(s_tc, 1)
                        act.wait_ge(s_gp, g + 1)
                        nc.scalar.activation(gap[:], gap[:], ACT.Exp).then_inc(s_ge, 1)

                @block.gpsimd
                def _(pool):
                    for g in range(NG):
                        pool.wait_ge(s_ms, g + 1)
                        nc.gpsimd.tensor_tensor(grms[:], gms[:], neg_half[:, 0:GR], ALU.pow).then_inc(s_rr, 1)
                        pool.wait_ge(s_sl, g + 1)
                        for i in range(GR):
                            for c in range(2):
                                pool.indirect_dma_start(
                                    out=x_rows[:, :], out_offset=bass.IndirectOffsetOnAxis(ap=slot_ids[:, g, c, i:i + 1], axis=0),
                                    in_=xs_rows[:, g * GR + i, c, :], in_offset=None).then_inc(s_xs, 16)

                @block.sync
                def _(sp):
                    for r in range(3):
                        for o, w in ((0, F), (F, F), (2 * F, D)):
                            sp.dma_start(bias3[r * E:(r + 1) * E, o:o + w].rearrange("e (c j) -> e c j", c=PIECES),
                                         bias_part[:, r, o // PIECES:(o + w) // PIECES]).then_inc(s_b3, 16)
                    sp.dma_start(x_rows[E * REGION:E * REGION + P, :], pad_rows[:]).then_inc(s_pad, 16)
                    sp.wait_ge(s_tab, 1)
                    for e in range(E):
                        first = sp.value_load(pad_tab[0:1, e:e + 1], min_val=0, max_val=E * REGION - P)
                        sp.dma_start(x_rows[bass.ds(first, P), :], pad_rows[:]).then_inc(s_pad, 16)

                @block.vector
                def _(dve):
                    TT, TR, TS = nc.vector.tensor_tensor, nc.vector.tensor_reduce, nc.vector.tensor_scalar

                    def lk(ins):
                        link(dve, ins, s_link)

                    nc.vector.memset(so_far[:, 0, :], 0.0)
                    nc.vector.tensor_copy(xs_rows[:, :, :, D], out_row[:])
                    iota = expert_m8[:].unsqueeze(1).broadcast_to([P, GR, E])

                    def over_e(ap):
                        return ap.unsqueeze(2).broadcast_to([P, GR, E])

                    for g in range(NG):
                        tg = tiles(g)
                        dve.wait_ge(s_sq, g + 1)
                        lk(TR(gms[:], gsq[:], X, ALU.add))
                        TS(gms[:], gms[:], 1.0 / D, EPS_RMS, ALU.mult, ALU.add).then_inc(s_ms, 1)
                        dve.wait_ge(s_rr, g + 1)
                        lk(TT(xs_rows[:, tg, 1, 0:D], x_res[:, tg, :], per_token(grms[:]), ALU.mult))
                        w = n2w[:].unsqueeze(1).broadcast_to([P, GR, D])
                        TT(xs_rows[:, tg, 0, 0:D], xs_rows[:, tg, 1, 0:D], w, ALU.mult).then_inc(s_xn, 1)
                        dve.wait_ge(s_xn, g + 1)
                        nc.vector.tensor_copy(xs_rows[:, tg, 1, 0:D], xs_rows[:, tg, 0, 0:D])
                        dve.wait_ge(s_lg, g + 1)
                        lk(TT(lg[:], bank[1][:, 0:GR * E].rearrange("p (t e) -> p t e", e=E),
                              rb[:].unsqueeze(1).broadcast_to([P, GR, E]), ALU.add))
                        for c, src in ((0, lg), (1, lg2)):
                            lk(TR(top[:, c, :], src[:], X, ALU.max))
                            lk(TT(hit[:], src[:], over_e(top[:, c, :]), ALU.is_equal))
                            lk(TT(hit[:], hit[:], iota, ALU.mult))
                            lk(TR(pick[:, c, :], hit[:], X, ALU.min))
                            lk(TT(chosen[:, c], iota, over_e(pick[:, c, :]), ALU.is_equal))
                            if c == 0:
                                lk(nc.vector.scalar_tensor_tensor(out=lg2[:], in0=chosen[:, 0], scalar=-3.0e38, in1=lg[:],
                                                                  op0=ALU.mult, op1=ALU.add))
                        TT(gap[:], top[:, 1, :], top[:, 0, :], ALU.subtract).then_inc(s_gp, 1)
                        lk(TT(both[:, tg, :], chosen[:, 0], chosen[:, 1], ALU.add))
                        for i in range(GR):
                            t = g * GR + i
                            last = TT(so_far[:, t + 1, :], so_far[:, t, :], both[:, t, :], ALU.add)
                            if i < GR - 1:
                                lk(last)
                        last.then_inc(s_ch, 1)
                        dve.wait_ge(s_ge, g + 1)
                        lk(TS(share[:, 0, tg], gap[:], 1.0, None, ALU.add))
                        lk(nc.vector.reciprocal(share[:, 0, tg], share[:, 0, tg]))
                        TT(share[:, 1, tg], gap[:], share[:, 0, tg], ALU.mult)
                        dve.wait_ge(s_ps, g + 1)
                        lk(TT(pos[:], bank[2][:, 0:GR * E].rearrange("p (t e) -> p t e", e=E),
                              expert_row[:].unsqueeze(1).broadcast_to([P, GR, E]), ALU.add))
                        lk(TT(pos2[:], chosen[:], pos[:].unsqueeze(1).broadcast_to([P, 2, GR, E]), ALU.mult))
                        lk(TR(slot[:], pos2[:], X, ALU.add))
                        nc.vector.tensor_copy(slot_ids[:, g], slot[:]).then_inc(s_sl, 1)

                    dve.wait_ge(s_cn, 1)
                    lk(nc.vector.tensor_copy(cnt[:], bank[3][:, 0:E]))
                    TT(padf[:], cnt[:], expert_row[:], ALU.add)
                    lk(TT(over[:], cnt[:].unsqueeze(2).broadcast_to([P, E, T]), blk128[:].unsqueeze(1).broadcast_to([P, E, T]),
                          ALU.is_gt))
                    nc.vector.tensor_copy(pad_tab[:], padf[:])
                    lk(TR(nblk[:], over[:], X, ALU.add))
                    lk(TT(trip[:], tri[:], nblk[:].unsqueeze(1).broadcast_to([P, E, E]), ALU.mult))
                    lk(TR(ends[:], trip[:], X, ALU.add))
                    lk(TT(past[:], blk_id[:].unsqueeze(2).broadcast_to([P, NBLK, E]),
                          ends[:].unsqueeze(1).broadcast_to([P, NBLK, E]), ALU.is_ge))
                    TR(eb[:], past[:], X, ALU.add)
                    lk(TT(past2[:], past[:], nblk[:].unsqueeze(1).broadcast_to([P, NBLK, E]), ALU.mult))
                    lk(TR(sbk[:], past2[:], X, ALU.add))
                    TS(inside[:], eb[:], float(E), None, ALU.is_lt)
                    TS(expf[:], eb[:], float(E - 1), None, ALU.min)
                    lk(TT(sbk[:], blk_id[:], sbk[:], ALU.subtract))
                    lk(TT(sbk[:], sbk[:], inside[:], ALU.mult))
                    lk(TS(sbk[:], sbk[:], float(P), None, ALU.mult))
                    lk(nc.vector.scalar_tensor_tensor(out=rowf[:], in0=eb[:], scalar=float(REGION), in1=sbk[:],
                                                      op0=ALU.mult, op1=ALU.add))
                    nc.vector.tensor_copy(exp_tab[:], expf[:])
                    nc.vector.tensor_copy(row_tab[:], rowf[:]).then_inc(s_tab, 1)

        route()

        xb = [sb(f"xb{i}", [P, XW]) for i in range(2)]
        xbT = [sb(f"xbT{i}", [P, P]) for i in range(2)]
        act1 = [xT[:, i * F:(i + 1) * F] for i in range(2)]
        gated = [xT[:, (2 + i) * F:(3 + i) * F] for i in range(2)]
        gT = [probs[:].rearrange("p h s -> p (h s)")[:, i * F:(i + 1) * F].rearrange("p (c q) -> p c q", c=FC) for i in range(2)]
        yb = [sb(f"yb{i}", [P, D]) for i in range(2)]
        dst_f = sb("dst_f", [P, NBLK])
        dst_id = [sb(f"dst_id{i}", [P, 1], u32) for i in range(2)]
        s_y = [sem(f"y_scattered{i}") for i in range(2)]

        def experts():
            s_ld = [sem(f"m_block_loaded{i}") for i in range(2)]
            s_xt = sem("m_xT_ready")
            s_xc = sem("m_xT_copied")
            s_h = sem("m_h_ready")
            s_a = sem("m_silu_ready")
            s_id = sem("m_row_ids_kept")
            s_g = sem("m_gated_ready")
            s_gt = sem("m_gT_ready")
            s_gc = sem("m_gT_copied")
            s_o = sem("m_out_ready")
            s_oc = sem("m_out_copied")

            def pe_xT(pe, b, u, i):
                pe.wait_ge(s_ld[u], 16 * i + 16)
                nc.tensor.transpose(bank[0][:, 0:P], xb[u][:, 0:D], ident[:]).then_inc(s_xt, 1)

            def pe_hidden(pe, b, u):
                pe.wait_ge(s_xc, b + 1)
                e = pe.value_load(exp_tab[0:1, bass.ds(b, 1)], min_val=0, max_val=E - 1)
                for bk, w, o in ((bank[1 + u], w1, 0), (bank[3 + u], w2, F)):
                    nc.tensor.matmul(bk[:], expert_sel[:, e, :], bias3[:, o:o + F], start=True, stop=False)
                    last = nc.tensor.matmul(bk[:], xbT[u][:], w[:, e, :], start=False, stop=True)
                last.then_inc(s_h, 1)

            def pe_gT(pe, b, u, first=False):
                pe.wait_ge(s_g, b + 1)
                if not first:
                    pe.wait_ge(s_gc, b)
                for c in range(FC):
                    last = nc.tensor.transpose(bank[5][:, c * P:(c + 1) * P], gated[u][:, c * P:(c + 1) * P], ident[:])
                last.then_inc(s_gt, 1)

            def pe_down(pe, b, u, first=False):
                pe.wait_ge(s_gc, b + 1)
                if not first:
                    pe.wait_ge(s_oc, b - 1)
                e = pe.value_load(exp_tab[0:1, bass.ds(b, 1)], min_val=0, max_val=E - 1)
                dst = bank[6 + u][:, 0:D]
                nc.tensor.matmul(dst, expert_sel[:, e, :], bias3[:, 2 * F:2 * F + D], start=True, stop=False)
                for c in range(FC):
                    last = nc.tensor.matmul(dst, gT[u][:, c, :], w3[:, e, c, :], start=False, stop=(c == FC - 1))
                last.then_inc(s_o, 1)

            def act_xT(act, b, u):
                act.wait_ge(s_xt, b + 1)
                nc.scalar.activation(xbT[u][:], bank[0][:, 0:P], ACT.Copy).then_inc(s_xc, 1)

            def act_silu(act, b, u):
                act.wait_ge(s_h, b + 1)
                nc.scalar.activation(act1[u], bank[1 + u][:], ACT.Silu).then_inc(s_a, 1)

            def act_gT(act, b, u):
                act.wait_ge(s_gt, b + 1)
                nc.scalar.activation(gT[u].rearrange("p c q -> p (c q)"), bank[5][:], ACT.Copy).then_inc(s_gc, 1)

            def dve_gate(dve, b, u, i):
                dve.wait_ge(s_ld[u], 16 * i + 16)
                nc.vector.tensor_copy(dst_f[:, bass.ds(b, 1)], xb[u][:, D:XW]).then_inc(s_id, 1)
                dve.wait_ge(s_a, b + 1)
                nc.vector.tensor_tensor(gated[u], act1[u], bank[3 + u][:], ALU.mult).then_inc(s_g, 1)

            def dve_out(dve, b, u, i, first=False):
                dve.wait_ge(s_o, b + 1)
                if not first:
                    dve.wait_ge(s_y[u], 16 * i)
                nc.vector.tensor_copy(yb[u][:], bank[6 + u][:, 0:D])
                nc.vector.tensor_copy(dst_id[u][:], dst_f[:, bass.ds(b, 1)]).then_inc(s_oc, 1)

            def pool_out(pool, b, u):
                pool.wait_ge(s_oc, b + 1)
                pool.nop(nofuse=True)
                pool.indirect_dma_start(out=y_rows[:, :], out_offset=bass.IndirectOffsetOnAxis(ap=dst_id[u][:, 0:1], axis=0),
                                        in_=yb[u][:], in_offset=None, bounds_check=2 * ROWS - 1,
                                        oob_is_err=False).then_inc(s_y[u], 16)

            def sp_load(sp, b, u, first=False):
                if not first:
                    sp.wait_ge(s_xt, b - 1)
                    sp.wait_ge(s_id, b - 1)
                r = sp.value_load(row_tab[0:1, bass.ds(b, 1)], min_val=0, max_val=E * REGION)
                sp.dma_start(xb[u][:], x_rows[bass.ds(r, P), :]).then_inc(s_ld[u], 16)

            N = NBLK

            def pe_step(pe, b, u, i, down="all", nxt=True, nxt2=True):
                if nxt:
                    pe_hidden(pe, b + 1, 1 - u)
                if nxt2:
                    pe_xT(pe, b + 2, u, i + 1)
                pe_gT(pe, b, u, first=(down is None))
                if down:
                    pe_down(pe, b - 1, 1 - u, first=(down == "first"))

            with nc.Block() as block:
                @block.sync
                def _(sp):
                    sp.wait_ge(s_xs, 16 * 2 * T)
                    sp.wait_ge(s_pad, 16 * (E + 1))
                    sp_load(sp, 0, 0, True)
                    sp_load(sp, 1, 1, True)
                    with sp.Fori(1, N // 2) as i:
                        for u in range(2):
                            sp_load(sp, 2 * i + u, u)
                    sp_load(sp, N - 1, (N - 1) % 2)

                @block.tensor
                def _(pe):
                    pe.wait_ge(s_b3, 16 * 9)
                    pe.wait_ge(s_mw, 48)
                    pe_xT(pe, 0, 0, 0)
                    pe.wait_ge(s_xc, 1)
                    pe_xT(pe, 1, 1, 0)
                    pe_hidden(pe, 0, 0)
                    pe_step(pe, 0, 0, 0, down=None)
                    pe_step(pe, 1, 1, 0, down="first")
                    pe_step(pe, 2, 0, 1, down="first")
                    with pe.Fori(1, N // 2 - 1) as i:
                        pe_step(pe, 2 * i + 1, 1, i)
                        pe_step(pe, 2 * i + 2, 0, i + 1)
                    pe_step(pe, N - 2, 1, N // 2 - 1, nxt2=False)
                    pe_step(pe, N - 1, 0, N // 2, nxt=False, nxt2=False)
                    pe_down(pe, N - 1, 0)

                @block.scalar
                def _(act):
                    act_xT(act, 0, 0)
                    act_xT(act, 1, 1)
                    act_silu(act, 0, 0)
                    with act.Fori(0, N // 2 - 1) as i:
                        for u in range(2):
                            act_silu(act, 2 * i + u + 1, 1 - u)
                            act_xT(act, 2 * i + u + 2, u)
                            act_gT(act, 2 * i + u, u)
                    act_silu(act, N - 2, 1)
                    act_xT(act, N - 1, 0)
                    act_gT(act, N - 3, 0)
                    act_silu(act, N - 1, 0)
                    act_gT(act, N - 2, 1)
                    act_gT(act, N - 1, 0)

                @block.vector
                def _(dve):
                    nc.vector.tensor_tensor(x_res[:], x_res[:], x_in[:], ALU.add)
                    dve_gate(dve, 0, 0, 0)
                    dve_gate(dve, 1, 1, 0)
                    dve_gate(dve, 2, 0, 1)
                    dve_out(dve, 0, 0, 0, True)
                    dve_gate(dve, 3, 1, 1)
                    dve_out(dve, 1, 1, 0, True)
                    with dve.Fori(2, N // 2) as i:
                        dve_gate(dve, 2 * i, 0, i)
                        dve_out(dve, 2 * i - 2, 0, i - 1)
                        dve_gate(dve, 2 * i + 1, 1, i)
                        dve_out(dve, 2 * i - 1, 1, i - 1)
                    dve_gate(dve, N - 1, 0, N // 2)
                    dve_out(dve, N - 3, 0, N // 2 - 1)
                    dve_out(dve, N - 2, 1, N // 2 - 1)
                    dve_out(dve, N - 1, 0, N // 2)

                @block.gpsimd
                def _(pool):
                    pool_out(pool, 0, 0)
                    with pool.Fori(0, N // 2) as i:
                        pool_out(pool, 2 * i + 1, 1)
                        pool_out(pool, 2 * i + 2, 0)

        experts()

        yy = freed[:, 0:T * 2 * D].rearrange("p (t c d) -> p t c d", t=T, c=2)
        res = x_in

        def combine():
            s_yl = [sem(f"c_y_loaded{g}") for g in range(NG)]
            s_gv = sem("c_var_ready")
            s_gr = sem("c_rstd_ready")
            s_f = sem("c_result_ready")
            with nc.Block() as block:
                @block.sync
                def _(sp):
                    sp.wait_ge(s_y[0], 16 * ((NBLK + 1) // 2))
                    sp.wait_ge(s_y[1], 16 * (NBLK // 2))
                    src = y_rows.rearrange("(t p c) d -> p t c d", p=P, c=2)
                    for g in range(NG):
                        tg = slice(g * GR, (g + 1) * GR)
                        sp.dma_start(yy[:, tg], src[:, tg]).then_inc(s_yl[g], 16)
                    dst = view(out)
                    for g in range(NG):
                        tg = slice(g * GR, (g + 1) * GR)
                        sp.wait_ge(s_f, g + 1)
                        sp.dma_start(dst[:, tg, :], res[:, tg, :]).then_inc(s_store, 16)
                    sp.wait_ge(s_store, 16 * NG)

                @block.gpsimd
                def _(pool):
                    for g in range(NG):
                        pool.wait_ge(s_gv, g + 1)
                        nc.gpsimd.tensor_tensor(grstd[:], gvar[:], neg_half[:, 0:GR], ALU.pow).then_inc(s_gr, 1)

                @block.vector
                def _(dve):
                    for g in range(NG):
                        tg = slice(g * GR, (g + 1) * GR)
                        dve.wait_ge(s_yl[g], 16)
                        for c in range(2):
                            for i in range(GR):
                                t = g * GR + i
                                last = nc.vector.scalar_tensor_tensor(out=x_res[:, t, :], in0=yy[:, t, c, :],
                                                                      scalar=share[:, c, t:t + 1], in1=x_res[:, t, :],
                                                                      op0=ALU.mult, op1=ALU.add)
                            link(dve, last, s_link)
                        for i in range(GR):
                            last = nc.vector.bn_stats(xst[:, i, :], x_res[:, g * GR + i, :])
                        link(dve, last, s_link)
                        dve_mean_var(dve, xst, gmean[:], gvar[:], gscr[:], EPS_LN, s_link).then_inc(s_gv, 1)
                        link(dve, nc.vector.tensor_tensor(res[:, tg, :], x_res[:, tg, :], per_token(gmean[:]), ALU.subtract), s_link)
                        dve.wait_ge(s_gr, g + 1)
                        nc.vector.tensor_tensor(res[:, tg, :], res[:, tg, :], per_token(grstd[:]), ALU.mult).then_inc(s_f, 1)

        combine()


HALF_TYPE = ("causal_q", "causal_k", "expert_sel")


def constants():
    import numpy as np
    p = np.arange(P)
    half = p // S
    c = {"ident": np.eye(P)}
    own = (half[:, None] == np.arange(2)[None, :]).astype(np.float64)
    c["vmask"] = np.stack([own] * H + [own * (DH * DH / (7.0 * 7.0 * DH))] * H, axis=1)
    c["slot_mask"] = np.broadcast_to((p[:, None] // SLOT == np.arange(J4)[None, :])[:, :, None], (P, J4, S))
    r = np.arange(S)
    later = (r[:, None] > (p % S)[None, :]).astype(np.float64)
    c["causal_q"] = np.vstack([later * -30512.0, later * -357.0])
    k = np.broadcast_to(np.eye(S)[:, None, :], (S, J4, S))
    c["causal_k"] = np.vstack([k * 32768.0, k * 512.0])
    assert 30512 * 32768 + 357 * 512 == 10 ** 9
    theta = np.float32(1.0) / np.float32(10000.0) ** (np.arange(D // 2, dtype=np.float32) / np.float32(D // 2))
    ang = (p % S).astype(np.float32)[:, None] * theta[None, :]
    c["rope"] = np.stack([np.cos(ang), np.sin(ang), -np.sin(ang)], axis=1)
    c["before"] = (p[:, None] < p[None, :]).astype(np.float64)
    c["expert_m8"] = np.broadcast_to(np.arange(E) - E, (P, E))
    c["expert_row"] = np.broadcast_to(np.arange(E) * REGION, (P, E))
    c["blk128"] = np.broadcast_to(np.arange(T) * P, (P, T))
    c["blk_id"] = np.broadcast_to(np.arange(NBLK), (P, NBLK))
    c["expert_sel"] = np.broadcast_to((np.arange(3 * E)[:, None] % E == np.arange(E)[None, :])[:, :, None], (3 * E, E, P))
    c["tri"] = np.broadcast_to(np.tril(np.ones((E, E))), (P, E, E))
    c["out_row"] = 2 * (np.arange(T)[None, :, None] * P + p[:, None, None]) + np.arange(2)[None, None, :]
    c["pad_rows"] = np.concatenate([np.zeros((P, D)), np.full((P, 1), 4.0 * ROWS)], axis=1)
    return {n: np.ascontiguousarray(np.asarray(v).astype(np.float16 if n in HALF_TYPE else np.float32)) for n, v in c.items()}


def kernel(**inputs):
    import numpy as np
    import concourse.bacc as bacc
    from concourse.bass_utils import run_bass_kernel_spmd as run

    nc = bacc.Bacc("TRN2", target_bir_lowering=False, num_devices=1)
    arrays = {n: np.ascontiguousarray(v) for n, v in inputs.items()}
    arrays["xT"] = np.ascontiguousarray(arrays["x"].reshape(ROWS, D).T)
    arrays["ctxT"] = np.ascontiguousarray(arrays.pop("ctx_512").reshape(ROWS, CD).T)
    for n in ("Wq", "Wk", "Wv", "Wo"):
        arrays["L0_attn_" + n] = np.ascontiguousarray(arrays["L0_attn_" + n].T)
    arrays.update(constants())
    a = {n: nc.dram_tensor(n + "_dram", v.shape, mybir.dt.from_np(v.dtype), kind="ExternalInput").ap()
         for n, v in arrays.items()}
    out = nc.dram_tensor("out_dram", (NB, S, D), fp32, kind="ExternalOutput").ap()
    program(nc, a, out)
    r = run(nc, [{n + "_dram": v for n, v in arrays.items()}], core_ids=[0])
    return r.results[0]["out_dram"]
```

```python
import concourse.bass as bass
from concourse import mybir
from contextlib import ExitStack

P = 128
NB, S, D = 32, 64, 128
T = NB * S // P
H, DH = 16, 8
G4, J4 = 4, 4
SLOT = P // J4
PAIRS = H // 2
VW = DH + 1
GR = 4
NG = T // GR
CD = 64
E, F, FC = 8, 512, 4
ROWS = NB * S
REGION = ROWS + P
NBLK = (2 * ROWS + E * (P - 1)) // P
XW = D + 2
EPS_LN, EPS_RMS = 1e-5, 1e-6

fp32, bf16, f16 = mybir.dt.float32, mybir.dt.bfloat16, mybir.dt.float16
i32, u32 = mybir.dt.int32, mybir.dt.uint32
ALU = mybir.AluOpType
ACT = mybir.ActivationFunctionType
X = mybir.AxisListType.X


def program(nc, a, out):
    ctx = ExitStack()
    with ctx:
        def sb(name, shape, dt=fp32):
            return ctx.enter_context(nc.sbuf_tensor(name, shape, dt))

        def sem(name):
            return ctx.enter_context(nc.semaphore(name))

        bank = [ctx.enter_context(nc.psum_tensor(f"bank{i}", [P, 512], fp32)) for i in range(8)]
        x_rows = nc.dram_tensor("x_rows", [(E + 1) * REGION, XW], fp32, kind="Internal").ap()
        y_rows = nc.dram_tensor("y_rows", [2 * ROWS, D], fp32, kind="Internal").ap()

        x_in = sb("x_in", [P, T, D])
        x_res = sb("x_res", [P, T, D])
        xT = sb("xT", [P, T * P])
        xT_tile = sb("xT_tile", [P, 2, 2, 2, S])
        r_tile = sb("r_tile", [P, D])
        stats_tile = sb("stats_tile", [P, 6])
        stats = sb("stats", [P, T, 6])
        wqk = [sb(f"wqk{k}", [P, 2, D]) for k in range(2)]
        wv = [sb(f"wv{k}", [P, D]) for k in range(2)]
        wo = [sb(f"wo{k}", [P, D]) for k in range(2)]
        wkv_g = sb("wkv_g", [P, 2, 32])
        wmean = sb("wmean", [P, 32])
        xwq = sb("xwq", [P, D])
        xwk = sb("xwk", [CD, D])
        xwv = sb("xwv", [CD, D])
        xbq = sb("xbq", [P, 1])
        xbk = sb("xbk", [P, 1])
        xbv = sb("xbv", [P, D])
        w12 = sb("w12", [P, E, 2, F])
        w3 = sb("w3", [P, E, FC, D])
        rw = sb("rw", [P, E])
        rb = sb("rb", [P, E])
        n1w = sb("n1w", [P, D])
        n2w = sb("n2w", [P, D])
        bias12 = sb("bias12", [2 * E * FC, P])
        bias_col = sb("bias_col", [P, 2, E, FC])
        b3 = sb("b3", [E, D])
        b3_rest = sb("b3_rest", [E, D])
        b3_part = sb("b3_part", [E, 3, D], bf16)
        bias3 = sb("bias3", [3, E * D], bf16)
        ident = sb("ident", [P, P])
        vmask = sb("vmask", [P, 2 * H, 2])
        slot_mask = sb("slot_mask", [P, J4, S])
        causal_q = sb("causal_q", [P, P], f16)
        causal_k = sb("causal_k", [P, J4, S], f16)
        rope = sb("rope", [P, 3, D // 2])
        rope_e = sb("rope_e", [P, 2, D // 2])
        rope_o = sb("rope_o", [P, 2, D // 2])
        before = sb("before", [P, P])
        ones = sb("ones", [P, P])
        expert_m8 = sb("expert_m8", [P, E])
        expert_row = sb("expert_row", [P, E])
        blk128 = sb("blk128", [P, T])
        blk_id = sb("blk_id", [P, NBLK])
        ones3 = sb("ones3", [3, P], bf16)
        neg_half = sb("neg_half", [P, T])
        pad_rows = sb("pad_rows", [P, XW])
        tri = sb("tri", [P, E, E])
        out_row = sb("out_row", [P, T, 2])
        q_nat = sb("q_nat", [P, 2, H, SLOT])
        squares = sb("squares", [P, 2, D])
        var = sb("var", [P, 2 * H])
        qT = sb("qT", [P, 2, G4, P])
        kT = sb("kT", [P, 2, G4, S])
        k_diag = sb("k_diag", [P, 2, G4, J4, S])
        v_diag = sb("v_diag", [P, T, PAIRS, 2, 2, VW])
        row_max = sb("row_max", [P, 2, 8])
        probs = sb("probs", [P, H, S])
        probsT = sb("probsT", [P, PAIRS, P])
        inv_sum = sb("inv_sum", [P, H])
        o_nat = sb("o_nat", [P, H, DH])
        oT = sb("oT", [P, P])

        ctxT = sb("ctxT", [CD, T * P])
        s_aw = sem("wq_wk_loaded"); s_wv0 = sem("wv_loaded"); s_wo0 = sem("wo_loaded")
        s_const = sem("const_loaded"); s_later = sem("later_loaded")
        s_xT0 = sem("xT_first_group_loaded"); s_x = sem("x_loaded")
        s_prep = sem("zeros_set"); s_wprep = sem("weights_prepared"); s_link = sem("dve_link")
        s_plink = sem("pool_link")
        s_b3 = sem("bias_rows_ready")
        s_store = sem("stored")

        def view(ap):
            return ap.rearrange("(t b) s d -> (b s) t d", b=2)

        links = {s_plink: 1}

        def link(eng, ins, sm):
            links[sm] = links.get(sm, 0) + 1
            ins.then_inc(sm, 1)
            eng.wait_ge(sm, links[sm])

        CONSTS = [(ident, "ident"), (vmask, "vmask"), (slot_mask, "slot_mask")]
        LATER_CONSTS = [(rope, "rope"), (causal_q, "causal_q"), (causal_k, "causal_k"), (before, "before"),
                        (expert_m8, "expert_m8"), (expert_row, "expert_row"), (blk128, "blk128"), (blk_id, "blk_id"),
                        (pad_rows, "pad_rows"), (tri, "tri"), (out_row, "out_row")]

        def row(name):
            return a[name].rearrange("(o d) -> o d", o=1)

        def col(name):
            return a[name].rearrange("(d o) -> d o", o=1)

        def load_later(sp):
            sp.dma_start(wo[0][:], a["L0_attn_Wo"]).then_inc(s_wo0, 16)
            sp.dma_start(x_in[:], view(a["x"])).then_inc(s_x, 16)
            for dst, name in LATER_CONSTS:
                sp.dma_start(dst[:], a[name]).then_inc(s_later, 16)
            for dst, src in [(wqk[1][:, 0, :], a["L0_ffn_Wq"]), (wkv_g[:, 0, :], a["L0_ffn_Wk"]),
                             (wkv_g[:, 1, :], a["L0_ffn_Wv"]), (wo[1][:], a["L0_ffn_Wo"]), (ctxT[:], a["ctxT"]),
                             (xwq[:], a["L0_xattn_Wq"]), (xwk[:], a["L0_xattn_Wk"]), (xwv[:], a["L0_xattn_Wv"]),
                             (xbq[:], col("L0_xattn_bq")), (xbk[:], col("L0_xattn_bk")),
                             (xbv[:], row("L0_xattn_bv").broadcast_to([P, D])),
                             (n1w[:], row("L0_ffn_norm1_w").broadcast_to([P, D])),
                             (n2w[:], row("L0_ffn_norm2_w").broadcast_to([P, D])),
                             (rb[:], row("L0_ffn_router_b").broadcast_to([P, E])),
                             (rw[:], a["L0_ffn_router_w"]),
                             (b3[:], a["L0_ffn_b3"])]:
                sp.dma_start(dst, src).then_inc(s_later, 16)
            for o, n in ((0, "b1"), (E * FC, "b2")):
                sp.dma_start(bias12[o:o + E * FC, :], a["L0_ffn_" + n].rearrange("e (c j) -> (e c) j", c=FC)).then_inc(s_later, 16)
            for k in range(2):
                sp.dma_start(w12[:, :, k, :], a[f"L0_ffn_W{k + 1}"].rearrange("e d f -> d e f")).then_inc(s_later, 16)
            sp.dma_start(w3[:], a["L0_ffn_W3"].rearrange("e (c p) d -> p e c d", p=P)).then_inc(s_later, 16)
            sp.wait_ge(s_later, 16 * (len(LATER_CONSTS) + 16 + 2 + 3))

        with nc.Block() as block:
            @block.sync
            def _(sp):
                sp.dma_start(wqk[0][:, 0, :], a["L0_attn_Wq"]).then_inc(s_aw, 16)
                sp.dma_start(wqk[0][:, 1, :], a["L0_attn_Wk"]).then_inc(s_aw, 16)
                sp.dma_start(xT[:, 0:GR * P], a["xT"][:, 0:GR * P]).then_inc(s_xT0, 16)
                sp.dma_start(xT[:, GR * P:], a["xT"][:, GR * P:]).then_inc(s_x, 16)

            @block.scalar
            def _(act):
                act.dma_start(wv[0][:], a["L0_attn_Wv"]).then_inc(s_wv0, 16)
                for dst, name in CONSTS:
                    act.dma_start(dst[:], a[name]).then_inc(s_const, 16)

            @block.gpsimd
            def _(pool):
                nc.gpsimd.memset(v_diag[:], 0.0).then_inc(s_plink, 1)
                nc.gpsimd.memset(neg_half[:], -0.5)
                nc.gpsimd.memset(ones3[:], 1.0)
                nc.gpsimd.memset(ones[:], 1.0).then_inc(s_prep, 1)

            @block.vector
            def _(dve):
                nc.vector.memset(q_nat[:], 0.0).then_inc(s_prep, 1)
                dve.wait_ge(s_aw, 32)
                w = wqk[0][:].rearrange("p a (h d) -> p (a h) d", d=DH)
                link(dve, nc.vector.tensor_reduce(wmean[:], w, X, ALU.add), s_link)
                link(dve, nc.vector.tensor_scalar(wmean[:], wmean[:], 1.0 / DH, None, ALU.mult), s_link)
                link(dve, nc.vector.tensor_tensor(w, w, wmean[:].unsqueeze(2).broadcast_to([P, 32, DH]), ALU.subtract), s_link)
                nc.vector.tensor_scalar(wqk[0][:, 1, :], wqk[0][:, 1, :], 1.0 / DH, None, ALU.mult).then_inc(s_wprep, 1)
                dve.wait_ge(s_plink, 1)
                for h2 in range(2):
                    last = nc.vector.memset(v_diag[64 * h2:64 * h2 + 64, :, :, :, h2, DH:VW], 1.0)
                last.then_inc(s_prep, 1)

        def attention(k, x_src):
            nm = f"a{k}_"
            s_xt = sem(nm + "xT_tile_ready")
            s_proj = sem(nm + "proj_ready")
            s_qk = sem(nm + "squares_ready")
            s_nat = sem(nm + "slots_ready")
            s_var = sem(nm + "var_ready")
            s_bt = sem(nm + "qkT_ready")
            s_qT = sem(nm + "qT_copied")
            s_kT = sem(nm + "kT_copied")
            s_kd = sem(nm + "k_diag_ready")
            s_sc = sem(nm + "scores_ready")
            s_mx = sem(nm + "max_ready")
            s_sh = sem(nm + "scores_shifted")
            s_ex = sem(nm + "probs_ready")
            s_pt = sem(nm + "probsT_ready")
            s_ps = sem(nm + "probsT_copied")
            s_pv = sem(nm + "pv_ready")
            s_iv = sem(nm + "inv_sum_ready")
            s_on = sem(nm + "o_normalised")
            s_ot = sem(nm + "oT_ready")
            s_oc = sem(nm + "oT_copied")
            s_wo = sem(nm + "wo_ready")
            s_rs = sem(nm + "residual_ready")
            s_st = sem(nm + "stats_ready")
            s_vr = sem(nm + "var_summed")
            W = P // 2

            def pe_project(pe, t, buf):
                pe.wait_ge(s_xt, t + 1)
                cols = xT_tile[:, buf].rearrange("p b r s -> p (b r s)")
                nc.tensor.matmul(bank[0][:, 0:2 * D], cols[:, S:3 * S], wqk[k][:].rearrange("p a d -> p (a d)"),
                                 start=True, stop=True)
                for b in range(2):
                    last = nc.tensor.matmul(bank[0][:, (2 + b) * D:(3 + b) * D], cols[:, 2 * b * S:2 * (b + 1) * S], wv[k][:], start=True, stop=True)
                last.then_inc(s_proj, 1)

            def pe_transpose_qk(pe, t, first=False):
                pe.wait_ge(s_nat, t + 1)
                if k == 0:
                    pe.wait_ge(s_var, t + 1)
                for qk in range(2):
                    if qk and not first:
                        pe.wait_ge(s_kT, t)
                    for g in range(G4):
                        last = nc.tensor.transpose(bank[2 - qk][:, g * P:(g + 1) * P],
                                                   q_nat[:, qk, g * J4:(g + 1) * J4, :].rearrange("p j s -> p (j s)"), ident[:])
                    last.then_inc(s_bt, 1)

            def pe_scores(pe, t, u):
                pe.wait_ge(s_qT, t + 1)
                pe.wait_ge(s_kd, t + 1)
                for half in range(2):
                    for g2 in range(2):
                        g = 2 * half + g2
                        dst = bank[4 + half][:, g2 * 256:(g2 + 1) * 256]
                        if k == 1:
                            nc.tensor.matmul(dst, causal_q[:], causal_k[:].rearrange("p h s -> p (h s)"), start=True, stop=False)
                        last = nc.tensor.matmul(dst, qT[:, u, g, :], k_diag[:, u, g, :, :].rearrange("p j s -> p (j s)"),
                                                start=(k == 0), stop=True)
                    last.then_inc(s_sc, 1)

            def pe_transpose_probs(pe, t, pairs):
                half = pairs[0] // 4
                pe.wait_ge(s_ex, 2 * t + half + 1)
                for pr in pairs:
                    q = pr % 4
                    last = nc.tensor.transpose(bank[6 + half][:, q * P:(q + 1) * P],
                                               probs[:, 2 * pr:2 * pr + 2, :].rearrange("p h s -> p (h s)"), ident[:])
                if q == 3:
                    last.then_inc(s_pt, 1)

            def pe_pv(pe, t, residual_done):
                pe.wait_ge(s_ps, 2 * t + 2)
                if residual_done:
                    pe.wait_ge(s_rs, t)
                for pr in range(PAIRS):
                    last = nc.tensor.matmul(bank[3][:, pr * 4 * VW:(pr + 1) * 4 * VW], probsT[:, pr, :],
                                            v_diag[:, t, pr, :, :, :].rearrange("p b h w -> p (b h w)"),
                                            start=True, stop=True)
                last.then_inc(s_pv, 1)

            def pe_transpose_o(pe, t, qT_count):
                pe.wait_ge(s_on, t + 1)
                pe.wait_ge(s_qT, qT_count)
                nc.tensor.transpose(bank[2][:, 0:P], o_nat[:].rearrange("p h d -> p (h d)"), ident[:]).then_inc(s_ot, 1)

            def pe_out(pe, t):
                pe.wait_ge(s_oc, t + 1)
                nc.tensor.matmul(bank[3][:, 0:D], oT[:], wo[k][:], start=True, stop=True).then_inc(s_wo, 1)

            def act_slots(act, t):
                act.wait_ge(s_proj, t + 1)
                for b in range(2):
                    nc.scalar.activation(
                        q_nat[b * W:(b + 1) * W, :, :, b * DH:(b + 1) * DH].rearrange("p a h d -> p (a h) d"),
                        bank[0][b * W:(b + 1) * W, 0:2 * D].rearrange("p (h d) -> p h d", d=DH), ACT.Copy)

            def act_squares(act, t):
                if k == 0:
                    nc.scalar.activation(squares[:].rearrange("p a d -> p (a d)"), bank[0][:, 0:2 * D],
                                         ACT.Square).then_inc(s_qk, 1)

            def act_values(act, t):
                for h2 in range(2):
                    src = bank[0][h2 * W:(h2 + 1) * W, 2 * D:4 * D].rearrange("p (b q h d) -> p b q h d", b=2, q=PAIRS, h=2)
                    last = nc.scalar.activation(
                        v_diag[h2 * W:(h2 + 1) * W, t, :, :, h2, 0:DH].rearrange("p q b d -> p b q d"),
                        src[:, :, :, h2, :], ACT.Copy)
                last.then_inc(s_nat, 1)

            def act_qT(act, t, u):
                act.wait_ge(s_bt, 2 * t + 1)
                nc.scalar.activation(qT[:, u].rearrange("p g q -> p (g q)"), bank[2][:], ACT.Copy).then_inc(s_qT, 1)

            def act_exp(act, t, half):
                act.wait_ge(s_sh, 2 * t + half + 1)
                p = probs[:, 8 * half:8 * half + 8, :].rearrange("p h s -> p (h s)")
                nc.scalar.activation(p, p, ACT.Exp).then_inc(s_ex, 1)

            def act_probsT(act, t, half):
                act.wait_ge(s_pt, 2 * t + half + 1)
                nc.scalar.activation(probsT[:, 4 * half:4 * half + 4, :].rearrange("p h s -> p (h s)"), bank[6 + half][:],
                                     ACT.Copy).then_inc(s_ps, 1)

            def act_oT(act, t):
                act.wait_ge(s_ot, t + 1)
                nc.scalar.activation(oT[:], bank[2][:, 0:P], ACT.Copy).then_inc(s_oc, 1)

            def dve_softmax(dve, t, half):
                dve.wait_ge(s_sc, 2 * t + half + 1)
                sc = bank[4 + half][:].rearrange("p (h s) -> p h s", s=S)
                nc.vector.tensor_reduce(row_max[:, half, :], sc, X, ALU.max).then_inc(s_mx, 1)
                dve.wait_ge(s_mx, 2 * t + half + 1)
                nc.vector.tensor_tensor(probs[:, 8 * half:8 * half + 8, :], sc,
                                        row_max[:, half, :].unsqueeze(2).broadcast_to([P, 8, S]),
                                        ALU.subtract).then_inc(s_sh, 1)

            def dve_kT(dve, t, u):
                dve.wait_ge(s_bt, 2 * t + 2)
                nc.vector.tensor_reduce(kT[:, u], bank[1][:].rearrange("p (g b s) -> p g s b", g=G4, b=2), X,
                                        ALU.add).then_inc(s_kT, 1)

            def dve_var(dve, t):
                if k == 1:
                    return
                dve.wait_ge(s_qk, t + 1)
                nc.vector.tensor_reduce(var[:], squares[:].rearrange("p a (h d) -> p (a h) d", d=DH), X,
                                        ALU.add).then_inc(s_vr, 1)
                dve.wait_ge(s_vr, t + 1)
                nc.vector.tensor_tensor(q_nat[:, :, :, 2 * DH:2 * DH + 2].rearrange("p a h b -> p (a h) b"),
                                        var[:].unsqueeze(2).broadcast_to([P, 2 * H, 2]), vmask[:],
                                        ALU.mult).then_inc(s_var, 1)

            def dve_normalise(dve, t):
                dve.wait_ge(s_pv, t + 1)
                o = bank[3][:, 0:PAIRS * 4 * VW].rearrange("p (q b h w) -> p q b h w", b=2, h=2, w=VW)
                for b in range(2):
                    r = slice(b * W, (b + 1) * W)
                    last = nc.vector.reciprocal(inv_sum[r, :].rearrange("p (q h) -> p q h", h=2), o[r, :, b, :, DH])
                last.then_inc(s_iv, 1)
                dve.wait_ge(s_iv, t + 1)
                for b in range(2):
                    r = slice(b * W, (b + 1) * W)
                    last = nc.vector.tensor_tensor(
                        o_nat[r].rearrange("p (q h) d -> p q h d", h=2), o[r, :, b, :, 0:DH],
                        inv_sum[r, :].rearrange("p (q h) -> p q h", h=2).unsqueeze(3).broadcast_to([W, PAIRS, 2, DH]),
                        ALU.mult)
                last.then_inc(s_on, 1)

            def dve_residual(dve, t):
                dve.wait_ge(s_wo, t + 1)
                nc.vector.tensor_tensor(r_tile[:], bank[3][:, 0:D], x_src[:, t, :], ALU.add).then_inc(s_rs, 1)
                dve.wait_ge(s_rs, t + 1)
                nc.vector.tensor_copy(x_res[:, t, :], r_tile[:])
                nc.vector.bn_stats(stats_tile[:], r_tile[:]).then_inc(s_st, 1)
                dve.wait_ge(s_st, t + 1)
                nc.vector.tensor_copy(stats[:, t, :], stats_tile[:])

            def pool_xT(pool, t, buf, need):
                if need is not None:
                    pool.wait_ge(s_proj, need)
                    pool.nop(nofuse=True)
                src = xT[:, bass.ds(t * P, P)].rearrange("p (b s) -> p b s", b=2).unsqueeze(2).broadcast_to([P, 2, 2, S])
                nc.gpsimd.tensor_copy(xT_tile[:, buf], src).then_inc(s_xt, 1)

            def pool_diag(pool, t, u):
                pool.wait_ge(s_kT, t + 1)
                pool.nop(nofuse=True)
                src = kT[:, u].unsqueeze(2).broadcast_to([P, G4, J4, S])
                own = slot_mask[:].unsqueeze(1).broadcast_to([P, G4, J4, S])
                last = nc.gpsimd.tensor_tensor(k_diag[:, u], src, own, ALU.mult)
                last.then_inc(s_kd, 1)

            def pe_step(pe, n, u, prev=True, nxt2=True, nxt3=True):
                pe_scores(pe, n, u)
                if prev:
                    pe_pv(pe, n - 1, prev != "first")
                if nxt2:
                    pe_transpose_qk(pe, n + 2)
                if nxt3:
                    pe_project(pe, n + 3, 1 - u)
                pe_transpose_probs(pe, n, (0, 1))
                if prev:
                    pe_transpose_o(pe, n - 1, n + 3 if nxt2 else T)
                pe_transpose_probs(pe, n, (2, 3))
                pe_transpose_probs(pe, n, (4, 5, 6, 7))
                if prev:
                    pe_out(pe, n - 1)

            def act_step(act, n, u, prev=True, nxt2=True, nxt3=True):
                act_exp(act, n, 0)
                if nxt2:
                    act_qT(act, n + 2, u)
                act_exp(act, n, 1)
                if nxt3:
                    act_slots(act, n + 3)
                if prev:
                    act_oT(act, n - 1)
                if nxt3:
                    act_squares(act, n + 3)
                act_probsT(act, n, 0)
                act_probsT(act, n, 1)
                if nxt3:
                    act_values(act, n + 3)

            def dve_step(dve, n, u, prev=True, nxt2=True, nxt3=True):
                dve_softmax(dve, n, 0)
                dve_softmax(dve, n, 1)
                if prev:
                    dve_normalise(dve, n - 1)
                if nxt2:
                    dve_kT(dve, n + 2, u)
                if nxt3:
                    dve_var(dve, n + 3)
                if prev:
                    dve_residual(dve, n - 1)

            def steps(eng, step):
                step(eng, 0, 0, prev=False)
                step(eng, 1, 1, prev="first")
                with eng.Fori(1, T // 2 - 2) as i:
                    for u in range(2):
                        step(eng, 2 * i + u, u)
                step(eng, T - 4, 0)
                step(eng, T - 3, 1, nxt3=False)
                step(eng, T - 2, 0, nxt2=False, nxt3=False)
                step(eng, T - 1, 1, nxt2=False, nxt3=False)

            with nc.Block() as block:
                if k == 0:
                    @block.sync
                    def _(sp):
                        load_later(sp)

                @block.tensor
                def _(pe):
                    if k == 0:
                        pe.wait_ge(s_wprep, 1)
                        pe.wait_ge(s_prep, 3)
                        pe.wait_ge(s_wv0, 16)
                    pe_project(pe, 0, 0)
                    if k == 0:
                        pe.wait_ge(s_const, 16 * len(CONSTS))
                    pe_transpose_qk(pe, 0, True)
                    pe_project(pe, 1, 1)
                    pe.wait_ge(s_qT, 1)
                    pe_transpose_qk(pe, 1)
                    pe_project(pe, 2, 0)
                    pe.wait_ge(s_qT, 2)
                    if k == 0:
                        pe.wait_ge(s_wo0, 16)
                    steps(pe, pe_step)
                    pe_pv(pe, T - 1, True)
                    pe_transpose_o(pe, T - 1, T)
                    pe_out(pe, T - 1)

                @block.scalar
                def _(act):
                    if k == 0:
                        act.wait_ge(s_prep, 3)
                    for t in range(3):
                        act_slots(act, t)
                        act_squares(act, t)
                        act_values(act, t)
                        if t < 2:
                            act_qT(act, t, t)
                    steps(act, act_step)
                    act_oT(act, T - 1)

                @block.vector
                def _(dve):
                    if k == 0:
                        dve.wait_ge(s_const, 16 * len(CONSTS))
                    dve_var(dve, 0)
                    dve_kT(dve, 0, 0)
                    dve_var(dve, 1)
                    dve_kT(dve, 1, 1)
                    dve_var(dve, 2)
                    if k == 0:
                        dve.wait_ge(s_x, 32)
                    steps(dve, dve_step)
                    dve_normalise(dve, T - 1)
                    dve_residual(dve, T - 1)

                @block.gpsimd
                def _(pool):
                    if k == 0:
                        pool.wait_ge(s_xT0, 16)
                    pool_xT(pool, 0, 0, None)
                    pool_xT(pool, 1, 1, None)
                    pool_xT(pool, 2, 0, 1)
                    if k == 0:
                        pool.wait_ge(s_const, 16 * len(CONSTS))
                    pool_diag(pool, 0, 0)
                    pool_xT(pool, 3, 1, 2)
                    if k == 0:
                        pool.wait_ge(s_x, 32)
                    with pool.Fori(0, T // 2 - 2) as i:
                        for u in range(2):
                            pool_diag(pool, 2 * i + u + 1, 1 - u)
                            pool_xT(pool, 2 * i + u + 4, u, 2 * i + u + 3)
                    for t in range(T - 3, T):
                        pool_diag(pool, t, t % 2)

        attention(0, x_in)


        def dve_mean_var(dve, st, mean, var_eps, scr, eps, sm):
            nc.vector.tensor_tensor(mean, st[:, :, 1], st[:, :, 4], ALU.add)
            nc.vector.tensor_tensor(scr, st[:, :, 1], st[:, :, 4], ALU.subtract)
            link(dve, nc.vector.tensor_tensor(var_eps, st[:, :, 2], st[:, :, 5], ALU.add), sm)
            nc.vector.tensor_scalar(mean, mean, 0.5, None, ALU.mult)
            nc.vector.tensor_scalar(var_eps, var_eps, 1.0 / D, eps, ALU.mult, ALU.add)
            link(dve, nc.vector.scalar_tensor_tensor(out=scr, in0=scr, scalar=0.25, in1=scr, op0=ALU.mult, op1=ALU.mult), sm)
            return nc.vector.tensor_tensor(var_eps, var_eps, scr, ALU.add)

        shift2 = sb("shift2", [P, T])
        xaT = [sb(f"xaT{i}", [P, GR * P]) for i in range(2)]
        xq = [sb(f"xq{i}", [P, GR, P]) for i in range(2)]
        xk = [sb(f"xk{i}", [P, GR, P]) for i in range(2)]
        xv = sb("xv", [P, T, D])
        xp = [sb(f"xp{i}", [P, GR, P]) for i in range(2)]
        xpT = sb("xpT", [P, GR, P])
        xmax = sb("xmax", [P, GR])
        xsum = [sb(f"xsum{i}", [P, GR]) for i in range(2)]
        mean = sb("mean", [P, T]); rstd = sb("rstd", [P, T]); vscr = sb("vscr", [P, T])
        mean2 = sb("mean2", [P, T]); var2 = sb("var2", [P, T]); rstd2 = sb("rstd2", [P, T])
        ms2 = sb("ms2", [P, T]); rms2 = sb("rms2", [P, T])
        rope_a = sb("rope_a", [P, GR, 2, D // 2])
        rope_b = sb("rope_b", [P, GR, 2, D // 2])
        xr = sb("xr", [P, GR, D])

        def cross_attention():
            s_va = sem("x_var_ready")
            s_rd = sem("x_rstd_ready")
            s_z = sem("x_zeros_set")
            s_rp = sem("x_rope_tables")
            s_xn = sem("x_normed")
            s_ht = sem("x_xT_ready")
            s_hc = sem("x_xT_copied")
            s_kc = sem("x_keys_copied")
            s_kv = sem("x_kv_ready")
            s_q = sem("x_q_ready")
            s_qc = sem("x_qk_copied")
            s_v = sem("x_v_copied")
            s_s = sem("x_scores_ready")
            s_sh = sem("x_scores_shifted")
            s_e = sem("x_probs_ready")
            s_t = sem("x_probsT_ready")
            s_tc = sem("x_probsT_copied")
            s_p = sem("x_pv_ready")
            s_x2 = sem("x_residual_ready")
            s_gv = sem("x_var2_ready")
            s_gr = sem("x_rstd2_ready")
            s_rr = sem("x_rms2_ready")
            s_x3 = sem("x_x3_ready")
            s_ro = sem("x_rope_odd")
            s_xr = sem("x_xr_ready")
            s_rt = sem("x_xrT_ready")
            s_rc = sem("x_xrT_copied")
            def rounds(parts):
                for k in range(NG + 4):
                    for lag, part in parts:
                        if 0 <= k - lag < NG:
                            part(k - lag)

            def tiles(g):
                return slice(g * GR, (g + 1) * GR)

            def halves():
                return [slice(S * h, S * h + S) for h in range(2)]

            with nc.Block() as block:
                @block.tensor
                def _(pe):
                    def keys_values(g, first=False):
                        if g == 0 and not first:
                            return
                        if g:
                            pe.wait_ge(s_kc, g)
                            pe.wait_ge(s_v, g)
                        nc.tensor.matmul(bank[2][:], xwk[:], ctxT[:, g * GR * P:(g + 1) * GR * P], start=True, stop=True)
                        for i in range(GR):
                            t = g * GR + i
                            last = nc.tensor.matmul(bank[3][:, i * P:(i + 1) * P], ctxT[:, t * P:(t + 1) * P], xwv[:],
                                                    start=True, stop=True)
                        last.then_inc(s_kv, 1)

                    def transpose_x(g):
                        pe.wait_ge(s_xn, g + 1)
                        for i in range(GR):
                            last = nc.tensor.transpose(bank[0][:, i * P:(i + 1) * P], x_res[:, g * GR + i, :], ident[:])
                        last.then_inc(s_ht, 1)

                    def queries(g):
                        pe.wait_ge(s_hc, g + 1)
                        if g:
                            pe.wait_ge(s_qc, g)
                        nc.tensor.matmul(bank[1][:], xwq[:], xaT[g % 2][:], start=True, stop=True).then_inc(s_q, 1)

                    def scores(g):
                        pe.wait_ge(s_qc, g + 1)
                        pe.wait_ge(s_kc, g + 1)
                        if g:
                            pe.wait_ge(s_sh, g)
                        for i in range(GR):
                            last = nc.tensor.matmul(bank[4][:, i * P:(i + 1) * P], xq[g % 2][:, i, :], xk[g % 2][:, i, :],
                                                    start=True, stop=True)
                        last.then_inc(s_s, 1)

                    def transpose_probs(g):
                        pe.wait_ge(s_e, g + 1)
                        for i in range(GR):
                            last = nc.tensor.transpose(bank[5][:, i * P:(i + 1) * P], xp[g % 2][:, i, :], ident[:])
                        last.then_inc(s_t, 1)

                    def values(g):
                        pe.wait_ge(s_tc, g + 1)
                        pe.wait_ge(s_v, g + 1)
                        if g:
                            pe.wait_ge(s_x2, g)
                        for i in range(GR):
                            last = nc.tensor.matmul(bank[6][:, i * P:(i + 1) * P], xpT[:, i, :], xv[:, g * GR + i, :],
                                                    start=True, stop=True)
                        last.then_inc(s_p, 1)

                    def transpose_rotated(g):
                        pe.wait_ge(s_xr, g + 1)
                        if g:
                            pe.wait_ge(s_rc, g)
                        for i in range(GR):
                            last = nc.tensor.transpose(bank[7][:, i * P:(i + 1) * P], xr[:, i, :], ident[:])
                        last.then_inc(s_rt, 1)

                    keys_values(0, first=True)
                    rounds([(0, transpose_x), (1, scores), (4, transpose_rotated), (0, queries), (2, transpose_probs),
                            (0, keys_values), (2, values)])

                @block.scalar
                def _(act):
                    def copy_keys(g, first=False):
                        if g == 0 and not first:
                            return
                        act.wait_ge(s_kv, g + 1)
                        nc.scalar.activation(xk[g % 2][:].rearrange("p i q -> p (i q)"), bank[2][:], ACT.Identity,
                                             bias=xbk[:, 0:1]).then_inc(s_kc, 1)

                    def copy_xT(g):
                        act.wait_ge(s_ht, g + 1)
                        nc.scalar.activation(xaT[g % 2][:], bank[0][:], ACT.Copy).then_inc(s_hc, 1)

                    def copy_queries(g):
                        act.wait_ge(s_q, g + 1)
                        nc.scalar.activation(xq[g % 2][:].rearrange("p i q -> p (i q)"), bank[1][:], ACT.Identity,
                                             bias=xbq[:, 0:1]).then_inc(s_qc, 1)

                    def exps(g):
                        act.wait_ge(s_sh, g + 1)
                        for r in halves():
                            last = nc.scalar.activation(xp[g % 2][r, :, r], xp[g % 2][r, :, r], ACT.Exp)
                        last.then_inc(s_e, 1)

                    def copy_probsT(g):
                        act.wait_ge(s_t, g + 1)
                        nc.scalar.activation(xpT[:].rearrange("p i q -> p (i q)"), bank[5][:], ACT.Copy).then_inc(s_tc, 1)

                    def copy_rotatedT(g):
                        act.wait_ge(s_rt, g + 1)
                        nc.scalar.activation(xT[:, g * GR * P:(g + 1) * GR * P], bank[7][:], ACT.Copy).then_inc(s_rc, 1)

                    copy_keys(0, first=True)
                    act.wait_ge(s_z, 1)
                    rounds([(0, copy_xT), (4, copy_rotatedT), (0, copy_queries), (2, copy_probsT), (1, exps), (0, copy_keys)])

                @block.vector
                def _(dve):
                    nc.vector.memset(q_nat[:, :, :, 2 * DH:2 * DH + 2], 0.0)
                    for dst, k, f in ((wqk[1][:, 1, :], 0, float(DH) ** -0.5), (wv[1][:], 1, 1.0)):
                        src = wkv_g[:, k, :].rearrange("p (g d) -> p g d", d=DH).unsqueeze(2).broadcast_to([P, G4, J4, DH])
                        nc.vector.tensor_scalar(dst.rearrange("p (g j d) -> p g j d", g=G4, j=J4), src, f, None, ALU.mult)
                    dve_mean_var(dve, stats, mean[:], rstd[:], vscr[:], EPS_LN, s_link).then_inc(s_va, 1)

                    def norm(g):
                        for t in range(g * GR, (g + 1) * GR):
                            last = nc.vector.tensor_scalar(x_res[:, t, :], x_res[:, t, :], mean[:, t:t + 1], rstd[:, t:t + 1],
                                                           ALU.subtract, ALU.mult)
                        last.then_inc(s_xn, 1)

                    def copy_values(g, first=False):
                        if g == 0 and not first:
                            return
                        dve.wait_ge(s_kv, g + 1)
                        nc.vector.tensor_tensor(xv[:, tiles(g), :], bank[3][:].rearrange("p (i d) -> p i d", i=GR),
                                                xbv[:].unsqueeze(1).broadcast_to([P, GR, D]), ALU.add).then_inc(s_v, 1)

                    def shift(g):
                        dve.wait_ge(s_s, g + 1)
                        s4 = bank[4][:].rearrange("p (i k) -> p i k", i=GR)
                        for r in halves():
                            last = nc.vector.tensor_reduce(xmax[r, :], s4[r, :, r], X, ALU.max)
                        link(dve, last, s_link)
                        for r in halves():
                            last = nc.vector.tensor_tensor(xp[g % 2][r, :, r], s4[r, :, r],
                                                           xmax[r, :].unsqueeze(2).broadcast_to([S, GR, S]), ALU.subtract)
                        last.then_inc(s_sh, 1)

                    def sums(g):
                        dve.wait_ge(s_e, g + 1)
                        link(dve, nc.vector.tensor_reduce(xsum[g % 2][:], xp[g % 2][:], X, ALU.add), s_link)
                        link(dve, nc.vector.reciprocal(xsum[g % 2][:], xsum[g % 2][:]), s_link)

                    def residual(g):
                        tg = tiles(g)
                        dve.wait_ge(s_p, g + 1)
                        for i in range(GR):
                            last = nc.vector.scalar_tensor_tensor(
                                out=x_res[:, g * GR + i, :], in0=bank[6][:, i * P:(i + 1) * P], scalar=xsum[g % 2][:, i:i + 1],
                                in1=x_res[:, g * GR + i, :], op0=ALU.mult, op1=ALU.add)
                        last.then_inc(s_x2, 1)
                        dve.wait_ge(s_x2, g + 1)
                        for i in range(GR):
                            last = nc.vector.bn_stats(stats[:, g * GR + i, :], x_res[:, g * GR + i, :])
                        link(dve, last, s_link)
                        dve_mean_var(dve, stats[:, tg, :], mean2[:, tg], var2[:, tg], vscr[:, tg], EPS_LN,
                                     s_link).then_inc(s_gv, 1)

                    def norm2(g):
                        tg = tiles(g)
                        dve.wait_ge(s_gr, g + 1)
                        for t in range(g * GR, (g + 1) * GR):
                            last = nc.vector.tensor_scalar(x_in[:, t, :], x_res[:, t, :], mean2[:, t:t + 1], rstd2[:, t:t + 1],
                                                           ALU.subtract, ALU.mult)
                        last.then_inc(s_x3, 1)

                    def rotate_even(g):
                        even = x_in[:, tiles(g), :].rearrange("p i (d e) -> p i e d", e=2)[:, :, 0, :]
                        dve.wait_ge(s_x3, g + 1)
                        dve.wait_ge(s_rp, 1)
                        link(dve, nc.vector.tensor_tensor(rope_a[:], even.unsqueeze(2).broadcast_to([P, GR, 2, D // 2]),
                                                          rope_e[:].unsqueeze(1).broadcast_to([P, GR, 2, D // 2]),
                                                          ALU.mult), s_link)

                    def rotate_odd(g):
                        dve.wait_ge(s_ro, g + 1)
                        if g:
                            dve.wait_ge(s_rt, g)
                        link(dve, nc.vector.tensor_tensor(xr[:], rope_a[:].rearrange("p i c d -> p i (c d)"),
                                                          rope_b[:].rearrange("p i c d -> p i (c d)"), ALU.add), s_link)
                        dve.wait_ge(s_rr, g + 1)
                        for i in range(GR):
                            t = g * GR + i
                            last = nc.vector.tensor_scalar(xr[:, i, :], xr[:, i, :], rms2[:, t:t + 1], None, ALU.mult)
                        last.then_inc(s_xr, 1)

                    dve.wait_ge(s_rd, 1)
                    norm(0)
                    copy_values(0, first=True)
                    dve.wait_ge(s_rd, 2)
                    rounds([(-1, norm), (2, sums), (1, shift), (3, norm2), (3, rotate_even), (0, copy_values), (2, residual),
                            (3, rotate_odd)])

                @block.gpsimd
                def _(pool):
                    pool.wait_ge(s_va, 1)
                    for tg in (slice(0, GR), slice(GR, T)):
                        nc.gpsimd.tensor_tensor(rstd[:, tg], rstd[:, tg], neg_half[:, tg], ALU.pow).then_inc(s_rd, 1)
                    for b in range(2):
                        last = nc.gpsimd.memset(xp[b][:], 0.0)
                    last.then_inc(s_z, 1)
                    w_eo = n1w[:].rearrange("p (d e) -> p e d", e=2)
                    nc.gpsimd.tensor_tensor(rope_e[:], rope[:, 0:2, :], w_eo[:, 0, :].unsqueeze(1).broadcast_to([P, 2, D // 2]), ALU.mult)
                    nc.gpsimd.tensor_tensor(rope_o[:, 1, :], rope[:, 0, :], w_eo[:, 1, :], ALU.mult)
                    nc.gpsimd.tensor_tensor(rope_o[:, 0, :], rope[:, 2, :], w_eo[:, 1, :], ALU.mult).then_inc(s_rp, 1)
                    link(pool, nc.gpsimd.tensor_copy(b3_part[:, 0, :], b3[:]), s_plink)
                    link(pool, nc.gpsimd.tensor_tensor(b3_rest[:], b3[:], b3_part[:, 0, :], ALU.subtract), s_plink)
                    link(pool, nc.gpsimd.tensor_copy(b3_part[:, 1, :], b3_rest[:]), s_plink)
                    link(pool, nc.gpsimd.tensor_tensor(b3_rest[:], b3_rest[:], b3_part[:, 1, :], ALU.subtract), s_plink)
                    nc.gpsimd.tensor_copy(b3_part[:, 2, :], b3_rest[:])
                    pool.wait_ge(s_rp, 1)
                    for g in range(NG):
                        tg = tiles(g)
                        pool.wait_ge(s_gv, g + 1)
                        nc.gpsimd.tensor_tensor(rstd2[:, tg], var2[:, tg], neg_half[:, tg], ALU.pow).then_inc(s_gr, 1)
                        pool.wait_ge(s_gr, g + 1)
                        link(pool, nc.gpsimd.tensor_scalar(ms2[:, tg], var2[:, tg], EPS_LN, None, ALU.subtract), s_plink)
                        link(pool, nc.gpsimd.tensor_tensor(ms2[:, tg], ms2[:, tg], rstd2[:, tg], ALU.mult), s_plink)
                        link(pool, nc.gpsimd.tensor_tensor(ms2[:, tg], ms2[:, tg], rstd2[:, tg], ALU.mult), s_plink)
                        link(pool, nc.gpsimd.tensor_scalar(ms2[:, tg], ms2[:, tg], EPS_RMS, None, ALU.add), s_plink)
                        nc.gpsimd.tensor_tensor(rms2[:, tg], ms2[:, tg], neg_half[:, tg], ALU.pow).then_inc(s_rr, 1)
                        pool.wait_ge(s_x3, g + 1)
                        if g:
                            pool.wait_ge(s_xr, g)
                        odd = x_in[:, tg, :].rearrange("p i (d e) -> p i e d", e=2)[:, :, 1, :]
                        nc.gpsimd.tensor_tensor(rope_b[:], odd.unsqueeze(2).broadcast_to([P, GR, 2, D // 2]),
                                                rope_o[:].unsqueeze(1).broadcast_to([P, GR, 2, D // 2]), ALU.mult).then_inc(s_ro, 1)

        cross_attention()
        attention(1, x_in)

        freed = v_diag[:].rearrange("p t q b h w -> p (t q b h w)")
        xs_rows = freed[:, 0:T * 2 * XW].rearrange("p (t c w) -> p t c w", t=T, c=2)
        xnT = sb("xnT", [P, GR * P])
        rms = sb("rms", [P, T]); sq_means = sb("sq_means", [P, T, 2])
        lg = sb("lg", [P, GR, E]); lg2 = sb("lg2", [P, GR, E]); hit = sb("hit", [P, GR, E])
        top = sb("top", [P, 2, GR]); pick = sb("pick", [P, 2, GR])
        chosen = sb("chosen", [P, 2, GR, E])
        both = sb("both", [P, T, E])
        so_far = sb("so_far", [P, T + 1, E])
        pos = sb("pos", [P, GR, E]); pos2 = sb("pos2", [P, 2, GR, E]); slot = sb("slot", [P, 2, GR])
        slot_ids = sb("slot_ids", [P, NG, 2, GR], u32)
        gap = sb("gap", [P, GR]); share0 = sb("share0", [P, GR])
        cnt = sb("cnt", [P, E]); over = sb("over", [P, E, T]); nblk = sb("nblk", [P, E])
        trip = sb("trip", [P, E, E]); ends = sb("ends", [P, E])
        past = sb("past", [P, NBLK, E]); past2 = sb("past2", [P, NBLK, E])
        eb = sb("eb", [P, NBLK]); sbk = sb("sbk", [P, NBLK]); inside = sb("inside", [P, NBLK]); rowf = sb("rowf", [P, NBLK])
        expf = sb("expf", [P, NBLK]); padf = sb("padf", [P, E])
        row_tab = sb("row_tab", [P, NBLK], i32); exp_tab = sb("exp_tab", [P, NBLK], i32); pad_tab = sb("pad_tab", [P, E], i32)
        s_xs = sem("rows_scattered")
        s_pad = sem("pads_written")
        s_tab = sem("block_tables_ready")

        def route():
            s_ms = sem("r_ms_ready")
            s_rr = sem("r_rms_ready")
            s_rc = sem("r_rows_copied")
            s_xn = sem("r_rows_ready")
            s_t = sem("r_xnT_ready")
            s_tc = sem("r_xnT_copied")
            s_lg = sem("r_logits_ready")
            s_ch = sem("r_choices_ready")
            s_gp = sem("r_gap_ready")
            s_ge = sem("r_gap_exp")
            s_ps = sem("r_positions_ready")
            s_sl = sem("r_slots_ready")
            s_cn = sem("r_counts_ready")
            s_bt = sem("r_bias_columns_ready")

            def tiles(g):
                return slice(g * GR, (g + 1) * GR)

            def pad_experts(eng, experts):
                for e in experts:
                    first = eng.value_load(pad_tab[0:1, e:e + 1], min_val=0, max_val=E * REGION - P)
                    eng.dma_start(x_rows[bass.ds(first, P), :], pad_rows[:]).then_inc(s_pad, 16)

            with nc.Block() as block:
                @block.tensor
                def _(pe):
                    def transposes(g):
                        pe.wait_ge(s_xn, g + 1)
                        for i in range(GR):
                            last = nc.tensor.transpose(bank[0][:, i * P:(i + 1) * P], xs_rows[:, g * GR + i, 0, 0:D], ident[:])
                        last.then_inc(s_t, 1)

                    nc.tensor.transpose(bank[4][:, 0:2 * E * FC], bias12[:], ident[0:2 * E * FC, 0:2 * E * FC]).then_inc(s_bt, 1)
                    transposes(0)
                    for g in range(NG):
                        pe.wait_ge(s_tc, g + 1)
                        for i in range(GR):
                            last = nc.tensor.matmul(bank[1][:, i * E:(i + 1) * E], xnT[:, i * P:(i + 1) * P], rw[:],
                                                    start=True, stop=True)
                        last.then_inc(s_lg, 1)
                        if g + 1 < NG:
                            transposes(g + 1)
                        pe.wait_ge(s_ch, g + 1)
                        dst = bank[2][:, 0:GR * E]
                        nc.tensor.matmul(dst, before[:], both[:, tiles(g), :].rearrange("p t e -> p (t e)"), start=True, stop=False)
                        nc.tensor.matmul(dst, ones[:], so_far[:, tiles(g), :].rearrange("p t e -> p (t e)"), start=False,
                                         stop=True).then_inc(s_ps, 1)
                    nc.tensor.matmul(bank[3][:, 0:E], ones[:], so_far[:, T, :], start=True, stop=True).then_inc(s_cn, 1)

                @block.scalar
                def _(act):
                    def copies(g):
                        act.wait_ge(s_t, g + 1)
                        nc.scalar.activation(xnT[:], bank[0][:], ACT.Copy).then_inc(s_tc, 1)
                        nc.scalar.activation(xs_rows[:, tiles(g), 1, 0:D], xs_rows[:, tiles(g), 0, 0:D], ACT.Copy).then_inc(s_rc, 1)

                    act.wait_ge(s_bt, 1)
                    nc.scalar.activation(bias_col[:].rearrange("p k e c -> p (k e c)"), bank[4][:, 0:2 * E * FC], ACT.Copy)
                    copies(0)
                    for g in range(NG):
                        if g + 1 < NG:
                            copies(g + 1)
                        act.wait_ge(s_gp, g + 1)
                        nc.scalar.activation(gap[:], gap[:], ACT.Exp).then_inc(s_ge, 1)
                    act.wait_ge(s_tab, 1)
                    pad_experts(act, range(E // 2, E))

                @block.gpsimd
                def _(pool):
                    pool.wait_ge(s_ms, 1)
                    for tg in (slice(0, GR), slice(GR, T)):
                        nc.gpsimd.tensor_tensor(rms[:, tg], rms[:, tg], neg_half[:, tg], ALU.pow).then_inc(s_rr, 1)
                    for g in range(NG):
                        pool.wait_ge(s_rc, g + 1)
                        pool.wait_ge(s_sl, g + 1)
                        for i in range(GR):
                            for c in range(2):
                                pool.indirect_dma_start(
                                    out=x_rows[:, :], out_offset=bass.IndirectOffsetOnAxis(ap=slot_ids[:, g, c, i:i + 1], axis=0),
                                    in_=xs_rows[:, g * GR + i, c, :], in_offset=None).then_inc(s_xs, 16)

                @block.sync
                def _(sp):
                    for r in range(3):
                        sp.dma_start(bias3[r:r + 1, :].rearrange("o (e d) -> o e d", d=D), b3_part[:, r, :]).then_inc(s_b3, 16)
                    sp.dma_start(x_rows[E * REGION:E * REGION + P, :], pad_rows[:]).then_inc(s_pad, 16)
                    sp.wait_ge(s_tab, 1)
                    pad_experts(sp, range(E // 2))

                @block.vector
                def _(dve):
                    TT, TR, TS = nc.vector.tensor_tensor, nc.vector.tensor_reduce, nc.vector.tensor_scalar

                    def lk(ins):
                        link(dve, ins, s_link)

                    nc.vector.memset(so_far[:, 0, :], 0.0)
                    nc.vector.tensor_copy(xs_rows[:, :, :, D], out_row[:])
                    iota = expert_m8[:].unsqueeze(1).broadcast_to([P, GR, E])

                    def over_e(ap):
                        return ap.unsqueeze(2).broadcast_to([P, GR, E])

                    def normed_rows(g):
                        for i in range(GR):
                            t = g * GR + i
                            last = nc.vector.scalar_tensor_tensor(out=xs_rows[:, t, 0, 0:D], in0=x_res[:, t, :],
                                                                  scalar=rms[:, t:t + 1], in1=n2w[:], op0=ALU.mult,
                                                                  op1=ALU.mult)
                        last.then_inc(s_xn, 1)

                    TT(sq_means[:], stats[:, :, 1:5:3], stats[:, :, 1:5:3], ALU.mult)
                    lk(TT(rms[:], stats[:, :, 2], stats[:, :, 5], ALU.add))
                    lk(TS(rms[:], rms[:], 1.0 / D, EPS_RMS, ALU.mult, ALU.add))
                    lk(nc.vector.scalar_tensor_tensor(out=rms[:], in0=sq_means[:, :, 0], scalar=0.5, in1=rms[:],
                                                      op0=ALU.mult, op1=ALU.add))
                    nc.vector.scalar_tensor_tensor(out=rms[:], in0=sq_means[:, :, 1], scalar=0.5, in1=rms[:],
                                                   op0=ALU.mult, op1=ALU.add).then_inc(s_ms, 1)
                    dve.wait_ge(s_rr, 1)
                    normed_rows(0)
                    for g in range(NG):
                        tg = tiles(g)
                        if g == 0:
                            dve.wait_ge(s_rr, 2)
                        if g + 1 < NG:
                            normed_rows(g + 1)
                        dve.wait_ge(s_lg, g + 1)
                        lk(TT(lg[:], bank[1][:, 0:GR * E].rearrange("p (t e) -> p t e", e=E),
                              rb[:].unsqueeze(1).broadcast_to([P, GR, E]), ALU.add))
                        for c, src in ((0, lg), (1, lg2)):
                            lk(TR(top[:, c, :], src[:], X, ALU.max))
                            lk(TT(hit[:], src[:], over_e(top[:, c, :]), ALU.is_equal))
                            lk(TT(hit[:], hit[:], iota, ALU.mult))
                            lk(TR(pick[:, c, :], hit[:], X, ALU.min))
                            lk(TT(chosen[:, c], iota, over_e(pick[:, c, :]), ALU.is_equal))
                            if c == 0:
                                lk(nc.vector.scalar_tensor_tensor(out=lg2[:], in0=chosen[:, 0], scalar=-3.0e38, in1=lg[:],
                                                                  op0=ALU.mult, op1=ALU.add))
                        TT(gap[:], top[:, 1, :], top[:, 0, :], ALU.subtract).then_inc(s_gp, 1)
                        lk(TT(both[:, tg, :], chosen[:, 0], chosen[:, 1], ALU.add))
                        for i in range(GR):
                            t = g * GR + i
                            last = TT(so_far[:, t + 1, :], so_far[:, t, :], both[:, t, :], ALU.add)
                            if i < GR - 1:
                                lk(last)
                        last.then_inc(s_ch, 1)
                        dve.wait_ge(s_ge, g + 1)
                        lk(TS(share0[:], gap[:], 1.0, None, ALU.add))
                        lk(nc.vector.reciprocal(share0[:], share0[:]))
                        TT(xs_rows[:, tg, 1, D + 1], gap[:], share0[:], ALU.mult)
                        nc.vector.tensor_copy(xs_rows[:, tg, 0, D + 1], share0[:])
                        dve.wait_ge(s_ps, g + 1)
                        lk(TT(pos[:], bank[2][:, 0:GR * E].rearrange("p (t e) -> p t e", e=E),
                              expert_row[:].unsqueeze(1).broadcast_to([P, GR, E]), ALU.add))
                        lk(TT(pos2[:], chosen[:], pos[:].unsqueeze(1).broadcast_to([P, 2, GR, E]), ALU.mult))
                        lk(TR(slot[:], pos2[:], X, ALU.add))
                        nc.vector.tensor_copy(slot_ids[:, g], slot[:]).then_inc(s_sl, 1)

                    dve.wait_ge(s_cn, 1)
                    lk(nc.vector.tensor_copy(cnt[:], bank[3][:, 0:E]))
                    TT(padf[:], cnt[:], expert_row[:], ALU.add)
                    lk(TT(over[:], cnt[:].unsqueeze(2).broadcast_to([P, E, T]), blk128[:].unsqueeze(1).broadcast_to([P, E, T]),
                          ALU.is_gt))
                    nc.vector.tensor_copy(pad_tab[:], padf[:])
                    lk(TR(nblk[:], over[:], X, ALU.add))
                    lk(TT(trip[:], tri[:], nblk[:].unsqueeze(1).broadcast_to([P, E, E]), ALU.mult))
                    lk(TR(ends[:], trip[:], X, ALU.add))
                    lk(TT(past[:], blk_id[:].unsqueeze(2).broadcast_to([P, NBLK, E]),
                          ends[:].unsqueeze(1).broadcast_to([P, NBLK, E]), ALU.is_ge))
                    TR(eb[:], past[:], X, ALU.add)
                    lk(TT(past2[:], past[:], nblk[:].unsqueeze(1).broadcast_to([P, NBLK, E]), ALU.mult))
                    lk(TR(sbk[:], past2[:], X, ALU.add))
                    TS(inside[:], eb[:], float(E), None, ALU.is_lt)
                    TS(expf[:], eb[:], float(E - 1), None, ALU.min)
                    lk(TT(sbk[:], blk_id[:], sbk[:], ALU.subtract))
                    lk(TT(sbk[:], sbk[:], inside[:], ALU.mult))
                    lk(TS(sbk[:], sbk[:], float(P), None, ALU.mult))
                    lk(nc.vector.scalar_tensor_tensor(out=rowf[:], in0=eb[:], scalar=float(REGION), in1=sbk[:],
                                                      op0=ALU.mult, op1=ALU.add))
                    nc.vector.tensor_copy(exp_tab[:], expf[:])
                    nc.vector.tensor_copy(row_tab[:], rowf[:]).then_inc(s_tab, 1)

        route()

        xb = [sb(f"xb{i}", [P, XW]) for i in range(2)]
        xbT = [sb(f"xbT{i}", [P, P]) for i in range(2)]
        act1 = [xT[:, i * F:(i + 1) * F] for i in range(2)]
        gated = [xT[:, (2 + i) * F:(3 + i) * F] for i in range(2)]
        diag_flat = k_diag[:].rearrange("p u g j s -> p (u g j s)")
        w_now = [diag_flat[:, 2 * i * F:2 * (i + 1) * F].rearrange("p (k f) -> p k f", k=2) for i in range(2)]
        bias_now = [sb(f"bias_now{i}", [P, 2, FC]) for i in range(2)]
        yb = [sb(f"yb{i}", [P, D]) for i in range(2)]
        meta_next = [sb(f"meta_next{i}", [P, 2]) for i in range(2)]
        meta_now = [sb(f"meta_now{i}", [P, 2]) for i in range(2)]
        dst_id = [sb(f"dst_id{i}", [P, 1], u32) for i in range(2)]
        s_y = [sem(f"y_scattered{i}") for i in range(2)]

        def experts():
            s_ld = [sem(f"m_block_loaded{i}") for i in range(2)]
            s_xt = sem("m_xT_ready")
            s_xc = sem("m_xT_copied")
            s_h = sem("m_h_ready")
            s_a = sem("m_silu_ready")
            s_id = sem("m_meta_kept")
            s_mn = sem("m_meta_now")
            s_g = sem("m_gated_ready")
            s_o = sem("m_out_ready")
            s_oc = sem("m_out_copied")

            def pe_xT(pe, b, u, i, first=False):
                pe.wait_ge(s_ld[u], 16 * i + 16)
                if not first:
                    pe.wait_ge(s_xc, b)
                nc.tensor.transpose(bank[0][:, 0:P], xb[u][:, 0:D], ident[:]).then_inc(s_xt, 1)

            def pe_hidden(pe, b, u, first=False):
                pe.wait_ge(s_xc, b + 1)
                if not first:
                    pe.wait_ge(s_g, b - 1)
                for k, bk in enumerate((bank[1 + u], bank[3 + u])):
                    for c in range(FC):
                        last = nc.tensor.matmul(bk[:, c * P:(c + 1) * P], w_now[u][:, k, c * P:(c + 1) * P], xbT[u][:],
                                                start=True, stop=True)
                last.then_inc(s_h, 1)

            def pe_down(pe, b, u, e, first=False):
                pe.wait_ge(s_g, b + 1)
                if not first:
                    pe.wait_ge(s_oc, b - 1)
                dst = bank[6 + u][:, 0:D]
                nc.tensor.matmul(dst, ones3[:], bias3[:, bass.ds(e * D, D)], start=True, stop=False)
                for c in range(FC):
                    last = nc.tensor.matmul(dst, gated[u][:, c * P:(c + 1) * P], w3[:, e, c, :], start=False, stop=(c == FC - 1))
                last.then_inc(s_o, 1)

            def block_expert(eng, b):
                return eng.value_load(exp_tab[0:1, bass.ds(b, 1)], min_val=0, max_val=E - 1)

            def act_weights(act, b, u, first=False):
                e = block_expert(act, b)
                if not first:
                    act.wait_ge(s_g, b - 1)
                nc.scalar.activation(bias_now[u][:], bias_col[:, :, e, :], ACT.Copy)
                nc.scalar.activation(w_now[u], w12[:, e, :, :], ACT.Copy)

            def act_xT(act, b, u):
                act.wait_ge(s_xt, b + 1)
                nc.scalar.activation(xbT[u][:], bank[0][:, 0:P], ACT.Copy).then_inc(s_xc, 1)

            def act_silu(act, b, u):
                act.wait_ge(s_h, b + 1)
                for c in range(FC):
                    r = slice(c * P, (c + 1) * P)
                    nc.scalar.activation(act1[u][:, r], bank[1 + u][:, r], ACT.Silu, bias=bias_now[u][:, 0, c:c + 1]).then_inc(s_a, 1)

            def dve_keep_meta(dve, b, u, i, first=False):
                if not first:
                    dve.wait_ge(s_mn, b - 1)
                dve.wait_ge(s_ld[u], 16 * i + 16)
                nc.vector.tensor_copy(meta_next[u][:], xb[u][:, D:XW]).then_inc(s_id, 1)

            def dve_gate(dve, b, u, first=False):
                if not first:
                    dve.wait_ge(s_o, b - 1)
                for c in range(FC):
                    r = slice(c * P, (c + 1) * P)
                    dve.wait_ge(s_a, FC * b + c + 1)
                    last = nc.vector.scalar_tensor_tensor(out=gated[u][:, r], in0=bank[3 + u][:, r], scalar=bias_now[u][:, 1, c:c + 1],
                                                          in1=act1[u][:, r], op0=ALU.add, op1=ALU.mult)
                last.then_inc(s_g, 1)

            def dve_meta_now(dve, b, u, first=False):
                dve.wait_ge(s_id, b + 1)
                if not first:
                    dve.wait_ge(s_oc, b - 1)
                nc.vector.tensor_copy(meta_now[u][:], meta_next[u][:]).then_inc(s_mn, 1)

            def dve_out(dve, b, u, i, first=False):
                dve.wait_ge(s_o, b + 1)
                dve.wait_ge(s_mn, b + 1)
                if not first:
                    dve.wait_ge(s_y[u], 16 * i)
                nc.vector.tensor_scalar(yb[u][:], bank[6 + u][:, 0:D], meta_now[u][:, 1:2], None, ALU.mult)
                nc.vector.tensor_copy(dst_id[u][:], meta_now[u][:, 0:1]).then_inc(s_oc, 1)

            def pool_out(pool, b, u):
                pool.wait_ge(s_oc, b + 1)
                pool.nop(nofuse=True)
                pool.indirect_dma_start(out=y_rows[:, :], out_offset=bass.IndirectOffsetOnAxis(ap=dst_id[u][:, 0:1], axis=0),
                                        in_=yb[u][:], in_offset=None, bounds_check=2 * ROWS - 1,
                                        oob_is_err=False).then_inc(s_y[u], 16)

            def sp_load(sp, b, u, first=False):
                if not first:
                    sp.wait_ge(s_xt, b - 1)
                    sp.wait_ge(s_id, b - 1)
                r = sp.value_load(row_tab[0:1, bass.ds(b, 1)], min_val=0, max_val=E * REGION)
                sp.dma_start(xb[u][:], x_rows[bass.ds(r, P), :]).then_inc(s_ld[u], 16)

            N = NBLK

            def pe_step(pe, b, u, i, down="all"):
                if not (isinstance(b, int) and b + 1 >= N):
                    pe_hidden(pe, b + 1, 1 - u, first=(down is None))
                e = block_expert(pe, b - 1) if down else None
                if not (isinstance(b, int) and b + 2 >= N):
                    pe_xT(pe, b + 2, u, i + 1)
                if down:
                    pe_down(pe, b - 1, 1 - u, e, first=(down == "first"))

            def steps(eng, step, start, after=3):
                loops = (N - after - start) // 4
                with eng.Fori(0, loops) as j:
                    for k in range(start, start + 4):
                        step(4 * j + k, k % 2, 2 * j + k // 2)
                for b in range(start + 4 * loops, N):
                    step(b, b % 2, b // 2)

            with nc.Block() as block:
                @block.sync
                def _(sp):
                    sp.wait_ge(s_xs, 16 * 2 * T)
                    sp.wait_ge(s_pad, 16 * (E + 1))
                    sp_load(sp, 0, 0, True)
                    sp_load(sp, 1, 1, True)
                    with sp.Fori(1, N // 2) as i:
                        for u in range(2):
                            sp_load(sp, 2 * i + u, u)
                    sp_load(sp, N - 1, (N - 1) % 2)

                @block.tensor
                def _(pe):
                    pe.wait_ge(s_b3, 16 * 3)
                    pe_xT(pe, 0, 0, 0, first=True)
                    pe_xT(pe, 1, 1, 0)
                    pe_hidden(pe, 0, 0, first=True)
                    pe_step(pe, 0, 0, 0, down=None)
                    pe_step(pe, 1, 1, 0, down="first")
                    pe_step(pe, 2, 0, 1, down="first")
                    steps(pe, lambda b, u, i: pe_step(pe, b, u, i), 3)
                    pe_down(pe, N - 1, 0, block_expert(pe, N - 1))

                @block.scalar
                def _(act):
                    act_weights(act, 0, 0, True)
                    act_weights(act, 1, 1, True)
                    act_xT(act, 0, 0)
                    act_xT(act, 1, 1)

                    def step(b, u, i):
                        act_silu(act, b, u)
                        if not (isinstance(b, int) and b + 2 >= N):
                            act_weights(act, b + 2, u)
                            act_xT(act, b + 2, u)

                    step(0, 0, 0)
                    step(1, 1, 0)
                    step(2, 0, 1)
                    steps(act, step, 3)

                @block.vector
                def _(dve):
                    for b in range(2):
                        dve_keep_meta(dve, b, b, 0, True)
                    nc.vector.tensor_tensor(x_res[:], x_res[:], x_in[:], ALU.add)

                    def step(b, u, i, out="all"):
                        dve_gate(dve, b, u, first=(out is None))
                        if out:
                            dve_out(dve, b - 2, u, i - 1, first=(out == "first"))
                        dve_meta_now(dve, b, u, first=(out is None))
                        if not (isinstance(b, int) and b + 2 >= N):
                            dve_keep_meta(dve, b + 2, u, i + 1)

                    for b in range(4):
                        step(b, b % 2, b // 2, None if b < 2 else "first")
                    steps(dve, step, 4)
                    dve_out(dve, N - 2, 1, N // 2 - 1)
                    dve_out(dve, N - 1, 0, N // 2)

                @block.gpsimd
                def _(pool):
                    steps(pool, lambda b, u, i: pool_out(pool, b, u), 0, after=0)

        experts()

        yy = freed[:, 0:T * 2 * D].rearrange("p (t c d) -> p t c d", t=T, c=2)
        res = x_in

        def combine():
            s_yl = [sem(f"c_y_loaded{g}") for g in range(NG)]
            s_gv = sem("c_var_ready")
            s_gr = sem("c_rstd_ready")
            s_gs = sem("c_shift_ready")
            s_f = sem("c_result_ready")
            s_fd = sem("c_last_result_ready")
            with nc.Block() as block:
                @block.sync
                def _(sp):
                    sp.wait_ge(s_y[0], 16 * ((NBLK + 1) // 2))
                    sp.wait_ge(s_y[1], 16 * (NBLK // 2))
                    src = y_rows.rearrange("(t p c) d -> p t c d", p=P, c=2)
                    for g in range(NG):
                        tg = slice(g * GR, (g + 1) * GR)
                        sp.dma_start(yy[:, tg], src[:, tg]).then_inc(s_yl[g], 16)
                    dst = view(out)
                    for g in range(NG):
                        tg = slice(g * GR, (g + 1) * GR)
                        sp.wait_ge(*((s_f, g + 1) if g < NG - 1 else (s_fd, 1)))
                        sp.dma_start(dst[:, tg, :], res[:, tg, :]).then_inc(s_store, 16)
                    sp.wait_ge(s_store, 16 * NG)

                @block.gpsimd
                def _(pool):
                    for g in range(NG):
                        tg = slice(g * GR, (g + 1) * GR)
                        pool.wait_ge(s_gv, g + 1)
                        nc.gpsimd.tensor_tensor(rstd2[:, tg], var2[:, tg], neg_half[:, tg], ALU.pow).then_inc(s_gr, 1)

                @block.vector
                def _(dve):
                    for g in range(NG + 1):
                        if g < NG:
                            tg = slice(g * GR, (g + 1) * GR)
                            dve.wait_ge(s_yl[g], 16)
                            link(dve, nc.vector.tensor_tensor(yy[:, tg, 0, :], yy[:, tg, 0, :], yy[:, tg, 1, :], ALU.add), s_link)
                            link(dve, nc.vector.tensor_tensor(x_res[:, tg, :], x_res[:, tg, :], yy[:, tg, 0, :], ALU.add), s_link)
                            for t in range(g * GR, (g + 1) * GR):
                                last = nc.vector.bn_stats(stats[:, t, :], x_res[:, t, :])
                            link(dve, last, s_link)
                            dve_mean_var(dve, stats[:, tg, :], mean2[:, tg], var2[:, tg], vscr[:, tg], EPS_LN,
                                         s_link).then_inc(s_gv, 1)
                        if g:
                            tg = slice((g - 1) * GR, g * GR)
                            dve.wait_ge(s_gr, g)
                            if g < NG:
                                nc.vector.scalar_tensor_tensor(out=shift2[:, tg], in0=mean2[:, tg], scalar=-1.0, in1=rstd2[:, tg],
                                                               op0=ALU.mult, op1=ALU.mult).then_inc(s_gs, 1)
                            else:
                                for t in range(T - GR, T):
                                    last = nc.vector.tensor_scalar(res[:, t, :], x_res[:, t, :], mean2[:, t:t + 1],
                                                                   rstd2[:, t:t + 1], ALU.subtract, ALU.mult)
                                last.then_inc(s_fd, 1)

                @block.scalar
                def _(act):
                    for g in range(NG - 1):
                        act.wait_ge(s_gs, g + 1)
                        for t in range(g * GR, (g + 1) * GR):
                            last = nc.scalar.activation(res[:, t, :], x_res[:, t, :], ACT.Identity, bias=shift2[:, t:t + 1],
                                                        scale=rstd2[:, t:t + 1])
                        last.then_inc(s_f, 1)

        combine()


HALF_TYPE = ("causal_q", "causal_k")


def constants():
    import numpy as np
    p = np.arange(P)
    half = p // S
    c = {"ident": np.eye(P)}
    own = (half[:, None] == np.arange(2)[None, :]).astype(np.float64)
    c["vmask"] = np.stack([own] * H + [own * (DH * DH / (7.0 * 7.0 * DH))] * H, axis=1)
    c["slot_mask"] = np.broadcast_to((p[:, None] // SLOT == np.arange(J4)[None, :])[:, :, None], (P, J4, S))
    r = np.arange(S)
    later = (r[:, None] > (p % S)[None, :]).astype(np.float64)
    c["causal_q"] = np.vstack([later * -30512.0, later * -357.0])
    k = np.broadcast_to(np.eye(S)[:, None, :], (S, J4, S))
    c["causal_k"] = np.vstack([k * 32768.0, k * 512.0])
    assert 30512 * 32768 + 357 * 512 == 10 ** 9
    theta = np.float32(1.0) / np.float32(10000.0) ** (np.arange(D // 2, dtype=np.float32) / np.float32(D // 2))
    ang = (p % S).astype(np.float32)[:, None] * theta[None, :]
    c["rope"] = np.stack([np.cos(ang), np.sin(ang), -np.sin(ang)], axis=1)
    c["before"] = (p[:, None] < p[None, :]).astype(np.float64)
    c["expert_m8"] = np.broadcast_to(np.arange(E) - E, (P, E))
    c["expert_row"] = np.broadcast_to(np.arange(E) * REGION, (P, E))
    c["blk128"] = np.broadcast_to(np.arange(T) * P, (P, T))
    c["blk_id"] = np.broadcast_to(np.arange(NBLK), (P, NBLK))
    c["tri"] = np.broadcast_to(np.tril(np.ones((E, E))), (P, E, E))
    c["out_row"] = 2 * (np.arange(T)[None, :, None] * P + p[:, None, None]) + np.arange(2)[None, None, :]
    c["pad_rows"] = np.concatenate([np.zeros((P, D)), np.full((P, 1), 4.0 * ROWS), np.zeros((P, 1))], axis=1)
    return {n: np.ascontiguousarray(np.asarray(v).astype(np.float16 if n in HALF_TYPE else np.float32)) for n, v in c.items()}


def kernel(**inputs):
    import numpy as np
    import concourse.bacc as bacc
    from concourse.bass_utils import run_bass_kernel_spmd as run

    nc = bacc.Bacc("TRN2", target_bir_lowering=False, num_devices=1)
    arrays = {n: np.ascontiguousarray(v) for n, v in inputs.items()}
    arrays["xT"] = np.ascontiguousarray(arrays["x"].reshape(ROWS, D).T)
    arrays["ctxT"] = np.ascontiguousarray(arrays.pop("ctx_512").reshape(ROWS, CD).T)
    for n in ("Wq", "Wk", "Wv", "Wo"):
        arrays["L0_attn_" + n] = np.ascontiguousarray(arrays["L0_attn_" + n].T)
    arrays.update(constants())
    a = {n: nc.dram_tensor(n + "_dram", v.shape, mybir.dt.from_np(v.dtype), kind="ExternalInput").ap()
         for n, v in arrays.items()}
    out = nc.dram_tensor("out_dram", (NB, S, D), fp32, kind="ExternalOutput").ap()
    program(nc, a, out)
    r = run(nc, [{n + "_dram": v for n, v in arrays.items()}], core_ids=[0])
    return r.results[0]["out_dram"]
```
